# Optimizing a Trainium2 kernel written in Bass

```python
import numpy as np
import jax
import jax.numpy as jnp

def _softmax(x, axis=-1):
    return jax.nn.softmax(x, axis=axis)

def _gelu(x):
    return jax.nn.gelu(x, approximate=True)

def _silu(x):
    return jax.nn.silu(x)

def _sigmoid(x):
    return jax.nn.sigmoid(x)

def _layernorm(x, axis=-1, eps=1e-05):
    m = jnp.mean(x, axis=axis, keepdims=True)
    v = jnp.var(x, axis=axis, keepdims=True)
    return (x - m) / jnp.sqrt(v + eps)

def _scatter_add(tgt, idx, src, axis=0):
    return tgt.at[idx].add(src)

def _segment_sum(src, seg, n):
    return jax.ops.segment_sum(src, seg, n)
kernel_name = 'mk_decoder_preln_d2_seqx_r8_f2540e'

def setup_inputs(seed: int=0):
    np.random.seed(seed)
    _w = jnp.asarray

    def _rec_inputs():
        import jax
        import jax.numpy as jnp
        _rk = jax.random.key(seed)
        x = 0.0002417 + 0.9998 * jax.random.normal(jax.random.fold_in(_rk, 1), (1, 1024, 128), jnp.float32)
        _lenS = 1024 - jax.random.randint(jax.random.fold_in(_rk, 7), (1,), 0, max(1, 1024 // 4) + 1, jnp.int32)
        _lenS2 = 6404 - jax.random.randint(jax.random.fold_in(_rk, 8), (1,), 0, max(1, 6404 // 4) + 1, jnp.int32)
        _ctx_1024P = jax.random.normal(jax.random.fold_in(_rk, 11), (1, 16, 128), jnp.float32)
        _ctx_1024c = jax.random.dirichlet(jax.random.fold_in(_rk, 511), 0.3 * jnp.ones((16,), jnp.float32), (1, 6404))
        _ctx_1024t = jnp.einsum('bsk,bkd->bsd', _ctx_1024c, _ctx_1024P)
        _ctx_1024t = _ctx_1024t * jax.lax.rsqrt(jnp.mean(jnp.square(_ctx_1024t)) + 1e-12) * 0.953939
        ctx_1024 = 7.22013e-05 + 1.00017 * (_ctx_1024t + 0.3 * jax.random.normal(jax.random.fold_in(_rk, 611), (1, 6404, 128), jnp.float32))
        _validS = jnp.arange(1024)[None, :] < _lenS[:, None]
        _validS2 = jnp.arange(6404)[None, :] < _lenS2[:, None]
        _causal = jnp.tril(jnp.ones((1024, 1024), dtype=bool))
        mask_Bx1x1xS2_if1 = jnp.where(jnp.ones((1, 1, 1, 6404), dtype=bool), 1, 0).astype(jnp.int32)
        mask_Bx1xSxS2_ik1 = jnp.where(jnp.broadcast_to(_validS2[:, None, None, :], (1, 1, 1024, 6404)), 1, 0).astype(jnp.int32)
        return (x, ctx_1024, mask_Bx1x1xS2_if1, mask_Bx1xSxS2_ik1)
    x, ctx_1024, mask_Bx1x1xS2_if1, mask_Bx1xSxS2_ik1 = _rec_inputs()

    def _L0_attn_setup():
        import jax, jax.numpy as jnp
        import numpy as np
        B, S, D = (2, 256, 128)
        N_HEADS = 16
        HEAD_DIM = D // N_HEADS
        WINDOW = 128
        STRIDE = 64

        def _sparse_mask(s):
            row = jnp.arange(s)[:, None]
            col = jnp.arange(s)[None, :]
            causal = col <= row
            in_window = (col >= row - WINDOW + 1) & causal
            is_global = (col % STRIDE == 0) & causal
            return in_window | is_global
        key = jax.random.key(seed)
        k1, k2, k3 = jax.random.split(key, 3)
        x = jax.random.normal(k1, (B, S, D), dtype=jnp.float32)
        Wqkv = jax.random.normal(k2, (D, 3 * D), dtype=jnp.float32) * 0.02
        Wproj = jax.random.normal(k3, (D, D), dtype=jnp.float32) * 0.02
        return {'x': x, 'Wqkv': Wqkv, 'Wproj': Wproj}
    _L0_attn_all = _L0_attn_setup()
    _L0_attn_in = {k: v for k, v in _L0_attn_all.items() if k in ('Wqkv', 'Wproj')}
    del _L0_attn_all

    def _L0_xattn_setup():
        import jax, jax.numpy as jnp
        import numpy as np
        NUM_HEADS = 16
        EMBED = 128
        N, S = (4, 256)
        key = jax.random.key(seed)
        k1, k2, k3, k4, k5 = jax.random.split(key, 5)
        return {'values': jax.random.normal(k1, (N, S, EMBED), dtype=jnp.float32), 'keys': jax.random.normal(k2, (N, S, EMBED), dtype=jnp.float32), 'query': jax.random.normal(k3, (N, S, EMBED), dtype=jnp.float32), 'mask': jnp.ones((N, 1, 1, S), dtype=jnp.int32), 'W_out': jax.random.normal(k4, (EMBED, EMBED), dtype=jnp.float32) * 0.02, 'b_out': jax.random.normal(k5, (EMBED,), dtype=jnp.float32) * 0.02}
    _L0_xattn_all = _L0_xattn_setup()
    _L0_xattn_in = {k: v for k, v in _L0_xattn_all.items() if k in ('W_out', 'b_out')}
    del _L0_xattn_all

    def _L0_ffn_setup():
        import jax, jax.numpy as jnp
        import numpy as np
        JITTER_EPS = 0.01
        NEG_INF = -jnp.inf

        def sparsemixer_eval(scores, jitter_eps):
            m1 = jnp.max(scores, axis=-1, keepdims=True)
            ind1 = jnp.argmax(scores, axis=-1)
            factor1 = jnp.maximum(jnp.abs(scores), m1)
            mask1 = jax.lax.stop_gradient((m1 - scores) / factor1 > 2.0 * jitter_eps)
            gates1 = jax.nn.softmax(jnp.where(mask1, NEG_INF, scores), axis=-1)
            mult1 = jnp.take_along_axis(gates1, ind1[:, None], axis=-1)[:, 0]
            E = scores.shape[-1]
            onehot1 = ind1[:, None] == jnp.arange(E)[None, :]
            masked_scores = jnp.where(onehot1, NEG_INF, scores)
            m2 = jnp.max(masked_scores, axis=-1, keepdims=True)
            ind2 = jnp.argmax(masked_scores, axis=-1)
            factor2 = jnp.maximum(jnp.abs(scores), m2)
            mask2 = jax.lax.stop_gradient((m2 - scores) / factor2 > 2.0 * jitter_eps)
            gates2 = jax.nn.softmax(jnp.where(mask2, NEG_INF, masked_scores), axis=-1)
            mult2 = jnp.take_along_axis(gates2, ind2[:, None], axis=-1)[:, 0]
            multiplier = jnp.stack([mult1, mult2], axis=-1)
            selected = jnp.stack([ind1, ind2], axis=-1)
            return (multiplier, selected)
        key = jax.random.key(seed)
        k0, k1, k2, k3, k4 = jax.random.split(key, 5)
        B, S, H, F, E = (2, 128, 128, 256, 8)
        scale = 0.02
        return {'hidden_states': jax.random.normal(k0, (B, S, H), dtype=jnp.float32), 'router_w': jax.random.normal(k1, (E, H), dtype=jnp.float32) * scale, 'w_gate': jax.random.normal(k2, (E, F, H), dtype=jnp.float32) * scale, 'w_up': jax.random.normal(k3, (E, F, H), dtype=jnp.float32) * scale, 'w_down': jax.random.normal(k4, (E, H, F), dtype=jnp.float32) * scale}
    _L0_ffn_all = _L0_ffn_setup()
    _L0_ffn_in = {k: v for k, v in _L0_ffn_all.items() if k in ('router_w', 'w_gate', 'w_up', 'w_down')}
    del _L0_ffn_all

    def _L1_attn_setup():
        import jax, jax.numpy as jnp
        import numpy as np
        N_EMBD = 128
        N_HEAD = 16
        HEAD_DIM = N_EMBD // N_HEAD
        KV_RANK = 32
        Q_RANK = 64
        ROPE_DIM = 32
        B, T = (2, 256)
        EPS = 1e-06

        def _rope_tables(T, dim):
            inv_freq = 1.0 / 10000.0 ** (np.arange(0, dim, 2, dtype=np.float32) / dim)
            t = np.arange(T, dtype=np.float32)
            freqs = np.outer(t, inv_freq)
            emb = np.concatenate([freqs, freqs], -1)
            return (jnp.asarray(np.cos(emb)), jnp.asarray(np.sin(emb)))

        def _apply_rope(x, cos, sin):
            d2 = x.shape[-1] // 2
            x1, x2 = (x[..., :d2], x[..., d2:])
            rot = jnp.concatenate([-x2, x1], axis=-1)
            return x * cos[None, None, :, :] + rot * sin[None, None, :, :]
        key = jax.random.key(seed)
        ks = jax.random.split(key, 10)

        def w(k, fan_in, fan_out):
            return jax.random.normal(k, (fan_in, fan_out), dtype=jnp.float32) * fan_in ** (-0.5)
        return {'x': jax.random.normal(ks[0], (B, T, N_EMBD), dtype=jnp.float32), 'W_kv': w(ks[1], N_EMBD, KV_RANK), 'g_kv': jnp.ones((KV_RANK,), dtype=jnp.float32), 'W_kdec': w(ks[2], KV_RANK, N_HEAD * HEAD_DIM), 'W_vdec': w(ks[3], KV_RANK, N_HEAD * HEAD_DIM), 'W_q': w(ks[4], N_EMBD, Q_RANK), 'W_qdec': w(ks[5], Q_RANK, N_HEAD * HEAD_DIM), 'W_krope': w(ks[6], N_EMBD, N_HEAD * ROPE_DIM), 'W_qrope': w(ks[7], Q_RANK, N_HEAD * ROPE_DIM), 'W_o': w(ks[8], N_HEAD * HEAD_DIM, N_EMBD)}
    _L1_attn_all = _L1_attn_setup()
    _L1_attn_in = {k: v for k, v in _L1_attn_all.items() if k in ('W_kv', 'g_kv', 'W_kdec', 'W_vdec', 'W_q', 'W_qdec', 'W_krope', 'W_qrope', 'W_o')}
    del _L1_attn_all

    def _L1_xattn_setup():
        import jax, jax.numpy as jnp
        import numpy as np
        EMB, HEADS = (128, 16)
        B, S = (4, 256)
        key = jax.random.key(seed)
        ks = jax.random.split(key, 12)
        scale = 1.0 / np.sqrt(EMB)
        inp = {'q': jax.random.normal(ks[0], (B, S, EMB), jnp.float32), 'k': jax.random.normal(ks[1], (B, S, EMB), jnp.float32), 'v': jax.random.normal(ks[2], (B, S, EMB), jnp.float32), 'mask': jax.random.randint(ks[3], (B, 1, S, S), 0, 2, jnp.int32), 'Wq': jax.random.normal(ks[4], (EMB, EMB), jnp.float32) * scale, 'bq': jnp.zeros((EMB,), jnp.float32), 'Wk': jax.random.normal(ks[5], (EMB, EMB), jnp.float32) * scale, 'bk': jnp.zeros((EMB,), jnp.float32), 'Wv': jax.random.normal(ks[6], (EMB, EMB), jnp.float32) * scale, 'bv': jnp.zeros((EMB,), jnp.float32), 'Wo': jax.random.normal(ks[7], (EMB, EMB), jnp.float32) * scale, 'bo': jnp.zeros((EMB,), jnp.float32)}
        return inp
    _L1_xattn_all = _L1_xattn_setup()
    _L1_xattn_in = {k: v for k, v in _L1_xattn_all.items() if k in ('Wq', 'bq', 'Wk', 'bk', 'Wv', 'bv', 'Wo', 'bo')}
    del _L1_xattn_all

    def _L1_ffn_setup():
        import jax, jax.numpy as jnp
        import numpy as np
        D = 128
        H = 4
        DF = 512
        E = 8
        EPS = 1e-05

        def _layer_norm(x, g, b):
            mu = jnp.mean(x, axis=-1, keepdims=True)
            var = jnp.mean(jnp.square(x - mu), axis=-1, keepdims=True)
            return (x - mu) * jax.lax.rsqrt(var + EPS) * g + b

        def _mha(x, Wqkv, bqkv, Wo, bo):
            S, B, _ = x.shape
            hd = D // H
            qkv = x @ Wqkv.T + bqkv
            q, k, v = jnp.split(qkv, 3, axis=-1)
            to_heads = lambda t: t.reshape(S, B, H, hd).transpose(1, 2, 0, 3)
            q, k, v = (to_heads(q), to_heads(k), to_heads(v))
            scores = jnp.einsum('bhqd,bhkd->bhqk', q, k) * (1.0 / np.sqrt(hd))
            att = jax.nn.softmax(scores, axis=-1)
            o = jnp.einsum('bhqk,bhkd->bhqd', att, v)
            o = o.transpose(2, 0, 1, 3).reshape(S, B, D)
            return o @ Wo.T + bo

        def _moe(x, Wg, W1, b1, W2, b2):
            S, B, _ = x.shape
            xf = x.reshape(S * B, D)
            logits = xf @ Wg.T
            idx = jnp.argmax(logits, axis=-1)
            out = jnp.zeros_like(xf)
            for e in range(E):
                m = (idx == e)[:, None].astype(xf.dtype)
                h = jax.nn.relu(xf @ W1[e] + b1[e])
                out = out + m * (h @ W2[e] + b2[e])
            return out.reshape(S, B, D)
        key = jax.random.key(seed)
        ks = jax.random.split(key, 16)
        S, B = (64, 8)
        s = lambda k, shape, fan: jax.random.normal(k, shape, jnp.float32) * (1.0 / np.sqrt(fan))
        return {'x': jax.random.normal(ks[0], (S, B, D), jnp.float32), 'Wqkv': s(ks[1], (3 * D, D), D), 'bqkv': jnp.zeros((3 * D,), jnp.float32), 'Wo': s(ks[2], (D, D), D), 'bo': jnp.zeros((D,), jnp.float32), 'g1': jnp.ones((D,), jnp.float32), 'be1': jnp.zeros((D,), jnp.float32), 'g2': jnp.ones((D,), jnp.float32), 'be2': jnp.zeros((D,), jnp.float32), 'Wg': s(ks[3], (E, D), D), 'W1': s(ks[4], (E, D, DF), D), 'b1': jnp.zeros((E, DF), jnp.float32), 'W2': s(ks[5], (E, DF, D), DF), 'b2': jnp.zeros((E, D), jnp.float32)}
    _L1_ffn_all = _L1_ffn_setup()
    _L1_ffn_in = {k: v for k, v in _L1_ffn_all.items() if k in ('Wqkv', 'bqkv', 'Wo', 'bo', 'g1', 'be1', 'g2', 'be2', 'Wg', 'W1', 'b1', 'W2', 'b2')}
    del _L1_ffn_all
    return {'x': x, 'ctx_1024': ctx_1024, 'mask_Bx1x1xS2_if1': mask_Bx1x1xS2_if1, 'mask_Bx1xSxS2_ik1': mask_Bx1xSxS2_ik1, 'L0_attn_Wqkv': _L0_attn_in['Wqkv'], 'L0_attn_Wproj': _L0_attn_in['Wproj'], 'L0_xattn_W_out': _L0_xattn_in['W_out'], 'L0_xattn_b_out': _L0_xattn_in['b_out'], 'L0_ffn_router_w': _L0_ffn_in['router_w'], 'L0_ffn_w_gate': _L0_ffn_in['w_gate'], 'L0_ffn_w_up': _L0_ffn_in['w_up'], 'L0_ffn_w_down': _L0_ffn_in['w_down'], 'L1_attn_W_kv': _L1_attn_in['W_kv'], 'L1_attn_g_kv': _L1_attn_in['g_kv'], 'L1_attn_W_kdec': _L1_attn_in['W_kdec'], 'L1_attn_W_vdec': _L1_attn_in['W_vdec'], 'L1_attn_W_q': _L1_attn_in['W_q'], 'L1_attn_W_qdec': _L1_attn_in['W_qdec'], 'L1_attn_W_krope': _L1_attn_in['W_krope'], 'L1_attn_W_qrope': _L1_attn_in['W_qrope'], 'L1_attn_W_o': _L1_attn_in['W_o'], 'L1_xattn_Wq': _L1_xattn_in['Wq'], 'L1_xattn_bq': _L1_xattn_in['bq'], 'L1_xattn_Wk': _L1_xattn_in['Wk'], 'L1_xattn_bk': _L1_xattn_in['bk'], 'L1_xattn_Wv': _L1_xattn_in['Wv'], 'L1_xattn_bv': _L1_xattn_in['bv'], 'L1_xattn_Wo': _L1_xattn_in['Wo'], 'L1_xattn_bo': _L1_xattn_in['bo'], 'L1_ffn_Wqkv': _L1_ffn_in['Wqkv'], 'L1_ffn_bqkv': _L1_ffn_in['bqkv'], 'L1_ffn_Wo': _L1_ffn_in['Wo'], 'L1_ffn_bo': _L1_ffn_in['bo'], 'L1_ffn_g1': _L1_ffn_in['g1'], 'L1_ffn_be1': _L1_ffn_in['be1'], 'L1_ffn_g2': _L1_ffn_in['g2'], 'L1_ffn_be2': _L1_ffn_in['be2'], 'L1_ffn_Wg': _L1_ffn_in['Wg'], 'L1_ffn_W1': _L1_ffn_in['W1'], 'L1_ffn_b1': _L1_ffn_in['b1'], 'L1_ffn_W2': _L1_ffn_in['W2'], 'L1_ffn_b2': _L1_ffn_in['b2']}

def reference(x, ctx_1024, mask_Bx1x1xS2_if1, mask_Bx1xSxS2_ik1, L0_attn_Wqkv, L0_attn_Wproj, L0_xattn_W_out, L0_xattn_b_out, L0_ffn_router_w, L0_ffn_w_gate, L0_ffn_w_up, L0_ffn_w_down, L1_attn_W_kv, L1_attn_g_kv, L1_attn_W_kdec, L1_attn_W_vdec, L1_attn_W_q, L1_attn_W_qdec, L1_attn_W_krope, L1_attn_W_qrope, L1_attn_W_o, L1_xattn_Wq, L1_xattn_bq, L1_xattn_Wk, L1_xattn_bk, L1_xattn_Wv, L1_xattn_bv, L1_xattn_Wo, L1_xattn_bo, L1_ffn_Wqkv, L1_ffn_bqkv, L1_ffn_Wo, L1_ffn_bo, L1_ffn_g1, L1_ffn_be1, L1_ffn_g2, L1_ffn_be2, L1_ffn_Wg, L1_ffn_W1, L1_ffn_b1, L1_ffn_W2, L1_ffn_b2):
    import jax
    import jax.numpy as jnp

    def _L0_attn_ref(x, Wqkv, Wproj):
        import jax, jax.numpy as jnp
        import numpy as np
        B, S, D = (2, 256, 128)
        N_HEADS = 16
        HEAD_DIM = D // N_HEADS
        WINDOW = 128
        STRIDE = 64

        def _sparse_mask(s):
            row = jnp.arange(s)[:, None]
            col = jnp.arange(s)[None, :]
            causal = col <= row
            in_window = (col >= row - WINDOW + 1) & causal
            is_global = (col % STRIDE == 0) & causal
            return in_window | is_global
        b, s, d = x.shape
        qkv = (x @ Wqkv).reshape(b, s, 3, N_HEADS, HEAD_DIM)
        q, k, v = (qkv[:, :, 0], qkv[:, :, 1], qkv[:, :, 2])
        scale = 1.0 / HEAD_DIM ** 0.5
        att = jnp.einsum('bshd,bthd->bhst', q, k) * scale
        can_attend = _sparse_mask(s)
        att = jnp.where(can_attend[None, None], att, -jnp.inf)
        att = jax.nn.softmax(att, axis=-1)
        att = jnp.nan_to_num(att, nan=0.0)
        y = jnp.einsum('bhst,bthd->bshd', att, v).reshape(b, s, d)
        return y @ Wproj

    def _L0_xattn_ref(values, keys, query, mask, W_out, b_out):
        import jax, jax.numpy as jnp
        import numpy as np
        NUM_HEADS = 16
        EMBED = 128
        N, S = (4, 256)
        n, q_len, e = query.shape
        h = NUM_HEADS
        d = e // h
        v = values.reshape(n, -1, h, d)
        k = keys.reshape(n, -1, h, d)
        q = query.reshape(n, q_len, h, d)
        sim = jnp.einsum('nqhd,nkhd->nhqk', q, k)
        sim = jnp.where(mask == 0, -jnp.inf, sim)
        attn = jax.nn.softmax(sim / jnp.sqrt(jnp.float32(e)), axis=3)
        out = jnp.einsum('nhqk,nkhd->nqhd', attn, v).reshape(n, q_len, e)
        return out @ W_out.T + b_out

    def _L0_ffn_ref(hidden_states, router_w, w_gate, w_up, w_down):
        import jax, jax.numpy as jnp
        import numpy as np
        JITTER_EPS = 0.01
        NEG_INF = -jnp.inf

        def sparsemixer_eval(scores, jitter_eps):
            m1 = jnp.max(scores, axis=-1, keepdims=True)
            ind1 = jnp.argmax(scores, axis=-1)
            factor1 = jnp.maximum(jnp.abs(scores), m1)
            mask1 = jax.lax.stop_gradient((m1 - scores) / factor1 > 2.0 * jitter_eps)
            gates1 = jax.nn.softmax(jnp.where(mask1, NEG_INF, scores), axis=-1)
            mult1 = jnp.take_along_axis(gates1, ind1[:, None], axis=-1)[:, 0]
            E = scores.shape[-1]
            onehot1 = ind1[:, None] == jnp.arange(E)[None, :]
            masked_scores = jnp.where(onehot1, NEG_INF, scores)
            m2 = jnp.max(masked_scores, axis=-1, keepdims=True)
            ind2 = jnp.argmax(masked_scores, axis=-1)
            factor2 = jnp.maximum(jnp.abs(scores), m2)
            mask2 = jax.lax.stop_gradient((m2 - scores) / factor2 > 2.0 * jitter_eps)
            gates2 = jax.nn.softmax(jnp.where(mask2, NEG_INF, masked_scores), axis=-1)
            mult2 = jnp.take_along_axis(gates2, ind2[:, None], axis=-1)[:, 0]
            multiplier = jnp.stack([mult1, mult2], axis=-1)
            selected = jnp.stack([ind1, ind2], axis=-1)
            return (multiplier, selected)
        B, S, H = hidden_states.shape
        E = router_w.shape[0]
        x = hidden_states.reshape(-1, H)
        T = x.shape[0]
        logits = x @ router_w.T
        routing_weights, selected = sparsemixer_eval(logits, JITTER_EPS)
        tok = jnp.arange(T)
        dense_w = jnp.zeros((T, E), dtype=x.dtype)
        dense_w = dense_w.at[tok, selected[:, 0]].add(routing_weights[:, 0])
        dense_w = dense_w.at[tok, selected[:, 1]].add(routing_weights[:, 1])
        out = jnp.zeros_like(x)
        for e in range(E):
            h = jax.nn.silu(x @ w_gate[e].T) * (x @ w_up[e].T)
            out = out + dense_w[:, e:e + 1] * (h @ w_down[e].T)
        return out.reshape(B, S, H)

    def _L1_attn_ref(x, W_kv, g_kv, W_kdec, W_vdec, W_q, W_qdec, W_krope, W_qrope, W_o):
        import jax, jax.numpy as jnp
        import numpy as np
        N_EMBD = 128
        N_HEAD = 16
        HEAD_DIM = N_EMBD // N_HEAD
        KV_RANK = 32
        Q_RANK = 64
        ROPE_DIM = 32
        B, T = (2, 256)
        EPS = 1e-06

        def _rope_tables(T, dim):
            inv_freq = 1.0 / 10000.0 ** (np.arange(0, dim, 2, dtype=np.float32) / dim)
            t = np.arange(T, dtype=np.float32)
            freqs = np.outer(t, inv_freq)
            emb = np.concatenate([freqs, freqs], -1)
            return (jnp.asarray(np.cos(emb)), jnp.asarray(np.sin(emb)))

        def _apply_rope(x, cos, sin):
            d2 = x.shape[-1] // 2
            x1, x2 = (x[..., :d2], x[..., d2:])
            rot = jnp.concatenate([-x2, x1], axis=-1)
            return x * cos[None, None, :, :] + rot * sin[None, None, :, :]
        Bx, Tx, C = x.shape
        kv_c = x @ W_kv
        kv_c = kv_c * jax.lax.rsqrt(jnp.mean(kv_c * kv_c, axis=-1, keepdims=True) + EPS) * g_kv
        q_c = x @ W_q

        def heads(y, d):
            return y.reshape(Bx, Tx, N_HEAD, d).transpose(0, 2, 1, 3)
        k_content = heads(kv_c @ W_kdec, HEAD_DIM)
        v = heads(kv_c @ W_vdec, HEAD_DIM)
        q_content = heads(q_c @ W_qdec, HEAD_DIM)
        k_rope = heads(x @ W_krope, ROPE_DIM)
        q_rope = heads(q_c @ W_qrope, ROPE_DIM)
        cos, sin = _rope_tables(Tx, ROPE_DIM)
        q_rope = _apply_rope(q_rope, cos, sin)
        k_rope = _apply_rope(k_rope, cos, sin)
        q = jnp.concatenate([q_content, q_rope], axis=-1)
        k = jnp.concatenate([k_content, k_rope], axis=-1)
        scale = 1.0 / jnp.sqrt(jnp.float32(q.shape[-1]))
        scores = jnp.einsum('bhqd,bhkd->bhqk', q, k) * scale
        causal = jnp.tril(jnp.ones((Tx, Tx), dtype=bool))
        scores = jnp.where(causal[None, None], scores, jnp.float32(-jnp.inf))
        attn = jax.nn.softmax(scores, axis=-1)
        out = jnp.einsum('bhqk,bhkd->bhqd', attn, v)
        out = out.transpose(0, 2, 1, 3).reshape(Bx, Tx, N_HEAD * HEAD_DIM)
        return out @ W_o

    def _L1_xattn_ref(q, k, v, mask, Wq, bq, Wk, bk, Wv, bv, Wo, bo):
        import jax, jax.numpy as jnp
        import numpy as np
        EMB, HEADS = (128, 16)
        B, S = (4, 256)
        Bq, Sq, E = q.shape
        H = HEADS
        D = E // H
        Q = (q @ Wq.T + bq).reshape(Bq, Sq, H, D).transpose(0, 2, 1, 3)
        K = (k @ Wk.T + bk).reshape(Bq, -1, H, D).transpose(0, 2, 1, 3)
        V = (v @ Wv.T + bv).reshape(Bq, -1, H, D).transpose(0, 2, 1, 3)
        scores = jnp.einsum('bhqd,bhkd->bhqk', Q, K) / jnp.sqrt(jnp.float32(D))
        scores = jnp.where(mask == 1, jnp.float32(-1000000000.0), scores)
        attn = jax.nn.softmax(scores, axis=-1)
        out = jnp.einsum('bhqk,bhkd->bhqd', attn, V)
        out = out.transpose(0, 2, 1, 3).reshape(Bq, Sq, E)
        return out @ Wo.T + bo

    def _L1_ffn_ref(x, Wqkv, bqkv, Wo, bo, g1, be1, g2, be2, Wg, W1, b1, W2, b2):
        import jax, jax.numpy as jnp
        import numpy as np
        D = 128
        H = 4
        DF = 512
        E = 8
        EPS = 1e-05

        def _layer_norm(x, g, b):
            mu = jnp.mean(x, axis=-1, keepdims=True)
            var = jnp.mean(jnp.square(x - mu), axis=-1, keepdims=True)
            return (x - mu) * jax.lax.rsqrt(var + EPS) * g + b

        def _mha(x, Wqkv, bqkv, Wo, bo):
            S, B, _ = x.shape
            hd = D // H
            qkv = x @ Wqkv.T + bqkv
            q, k, v = jnp.split(qkv, 3, axis=-1)
            to_heads = lambda t: t.reshape(S, B, H, hd).transpose(1, 2, 0, 3)
            q, k, v = (to_heads(q), to_heads(k), to_heads(v))
            scores = jnp.einsum('bhqd,bhkd->bhqk', q, k) * (1.0 / np.sqrt(hd))
            att = jax.nn.softmax(scores, axis=-1)
            o = jnp.einsum('bhqk,bhkd->bhqd', att, v)
            o = o.transpose(2, 0, 1, 3).reshape(S, B, D)
            return o @ Wo.T + bo

        def _moe(x, Wg, W1, b1, W2, b2):
            S, B, _ = x.shape
            xf = x.reshape(S * B, D)
            logits = xf @ Wg.T
            idx = jnp.argmax(logits, axis=-1)
            out = jnp.zeros_like(xf)
            for e in range(E):
                m = (idx == e)[:, None].astype(xf.dtype)
                h = jax.nn.relu(xf @ W1[e] + b1[e])
                out = out + m * (h @ W2[e] + b2[e])
            return out.reshape(S, B, D)
        y = _layer_norm(x + _mha(x, Wqkv, bqkv, Wo, bo), g1, be1)
        z = _layer_norm(y + _moe(y, Wg, W1, b1, W2, b2), g2, be2)
        return z
    x = x + _L0_attn_ref(_layernorm(x, axis=-1), L0_attn_Wqkv, L0_attn_Wproj)
    x = x + _L0_xattn_ref(ctx_1024, ctx_1024, _layernorm(x, axis=-1), mask_Bx1x1xS2_if1, L0_xattn_W_out, L0_xattn_b_out)
    x = x + _L0_ffn_ref(_layernorm(x, axis=-1), L0_ffn_router_w, L0_ffn_w_gate, L0_ffn_w_up, L0_ffn_w_down)
    x = x + _L1_attn_ref(_layernorm(x, axis=-1), L1_attn_W_kv, L1_attn_g_kv, L1_attn_W_kdec, L1_attn_W_vdec, L1_attn_W_q, L1_attn_W_qdec, L1_attn_W_krope, L1_attn_W_qrope, L1_attn_W_o)
    x = x + _L1_xattn_ref(_layernorm(x, axis=-1), ctx_1024, ctx_1024, mask_Bx1xSxS2_ik1, L1_xattn_Wq, L1_xattn_bq, L1_xattn_Wk, L1_xattn_bk, L1_xattn_Wv, L1_xattn_bv, L1_xattn_Wo, L1_xattn_bo)
    x = x + _L1_ffn_ref(_layernorm(x, axis=-1), L1_ffn_Wqkv, L1_ffn_bqkv, L1_ffn_Wo, L1_ffn_bo, L1_ffn_g1, L1_ffn_be1, L1_ffn_g2, L1_ffn_be2, L1_ffn_Wg, L1_ffn_W1, L1_ffn_b1, L1_ffn_W2, L1_ffn_b2)
    return x

_drawn_inputs = setup_inputs


def setup_inputs(seed=0):
    import zlib

    import numpy as np

    out = dict(_drawn_inputs(seed))
    spreads = {'L1_attn_g_kv': (1.0, 0.2),
     'L1_xattn_bq': (0.0, 0.1),
     'L1_xattn_bk': (0.0, 0.8),
     'L1_xattn_bv': (0.0, 0.1),
     'L1_xattn_bo': (0.0, 0.1),
     'L1_ffn_bqkv': (0.0, 0.1),
     'L1_ffn_bo': (0.0, 0.1),
     'L1_ffn_g1': (1.0, 0.2),
     'L1_ffn_be1': (0.0, 0.1),
     'L1_ffn_g2': (1.0, 0.2),
     'L1_ffn_be2': (0.0, 0.1),
     'L1_ffn_b1': (0.0, 0.272),
     'L1_ffn_b2': (0.0, 0.1)}
    factors = {'L0_attn_Wqkv': 2.765, 'L0_attn_Wproj': 3.312}
    for name, (base, spread) in spreads.items():
        noise = np.random.default_rng([zlib.crc32(name.encode()), seed]).standard_normal(out[name].shape)
        drawn = base * np.exp(spread * noise) if base else spread * noise
        out[name] = jnp.asarray(drawn.astype(out[name].dtype))
    for name, factor in factors.items():
        out[name] = (out[name] * factor).astype(out[name].dtype)
    return out
```

```python
from contextlib import ExitStack, contextmanager

import numpy as np

import concourse.bass as bass
from concourse import mybir

F32 = mybir.dt.float32
BF16 = mybir.dt.bfloat16
I32 = mybir.dt.int32
ALU = mybir.AluOpType
ACT = mybir.ActivationFunctionType
AXX = mybir.AxisListType.X

P = 128
S = 1024
T = S // P
D = 128
H = 16
HD = D // H
S2 = 6404
NKB = -(-S2 // P)
LASTK = S2 - (NKB - 1) * P
E = 8
MASKED = -(2.0 ** 100)
PAIRS = ((0, 0), (0, 1), (0, 2), (1, 0), (1, 1), (2, 0))
CHUNK_PAIRS = (((0, 0), (0, 1), (1, 0)), ((0, 2), (2, 0), (1, 1)))


def static(x):
    return isinstance(x, int)


class Chain:

    def __init__(self, eng, sem, start=0):
        self.eng, self.sem, self.n = eng, sem, start

    def __call__(self, ins):
        ins.then_inc(self.sem, 1)
        self.n += 1
        self.eng.wait_ge(self.sem, self.n)


class Core:

    def __init__(self, nc, ctx):
        self.nc, self.ctx, self.names, self.sem_names = nc, ctx, {}, {}
        self.scopes = [(ctx, [])]
        self.X = self.sb(ctx, "X", [P, T, D], F32)
        self.ident = self.sb(ctx, "ident", [P, P], F32)
        self.identb = self.sb(ctx, "identb", [P, P], BF16)
        self.ps = ctx.enter_context(nc.psum_tensor("ps", [P, 8, 512], F32))

    def sb(self, ctx, name, shape, dt):
        self.names[name] = self.names.get(name, 0) + 1
        name += f"_{self.names[name]}"
        return ctx.enter_context(self.nc.sbuf_tensor(name, shape, dt))

    def sem(self, name):
        self.sem_names[name] = self.sem_names.get(name, 0) + 1
        s = self.scopes[-1][0].enter_context(self.nc.semaphore(f"{name}_{self.sem_names[name]}"))
        self.scopes[-1][1].append(s)
        return s

    @contextmanager
    def stage(self):
        with ExitStack() as ctx:
            self.scopes.append((ctx, []))
            yield
            _, sems = self.scopes.pop()
            with self.nc.Block() as block:
                @block.sync
                def _(sp):
                    for s in sems:
                        sp.sem_clear(s)


def start_block(core, x_dram, ident_dram):
    nc = core.nc
    loaded, copied = core.sem("start_loaded"), core.sem("start_copied")
    with nc.Block() as block:
        @block.sync
        def _(sp):
            sp.dma_start(core.X[:, :, :], x_dram.rearrange("a (t p) d -> p (a t) d", p=P)).then_inc(loaded, 16)
            sp.dma_start(core.ident[:, :], ident_dram).then_inc(loaded, 16)
            sp.wait_ge(loaded, 32)

        @block.vector
        def _(dve):
            dve.wait_ge(loaded, 32)
            nc.vector.tensor_copy(core.identb[:, :], core.ident[:, :]).then_inc(copied, 1)
            for b in range(8):
                nc.vector.memset(core.ps[:, b, :], 0.0).then_inc(copied, 1)
            dve.wait_ge(copied, 9)


def narrow(core, dst, src):
    done = core.sem("narrowed")
    with core.nc.Block() as block:
        @block.vector
        def _(dve):
            core.nc.vector.tensor_copy(dst, src).then_inc(done, 1)
            dve.wait_ge(done, 1)


class LayerNorm:

    def __init__(self, core, ctx):
        self.core = core
        sb = lambda n, s, d=F32: core.sb(ctx, n, s, d)
        self.stats, self.mv = sb("ln_stats", [P, T, 6]), sb("ln_mv", [P, T, 2])
        self.std, self.rstd = sb("ln_std", [P, T]), sb("ln_rstd", [P, T])
        self.dve_done = core.sem("ln_dve_done")
        self.var_ready, self.std_ready = core.sem("ln_var_ready"), core.sem("ln_std_ready")
        self.xn_ready, self.turned, self.hT_ready = core.sem("ln_xn_ready"), core.sem("ln_turned"), core.sem("ln_hT_ready")
        self.loaded = core.sem("ln_loaded")
        self.calls = self.chain_n = self.loads_n = 0

    def normalise(self, dve, link, src, dst, call, eps=1e-5):
        nc = self.core.nc
        for t in range(T):
            link(nc.vector.bn_stats(self.stats[:, t, :], src[:, t, :]))
        for t in range(T):
            link(nc.vector.bn_aggr(self.mv[:, t, :], self.stats[:, t, :]))
        nc.vector.tensor_scalar(self.mv[:, :, 1], self.mv[:, :, 1], eps, None, ALU.add).then_inc(self.var_ready, 1)
        dve.wait_ge(self.std_ready, call + 1)
        link(nc.vector.reciprocal(self.rstd[:, :], self.std[:, :]))
        for t in range(T):
            nc.vector.tensor_scalar(dst[:, t, :], src[:, t, :], self.mv[:, t, 0:1], self.rstd[:, t:t + 1],
                                    ALU.subtract, ALU.mult).then_inc(self.xn_ready, 1)
        dve.wait_ge(self.xn_ready, T * (call + 1))

    def root(self, act, call):
        act.wait_ge(self.var_ready, call + 1)
        self.core.nc.scalar.activation(self.std[:, :], self.mv[:, :, 1], ACT.Sqrt).then_inc(self.std_ready, 1)

    def turn(self, pe, call, src, banks=(0, 1)):
        core = self.core
        for t in range(T):
            pe.wait_ge(self.xn_ready, T * call + t + 1)
            core.nc.tensor.transpose(core.ps[:, banks[t // 4], (t % 4) * P:(t % 4 + 1) * P], src[:, t, :],
                                     core.ident[:, :]).then_inc(self.turned, 1)

    def take(self, act, call, hT, banks=(0, 1)):
        core = self.core
        for b in range(2):
            act.wait_ge(self.turned, T * call + 4 * (b + 1))
            core.nc.scalar.copy(hT[:, b * 512:(b + 1) * 512], core.ps[:, banks[b], :]).then_inc(self.hT_ready, 1)

    def block(self, hT, xn, loads):
        core, nc, call = self.core, self.core.nc, self.calls
        self.calls += 1
        with nc.Block() as block:
            @block.sync
            def _(sp):
                for dst, src in loads:
                    sp.dma_start(dst, src).then_inc(self.loaded, 16)
                    self.loads_n += 16
                sp.wait_ge(self.loaded, self.loads_n)

            @block.vector
            def _(dve):
                link = Chain(dve, self.dve_done, self.chain_n)
                self.normalise(dve, link, core.X, xn, call)
                self.chain_n = link.n

            @block.scalar
            def _(act):
                self.root(act, call)
                self.take(act, call, hT)

            @block.tensor
            def _(pe):
                self.turn(pe, call, xn)


class Turner:

    def __init__(self, core):
        self.core, self.n = core, 0
        self.turned, self.taken = core.sem("tw_turned"), core.sem("tw_taken")

    def block(self, pairs):
        core, nc, n0 = self.core, self.core.nc, self.n
        self.n += len(pairs)
        with nc.Block() as block:
            @block.tensor
            def _(pe):
                for n, (src, dst) in enumerate(pairs):
                    r, c = src.shape
                    if n >= 4:
                        pe.wait_ge(self.taken, n0 + n - 3)
                    nc.tensor.transpose(core.ps[0:c, n % 4, 0:r], src, core.ident[0:r, 0:r]).then_inc(self.turned, 1)

            @block.scalar
            def _(act):
                for n, (src, dst) in enumerate(pairs):
                    r, c = src.shape
                    act.wait_ge(self.turned, n0 + n + 1)
                    nc.scalar.copy(dst, core.ps[0:c, n % 4, 0:r]).then_inc(self.taken, 1)
                act.wait_ge(self.taken, n0 + len(pairs))


class Splitter:

    def buffers(self, ctx):
        core = self.core
        self.full = core.sb(ctx, "sp_full", [P, 2, 1024], F32)
        self.rest = core.sb(ctx, "sp_rest", [P, 2, 1024], F32)
        self.turned_part = core.sb(ctx, "sp_sin", [P, 1024], F32)
        self.parts = core.sb(ctx, "sp_parts", [P, 2, 3, 1024], BF16)
        return self

    def __init__(self, core):
        self.core = core
        self.projected, self.full_ready = core.sem("sp_projected"), core.sem("sp_full_ready")
        self.hi_ready, self.rest_ready = core.sem("sp_hi_ready"), core.sem("sp_rest_ready")
        self.mid_ready, self.lo_ready = core.sem("sp_mid_ready"), core.sem("sp_lo_ready")
        self.rope_done = core.sem("sp_rope_done")
        self.written = [core.sem("sp_written0"), core.sem("sp_written1")]
        self.count, self.ropes, self.writes = 0, 0, [0, 0]

    def block(self, items):
        core, nc = self.core, self.core.nc
        n0, r0, w0 = self.count, self.ropes, list(self.writes)
        assert n0 % 2 == 0
        self.count += len(items) + len(items) % 2
        pad = len(items) % 2
        ps = core.ps

        def done(par, upto):
            return w0[par] + 16 * sum(len(it[4]) for k, it in enumerate(items[:upto]) if k % 2 == par)

        with nc.Block() as block:
            @block.tensor
            def _(pe):
                for n, (w, matmuls, bias, rope, writes) in enumerate(items):
                    if n >= 2:
                        pe.wait_ge(self.full_ready, n0 + n - 1)
                    b = 4 * (n % 2)
                    matmuls(pe, ps[:, b:b + 2, :].rearrange("p b c -> p (b c)"),
                            ps[:, b + 2:b + 4, :].rearrange("p b c -> p (b c)")).then_inc(self.projected, 1 + pad * (n == len(items) - 1))

            @block.scalar
            def _(act):
                for n, (w, matmuls, bias, rope, writes) in enumerate(items):
                    b, q, last = 4 * (n % 2), n % 2, pad * (n == len(items) - 1)
                    if rope is None:
                        act.wait_ge(self.projected, n0 + n + 1)
                        if n >= 2:
                            act.wait_ge(self.rest_ready, n0 + n - 1)
                        src = ps[:, b:b + 2, :].rearrange("p b c -> p (b c)")[:, 0:w]
                        if bias is None:
                            ins = nc.scalar.copy(self.full[:, q, 0:w], src)
                        else:
                            ins = nc.scalar.activation(self.full[:, q, 0:w], src, ACT.Identity, bias=bias)
                        ins.then_inc(self.full_ready, 1 + last)
                    act.wait_ge(self.full_ready, n0 + n + 1)
                    if n >= 2:
                        act.wait_ge(self.written[q], done(q, n))
                    nc.scalar.copy(self.parts[:, q, 0, 0:w], self.full[:, q, 0:w]).then_inc(self.hi_ready, 1 + last)
                    act.wait_ge(self.rest_ready, n0 + n + 1)
                    nc.scalar.copy(self.parts[:, q, 1, 0:w], self.rest[:, q, 0:w]).then_inc(self.mid_ready, 1 + last)

            @block.vector
            def _(dve):
                ropes = r0
                for n, (w, matmuls, bias, rope, writes) in enumerate(items):
                    b, q, last = 4 * (n % 2), n % 2, pad * (n == len(items) - 1)
                    if rope is not None:
                        dve.wait_ge(self.projected, n0 + n + 1)
                        if n >= 2:
                            dve.wait_ge(self.rest_ready, n0 + n - 1)
                            dve.wait_ge(self.hi_ready, n0 + n - 1)
                        nc.vector.tensor_tensor(self.full[:, q, :], ps[:, b:b + 2, :].rearrange("p b c -> p (b c)"),
                                                rope[0], ALU.mult).then_inc(self.rope_done, 1)
                        nc.vector.tensor_tensor(self.turned_part[:, :], ps[:, b + 2:b + 4, :].rearrange("p b c -> p (b c)"),
                                                rope[1], ALU.mult).then_inc(self.rope_done, 1)
                        ropes += 2
                        dve.wait_ge(self.rope_done, ropes)
                        nc.vector.tensor_tensor(self.full[:, q, :], self.full[:, q, :], self.turned_part[:, :],
                                                ALU.add).then_inc(self.full_ready, 1 + last)
                    dve.wait_ge(self.full_ready, n0 + n + 1)
                    dve.wait_ge(self.hi_ready, n0 + n + 1)
                    nc.vector.tensor_tensor(self.rest[:, q, 0:w], self.full[:, q, 0:w], self.parts[:, q, 0, 0:w],
                                            ALU.subtract).then_inc(self.rest_ready, 1 + last)
                    dve.wait_ge(self.mid_ready, n0 + n + 1)
                    nc.vector.tensor_tensor(self.parts[:, q, 2, 0:w], self.rest[:, q, 0:w], self.parts[:, q, 1, 0:w],
                                            ALU.subtract).then_inc(self.lo_ready, 1 + last)
                self.ropes = ropes

            @block.sync
            def _(sp):
                for n, (w, matmuls, bias, rope, writes) in enumerate(items):
                    sp.wait_ge(self.lo_ready, n0 + n + 1)
                    for dst, part in writes:
                        sp.dma_start(dst, self.parts[:, n % 2, part, 0:w]).then_inc(self.written[n % 2], 16)
                for q in range(2):
                    self.writes[q] = done(q, len(items))
                    sp.wait_ge(self.written[q], self.writes[q])


def project(core, w, hT, width=1024, at=0):
    def matmuls(pe, a, b):
        for c in range(0, width, 512):
            n = min(512, width - c)
            last = core.nc.tensor.matmul(a[:, c:c + n], w, hT[:, at + c:at + c + n], start=True, stop=True)
        return last
    return matmuls


def project_two(core, w, turned, hT):
    def matmuls(pe, a, b):
        for dst, weights in ((a, w), (b, turned)):
            for c in range(0, S, 512):
                last = core.nc.tensor.matmul(dst[:, c:c + 512], weights, hT[:, c:c + 512], start=True, stop=True)
        return last
    return matmuls


def values_block(core, name, Vaug, tiles, bias_rows=None):
    nc = core.nc
    ones, made, taken = core.sem(name + "_ones"), core.sem(name + "_made"), core.sem(name + "_taken")
    with nc.Block() as block:
        @block.gpsimd
        def _(pool):
            nc.gpsimd.memset(Vaug[:, :, :, :], 0.0).then_inc(ones, 1)
            pool.wait_ge(ones, 1)
            for h in range(H):
                nc.gpsimd.memset(Vaug[:, h, :, HD:HD + 1], 1.0).then_inc(ones, 1)
            pool.wait_ge(ones, 1 + H)

        @block.tensor
        def _(pe):
            for t, (rows, lhsT, rhs) in enumerate(tiles):
                if t >= 8:
                    pe.wait_ge(taken, t - 7)
                nc.tensor.matmul(core.ps[0:rows, t % 8, 0:D], lhsT, rhs, start=True, stop=True).then_inc(made, 1)

        @block.vector
        def _(dve):
            dve.wait_ge(ones, 1 + H)
            for t, (rows, lhsT, rhs) in enumerate(tiles):
                dve.wait_ge(made, t + 1)
                dst = Vaug[0:rows, :, t, 0:HD]
                src = core.ps[0:rows, t % 8, 0:D].rearrange("p (h d) -> p h d", h=H)
                if bias_rows is None:
                    nc.vector.tensor_copy(dst, src).then_inc(taken, 1)
                else:
                    nc.vector.tensor_tensor(dst, src, bias_rows[0:rows, :].rearrange("p (h d) -> p h d", h=H),
                                            ALU.add).then_inc(taken, 1)
            dve.wait_ge(taken, len(tiles))


def negated_max_parts(nc, link, mx, m, rest, parts, done):
    link(nc.vector.tensor_reduce(m, mx, AXX, ALU.max))
    link(nc.vector.tensor_scalar(parts[:, 0, :], m, -1.0, None, ALU.mult))
    link(nc.vector.scalar_tensor_tensor(rest, m, -1.0, parts[:, 0, :], ALU.mult, ALU.subtract))
    link(nc.vector.tensor_copy(parts[:, 1, :], rest))
    nc.vector.tensor_tensor(parts[:, 2, :], rest, parts[:, 1, :], ALU.subtract).then_inc(done, 1)


class SelfAttention:

    def __init__(self, core, name, chunks, fills, tiles, slots):
        self.core, self.name, self.chunks, self.fills, self.tiles, self.slots = core, name, chunks, fills, tiles, slots

    def run(self, ctx, loads, Vaug, Vglob, scale, O_dram):
        core, nc, name = self.core, self.core.nc, self.name
        ps, ident = core.ps, core.identb
        nt, nf = len(self.tiles), len(self.fills)
        sb = lambda n, s, d: core.sb(ctx, name + n, s, d)
        sem = lambda n: core.sem(name + n)
        nch = self.chunks
        Qa = [sb(f"Qa{p}", [P, nch, S], BF16) for p in range(2)]
        Qb = [sb(f"Qb{p}", [P, nch, S], BF16) for p in range(2)]
        Ka = [sb(f"Ka{p}", [P, nch, S], BF16) for p in range(2)]
        Kb = [sb(f"Kb{p}", [P, nch, S], BF16) for p in range(2)]
        V = [sb(f"V{p}", [P, T, HD + 1], F32) for p in range(2)]
        VG = [sb(f"VG{p}", [P, HD + 1], F32) for p in range(2)]
        Pt = [sb(f"P{u}", [P, S], F32) for u in range(nt)]
        O = sb("O", [P, S], F32)
        mx = [sb(f"mx{p}", [P, T, self.slots], F32) for p in range(2)]
        m, rest = sb("m", [P, T], F32), sb("rest", [P, T], F32)
        mparts = [sb(f"mparts{p}", [P, 3, T], BF16) for p in range(2)]
        cleared = sem("cleared")
        qa_ready = [sem(f"qa_ready{p}") for p in range(2)]
        qb_ready = [sem(f"qb_ready{p}") for p in range(2)]
        scores_ready, exp_done, p_used = sem("scores_ready"), sem("exp_done"), sem("p_used")
        fill_ready, fill_taken = sem("fill_ready"), sem("fill_taken")
        maxes_ready, rows_ready, rows_copied = sem("maxes_ready"), sem("rows_ready"), sem("rows_copied")
        o_copied, o_written, v_ready, vec = sem("o_copied"), sem("o_written"), sem("v_ready"), sem("vec")
        vg_ready = sem("vg_ready")
        slots = Qa + Qb + Ka + Kb

        with nc.Block() as block:
            @block.gpsimd
            def _(pool):
                for n, t in enumerate(slots):
                    nc.gpsimd.memset(t[:, :, :], 0.0).then_inc(cleared, 1)
                for t in VG:
                    nc.gpsimd.memset(t[:, :], 0.0).then_inc(cleared, 1)
                for t in mx:
                    nc.gpsimd.memset(t[:, :, :], MASKED).then_inc(cleared, 1)
                for t in Pt:
                    nc.gpsimd.memset(t[:, :], 0.0).then_inc(cleared, 1)
                n = len(slots) + len(VG) + len(mx) + nt
                pool.wait_ge(cleared, n)
                for t in Kb:
                    nc.gpsimd.memset(t[96:99, 0, :], 1.0).then_inc(cleared, 1)
                pool.wait_ge(cleared, n + 2)

            @block.vector
            def _(dve):
                for b in (4, 5):
                    nc.vector.memset(ps[:, b, :], 0.0).then_inc(vec, 1)
                dve.wait_ge(vec, 2)

            @block.sync
            def _(sp):
                sp.sem_inc(fill_ready, 2 * nf)
                sp.sem_inc(scores_ready, 2 * nt)
                sp.sem_inc(exp_done, 2)
                sp.sem_inc(fill_taken, 2)
                sp.sem_inc(p_used, 2 * nt)
                sp.sem_inc(o_copied, 1)
                sp.sem_inc(o_written, 4 * 16)

        def load(sp, dst, kind, g, ready):
            for rows, src in loads[kind]:
                sp.dma_start(dst[rows[0]:rows[1], :, :], src(g)).then_inc(ready, 16)

        nq, nk = len(loads["q"]), len(loads["k"])

        with nc.Block() as block:
            @block.sync
            def _(sp):
                with sp.Fori(0, H // 2) as i:
                    for p in range(2):
                        g = i * 2 + p
                        sp.wait_ge(fill_ready, g * nf + nf)
                        load(sp, Qa[p], "q", g, qa_ready[p])
                        load(sp, Ka[p], "k", g, qa_ready[p])
                        sp.wait_ge(scores_ready, g * nt + nt)
                        load(sp, Qb[p], "q", g, qb_ready[p])
                        load(sp, Kb[p], "k", g, qb_ready[p])

            @block.gpsimd
            def _(pool):
                with pool.Fori(0, H // 2) as i:
                    for p in range(2):
                        g = i * 2 + p
                        pool.wait_ge(p_used, g * nt + nt)
                        nc.gpsimd.tensor_copy(V[p][:, :, :], Vaug[:, bass.ds(g, 1), :, :].rearrange(
                            "p a t c -> p (a t) c")).then_inc(v_ready, 1)
                        if Vglob is not None:
                            nc.gpsimd.tensor_copy(VG[p][0:16, :], Vglob[0:16, bass.ds(g, 1), :].rearrange(
                                "p a c -> p (a c)")).then_inc(vg_ready, 1)

            def fill_scores(pe, g, p, f, i):
                n = (p * nf + f) % 2
                pe.wait_ge(fill_taken, g * nf + f + 1)
                if f == 0:
                    pe.wait_ge(qa_ready[p], (i + 1) * 16 * (nq + nk))
                for k, (kind, a, b, col, w) in enumerate(self.fills[f][0]):
                    dst = ps[:, 6 + n, col:col + w]
                    if kind == "mask":
                        last = nc.tensor.matmul(dst, ident[:, :], b, start=(k == 0), stop=False, skip_group_check=True)
                        continue
                    for c in range(nch):
                        rhs = b(Ka[p][:, c, :])
                        last = nc.tensor.matmul(dst, Qa[p][:, c, a * P:(a + 1) * P], rhs, start=(k == 0 and c == 0),
                                                stop=False, skip_group_check=True)
                last.then_inc(fill_ready, 1)

            def max_rows(pe, g, p):
                pe.wait_ge(maxes_ready, g + 1)
                for t in range(T):
                    last = nc.tensor.matmul(ps[96:99, 6 + t // 4, (t % 4) * P:(t % 4 + 1) * P], mparts[p][:, :, t],
                                            ident[:, :], start=(t % 4 == 0), stop=False, skip_group_check=True)
                last.then_inc(rows_ready, 1)

            def tile_scores(pe, g, p, u, i):
                n = (p * nt + u) % 2
                pe.wait_ge(exp_done, g * nt + u + 1)
                if u == 0:
                    pe.wait_ge(qb_ready[p], (i + 1) * 16 * (nq + nk))
                    pe.wait_ge(rows_copied, g + 1)
                begun = set()
                for kind, a, b, col, w in self.tiles[u]["scores"]:
                    bank, rows = 2 * n + col // 512, self.tiles[u]["rows"]
                    dst = ps[0:rows, bank, col % 512:col % 512 + w]
                    if kind == "mask":
                        last = nc.tensor.matmul(dst, ident[:, 0:rows], b, start=bank not in begun, stop=False,
                                                skip_group_check=True)
                        begun.add(bank)
                        continue
                    for c in range(nch):
                        last = nc.tensor.matmul(dst, a(Kb[p][:, c, :]), Qb[p][:, c, b:b + w], start=bank not in begun,
                                                stop=False, skip_group_check=True)
                        begun.add(bank)
                last.then_inc(scores_ready, 1)

            def tile_values(pe, g, p, u, begun):
                pe.wait_ge(exp_done, 2 + g * nt + u + 1)
                if u == 0:
                    pe.wait_ge(v_ready, g + 1)
                    if Vglob is not None:
                        pe.wait_ge(vg_ready, g + 1)
                    pe.wait_ge(o_copied, g + 1)
                for col, w, kb, j, q0 in self.tiles[u]["values"]:
                    key = (q0 // 512, j)
                    lhsT = VG[p][:, :] if kb is None else V[p][:, kb, :]
                    last = nc.tensor.matmul(ps[32 * j:32 * j + HD + 1, 4 + q0 // 512, q0 % 512:q0 % 512 + w], lhsT,
                                            Pt[u][:, col:col + w], start=key not in begun, stop=False,
                                            skip_group_check=True)
                    begun.add(key)
                last.then_inc(p_used, 1)

            @block.tensor
            def _(pe):
                for f in range(nf):
                    fill_scores(pe, 0, 0, f, 0)
                max_rows(pe, 0, 0)

                def head(g, p, i, more):
                    begun = set()
                    f = 0
                    for u in range(nt):
                        tile_scores(pe, g, p, u, i)
                        while more and f < (u + 1) * nf // nt:
                            fill_scores(pe, g + 1, 1 - p, f, i + p)
                            f += 1
                        if u >= 1:
                            tile_values(pe, g, p, u - 1, begun)
                    tile_values(pe, g, p, nt - 1, begun)
                    if more:
                        max_rows(pe, g + 1, 1 - p)
                with pe.Fori(0, H // 2 - 1) as i:
                    head(i * 2, 0, i, True)
                    head(i * 2 + 1, 1, i, True)
                head(H - 2, 0, H // 2 - 1, True)
                head(H - 1, 1, H // 2 - 1, False)

            @block.vector
            def _(dve):
                def maxima(g, p, base):
                    for f in range(nf):
                        dve.wait_ge(fill_ready, g * nf + (2 * nf + f + 1))
                        reds = self.fills[f][1]
                        for k, (col, w, nseg, dst) in enumerate(reds):
                            src = ps[:, 6 + (p * nf + f) % 2, col:col + w]
                            out = mx[p][:, dst[0]:dst[0] + nseg, dst[1]]
                            ins = nc.vector.tensor_reduce(out, src.rearrange("p (n w) -> p n w", n=nseg), AXX, ALU.max)
                            if k == len(reds) - 1:
                                ins.then_inc(fill_taken, 1)
                            else:
                                ins.then_inc(vec, 1)
                    dve.wait_ge(fill_taken, 2 + (g + 1) * nf)
                    extra = sum(len(x[1]) - 1 for x in self.fills)
                    n = 4 + extra
                    start = 2 + g * n + extra
                    if extra:
                        dve.wait_ge(vec, start)
                    link = Chain(dve, vec, start)
                    negated_max_parts(nc, link, mx[p][:, :, :], m[:, :], rest[:, :], mparts[p], maxes_ready)
                    dve.wait_ge(maxes_ready, g + 1)
                maxima(0, 0, 0)
                with dve.Fori(0, H // 2 - 1) as i:
                    maxima(i * 2 + 1, 1, 0)
                    maxima(i * 2 + 2, 0, 0)
                maxima(H - 1, 1, 0)

            @block.scalar
            def _(act):
                def rows(g, p):
                    act.wait_ge(rows_ready, g + 1)
                    nc.scalar.copy(Qb[p][96:99, 0, :], ps[96:99, 6:8, :].rearrange("p b c -> p (b c)")).then_inc(rows_copied, 1)

                def head(g, p, more):
                    for u in range(nt):
                        n, r, w = (p * nt + u) % 2, self.tiles[u]["rows"], self.tiles[u]["width"]
                        act.wait_ge(scores_ready, g * nt + (2 * nt + u + 1))
                        act.wait_ge(p_used, g * nt + (nt + u + 1))
                        nc.scalar.activation(Pt[u][0:r, 0:w], ps[0:r, 2 * n:2 * n + 2, :].rearrange(
                            "p b c -> p (b c)")[:, 0:w], ACT.Exp, scale=scale).then_inc(exp_done, 1)
                    act.wait_ge(p_used, g * nt + 3 * nt)
                    act.wait_ge(o_written, (g + 1) * 64)
                    nc.scalar.copy(O[:, :], ps[:, 4:6, :].rearrange("p b c -> p (b c)")).then_inc(o_copied, 1)
                    act.wait_ge(o_copied, 1 + g + 1)
                    for j in range(4):
                        act.dma_start(O_dram[bass.ds(g, 1), j].rearrange("a r c -> (a r) c"),
                                      O[32 * j:32 * j + HD + 1, :]).then_inc(o_written, 16)
                    if more:
                        rows(g + 1, 1 - p)
                rows(0, 0)
                with act.Fori(0, H // 2 - 1) as i:
                    head(i * 2, 0, True)
                    head(i * 2 + 1, 1, True)
                head(H - 2, 0, True)
                head(H - 1, 1, False)
                act.wait_ge(o_written, (H + 1) * 64)


class Combiner:

    def __init__(self, core):
        self.core = core
        self.loaded, self.vec = core.sem("cb_loaded"), core.sem("cb_vec")
        self.y_ready, self.proj, self.added = core.sem("cb_y_ready"), core.sem("cb_proj"), core.sem("cb_added")
        self.calls = self.loads = self.chain = 0

    def block(self, Osum, Ssum, tmp, parts, W, bias_rows):
        core, nc, call = self.core, self.core.nc, self.calls
        self.calls += 1
        loads0 = self.loads
        n_each = 2 * len(parts[0])
        self.loads += 16 * n_each * len(parts)
        with nc.Block() as block:
            @block.sync
            def _(sp):
                for j, part in enumerate(parts):
                    for (c0, c1), o_src, s_src in part:
                        sp.dma_start(Osum[:, j, c0:c1], o_src).then_inc(self.loaded, 16)
                        sp.dma_start(Ssum[:, j, c0:c1], s_src).then_inc(self.loaded, 16)
                sp.wait_ge(self.loaded, self.loads)

            @block.vector
            def _(dve):
                link = Chain(dve, self.vec, self.chain)
                dve.wait_ge(self.loaded, self.loads)
                for j in range(1, len(parts)):
                    link(nc.vector.tensor_tensor(Osum[:, 0, :], Osum[:, 0, :], Osum[:, j, :], ALU.add))
                    link(nc.vector.tensor_tensor(Ssum[:, 0, :], Ssum[:, 0, :], Ssum[:, j, :], ALU.add))
                link(nc.vector.reciprocal(Ssum[:, 0, :], Ssum[:, 0, :]))
                nc.vector.tensor_tensor(tmp[:, :], Osum[:, 0, :], Ssum[:, 0, :], ALU.mult).then_inc(self.y_ready, 1)
                for t in range(T):
                    if bias_rows is not None:
                        link(nc.vector.tensor_tensor(core.X[:, t, :], core.X[:, t, :], bias_rows, ALU.add))
                    dve.wait_ge(self.proj, T * call + t + 1)
                    nc.vector.tensor_tensor(core.X[:, t, :], core.X[:, t, :], core.ps[:, t, 0:D],
                                            ALU.add).then_inc(self.added, 1)
                dve.wait_ge(self.added, T * (call + 1))
                self.chain = link.n

            @block.tensor
            def _(pe):
                pe.wait_ge(self.y_ready, call + 1)
                for t in range(T):
                    nc.tensor.matmul(core.ps[:, t, 0:D], tmp[:, t * P:(t + 1) * P], W, start=True,
                                     stop=True).then_inc(self.proj, 1)


class CrossAttention:

    SQ = 512
    NU = (NKB + 1) // 2
    CH = [0, 1536, 3072, 4608, S2]
    CH_LAST_TILE = [5, 11, 17, 25]
    NPC = -(-S2 // 512)
    LEAD = 10
    NP = 4 * NPC

    def __init__(self, core, ctx, name, scale, masked):
        self.core, self.name, self.scale, self.masked = core, name, scale, masked
        sb = lambda n, s, d: core.sb(ctx, name + n, s, d)
        sem = lambda n: core.sem(name + n)
        SQ = self.SQ
        self.K = [sb(f"K{p}", [P, S2], BF16) for p in range(2)]
        self.Qa = [sb(f"Qa{p}", [P, SQ], BF16) for p in range(2)]
        self.Qb = [sb(f"Qb{p}", [P, SQ], BF16) for p in range(2)]
        self.V = [sb(f"V{p}", [P, NKB, HD + 1], F32) for p in range(2)]
        self.Pt = sb("P", [P, 4, 2 * SQ], F32)
        self.O = [sb(f"O{p}", [P, SQ], F32) for p in range(2)]
        self.mx = [sb(f"mx{p}", [P, 4, self.NPC], F32) for p in range(2)]
        self.m, self.rest = sb("m", [P, 4], F32), sb("rest", [P, 4], F32)
        self.mparts = [sb(f"mparts{p}", [P, 3, 4], BF16) for p in range(2)]
        self.junk = sb("junk", [P, 2, SQ], BF16) if masked else None
        self.cleared = sem("cleared")
        self.k_ready = [[sem(f"k_ready{p}{c}") for c in range(4)] for p in range(2)]
        self.qa_ready = [sem(f"qa_ready{p}") for p in range(2)]
        self.qb_ready = [sem(f"qb_ready{p}") for p in range(2)]
        self.scores_ready, self.exp_done, self.p_used = sem("scores_ready"), sem("exp_done"), sem("p_used")
        self.piece_ready, self.piece_taken = sem("piece_ready"), sem("piece_taken")
        self.maxes_ready, self.rows_ready, self.rows_copied = sem("maxes_ready"), sem("rows_ready"), sem("rows_copied")
        self.o_copied, self.piece_seen = sem("o_copied"), sem("piece_seen")
        self.o_written = [sem(f"o_written{p}") for p in range(2)]
        self.v_ready, self.vec = sem("v_ready"), sem("vec")

    def clear_block(self, bias_row):
        core, nc = self.core, self.core.nc
        tiles = self.K + self.Qa + self.Qb + self.O
        bias_loaded = core.sem(self.name + "bias_loaded")
        with nc.Block() as block:
            @block.gpsimd
            def _(pool):
                for t in tiles:
                    nc.gpsimd.memset(t[:, :], 0.0).then_inc(self.cleared, 1)
                pool.wait_ge(self.cleared, 8)
                for t in self.K:
                    nc.gpsimd.memset(t[96:99, :], 1.0).then_inc(self.cleared, 1)
                for t in self.Qa + self.Qb:
                    nc.gpsimd.memset(t[64:65, :], 1.0).then_inc(self.cleared, 1)
                pool.wait_ge(self.cleared, 14)

            @block.vector
            def _(dve):
                for b in (4, 7):
                    nc.vector.memset(core.ps[:, b, :], 0.0).then_inc(self.vec, 1)
                dve.wait_ge(self.vec, 2)

            @block.sync
            def _(sp):
                sp.wait_ge(self.cleared, 14)
                if bias_row is not None:
                    for t in self.K:
                        sp.dma_start(t[64:65, :], bias_row).then_inc(bias_loaded, 16)
                    sp.wait_ge(bias_loaded, 32)
                sp.sem_inc(self.piece_ready, 2 * self.NP)
                sp.sem_inc(self.scores_ready, 2 * self.NU)
                sp.sem_inc(self.exp_done, 2)
                sp.sem_inc(self.p_used, self.NU + 4)
                sp.sem_inc(self.piece_taken, 2)
                sp.sem_inc(self.o_copied, 2)

    def block(self, halves, Qs, Ks, Vaug, O_dram, nat=None, maskT=None):
        core, nc = self.core, self.core.nc
        ps, ident, SQ, NU, NPC = core.ps, core.identb, self.SQ, self.NU, self.NPC
        K, Qa, Qb, V, Pt, O, mx, mparts = self.K, self.Qa, self.Qb, self.V, self.Pt, self.O, self.mx, self.mparts
        NP = self.NP
        LEAD = self.LEAD
        g0, i0, i1 = H * halves[0], H * halves[0] // 2, H * (halves[-1] + 1) // 2
        end = 2 * i1
        vec0 = 2

        with nc.Block() as block:
            @block.sync
            def _(sp):
                def store(g, p):
                    sp.wait_ge(self.o_copied, g + 1)
                    for j in range(4):
                        sp.dma_start(O_dram[bass.ds(g, 1), j].rearrange("a r c -> (a r) c"),
                                     O[1 - p][32 * j:32 * j + HD + 1, :]).then_inc(self.o_written[1 - p], 16)

                for half in halves:
                  with sp.Fori(half * H // 2, (half + 1) * H // 2) as i:
                    for p in range(2):
                        g = i * 2 + p
                        h = i * 2 + (p - half * H)
                        src = Qs[bass.ds(h, 1), :, half * SQ:(half + 1) * SQ].rearrange("a r c -> (a r) c")
                        sp.wait_ge(self.piece_ready, g * NP + NP)
                        sp.dma_start(Qa[p][0:48, :], src).then_inc(self.qa_ready[p], 16)
                        store(g, p)
                        for c in range(4):
                            sp.wait_ge(self.scores_ready, g * NU + (self.CH_LAST_TILE[c] + 1))
                            a, b = self.CH[c], self.CH[c + 1]
                            sp.dma_start(K[p][0:48, a:b], Ks[bass.ds(h, 1), :, a:b].rearrange(
                                "a r c -> (a r) c")).then_inc(self.k_ready[p][c], 16)
                        sp.dma_start(Qb[p][0:48, :], src).then_inc(self.qb_ready[p], 16)
                if halves[-1] == 1:
                    for g in range(2 * H, 2 * H + 3):
                        store(g, g % 2)
                    sp.wait_ge(self.o_written[0], 64 * (H + 1))
                    sp.wait_ge(self.o_written[1], 64 * (H + 2))

            @block.gpsimd
            def _(pool):
                for half in halves:
                  with pool.Fori(half * H // 2, (half + 1) * H // 2) as i:
                    for p in range(2):
                        g = i * 2 + p
                        pool.wait_ge(self.p_used, g * NU + 4)
                        nc.gpsimd.tensor_copy(V[p][:, :, :], Vaug[:, bass.ds(i * 2 + (p - half * H), 1), :, :].rearrange(
                            "p a t c -> p (a t) c")).then_inc(self.v_ready, 1)

            @block.tensor
            def _(pe):
                def piece(g, p, k, i):
                    c, t = k // 4, k % 4
                    w = min(512, S2 - c * 512)
                    pe.wait_ge(self.piece_taken, g * NP + (k + 1))
                    if k == 0:
                        pe.wait_ge(self.qa_ready[p], i * 16 + 16)
                    if t == 0 and c * 512 in self.CH:
                        pe.wait_ge(self.k_ready[p][self.CH.index(c * 512)], i * 16 + 16)
                    ins = nc.tensor.matmul(ps[:, 5 + k % 2, 0:w], Qa[p][:, t * P:(t + 1) * P],
                                           K[p][:, c * 512:c * 512 + w], start=True, stop=True)
                    ins.then_inc(self.piece_ready, 1)

                def rows(g, p):
                    pe.wait_ge(self.maxes_ready, g + 1)
                    pe.wait_ge(self.o_copied, g + 2)
                    for t in range(4):
                        last = nc.tensor.matmul(ps[96:99, 4 + 3 * p, t * P:(t + 1) * P], mparts[p][:, :, t], ident[:, :],
                                                start=(t == 0), stop=False, skip_group_check=True)
                    last.then_inc(self.rows_ready, 1)

                def scores(g, p, u, i):
                    pe.wait_ge(self.exp_done, g * NU + (u + 1))
                    if u == 0:
                        pe.wait_ge(self.qb_ready[p], i * 16 + 16)
                        pe.wait_ge(self.rows_copied, g + 1)
                    for kb in range(2 * u, min(2 * u + 2, NKB)):
                        r = min(P, S2 - kb * P)
                        dst = ps[0:r, 2 * (u % 2) + kb % 2, :]
                        if self.masked:
                            nc.tensor.matmul(dst, ident[:, 0:r], maskT[:, kb, :], start=True, stop=False)
                        last = nc.tensor.matmul(dst, K[p][:, kb * P:kb * P + r], Qb[p][:, :],
                                                start=not self.masked, stop=True)
                    last.then_inc(self.scores_ready, 1)

                def values(g, p, q):
                    pe.wait_ge(self.exp_done, g * NU + (2 + 2 * q + 2))
                    if q == 0:
                        pe.wait_ge(self.v_ready, g + 1)
                    for kb in range(4 * q, min(4 * q + 4, NKB)):
                        r, u, j = min(P, S2 - kb * P), kb // 2, kb % 4
                        last = nc.tensor.matmul(ps[32 * j:32 * j + HD + 1, 4 + 3 * p, :], V[p][0:r, kb, :],
                                                Pt[0:r, (2 * p + u) % 4, (kb % 2) * SQ:(kb % 2 + 1) * SQ],
                                                start=(q == 0), stop=False, skip_group_check=True)
                    last.then_inc(self.p_used, 2)

                def step(g, p, i, more, more2):
                    pieces = [(g + 1, 1 - p, k, i + p) for k in range(LEAD, NP)] if more else []
                    pieces += [(g + 2, p, k, i + 1) for k in range(LEAD)] if more2 else []

                    def some(n):
                        for _ in range(min(n, len(pieces))):
                            piece(*pieces.pop(0))
                    for u in range(0, NU, 2):
                        scores(g, p, u, i)
                        some(1)
                        scores(g, p, u + 1, i)
                        some(1)
                        if u == NU - 2 and more:
                            rows(g + 1, 1 - p)
                        if u:
                            values(g, p, u // 2 - 1)
                        some(2)
                    values(g, p, NU // 2 - 1)

                for k in range(NP):
                    piece(g0, 0, k, i0)
                rows(g0, 0)
                for k in range(LEAD):
                    piece(g0 + 1, 1, k, i0)
                with pe.Fori(i0, i1 - 1) as i:
                    step(i * 2, 0, i, True, True)
                    step(i * 2 + 1, 1, i, True, True)
                step(end - 2, 0, i1 - 1, True, False)
                step(end - 1, 1, i1 - 1, False, False)

            @block.vector
            def _(dve):
                def maxima(g, p, pieces):
                    for k in pieces:
                        c, t = k // 4, k % 4
                        w = min(512, S2 - c * 512)
                        dve.wait_ge(self.piece_ready, g * NP + (2 * NP + k + 1))
                        src = ps[:, 5 + k % 2, 0:w]
                        if self.masked:
                            dve.sem_inc(self.piece_seen, 1)
                            ins = nc.vector.tensor_tensor_reduce(self.junk[:, k % 2, 0:w], src, nat[:, t, c * 512:c * 512 + w], 1.0,
                                                                 MASKED, ALU.add, ALU.max, mx[p][:, t, c:c + 1])
                        else:
                            ins = nc.vector.tensor_reduce(mx[p][:, t, c:c + 1], src, AXX, ALU.max)
                        ins.then_inc(self.piece_taken, 1)
                    if k < NP - 1:
                        return
                    dve.wait_ge(self.piece_taken, g * NP + (2 + NP))
                    link = Chain(dve, self.vec, g * 4 + vec0)
                    negated_max_parts(nc, link, mx[p][:, :, :], self.m[:, :], self.rest[:, :], mparts[p], self.maxes_ready)
                    dve.wait_ge(self.maxes_ready, g + 1)
                first, rest = range(LEAD), range(LEAD, NP)
                maxima(g0, 0, first)
                with dve.Fori(i0, i1 - 1) as i:
                    for p in range(2):
                        maxima(i * 2 + p, p, rest)
                        maxima(i * 2 + (p + 1), 1 - p, first)
                maxima(end - 2, 0, rest)
                maxima(end - 1, 1, first)
                maxima(end - 1, 1, rest)

            @block.scalar
            def _(act):
                def rows(g, p):
                    act.wait_ge(self.rows_ready, g + 1)
                    nc.scalar.copy(Qb[p][96:99, :], ps[96:99, 4 + 3 * p, :]).then_inc(self.rows_copied, 1)

                def output(g, p, n):
                    act.wait_ge(self.p_used, g * NU + (NU + 4))
                    act.wait_ge(self.o_written[p], n * 64 + 64)
                    nc.scalar.copy(O[p][:, :], ps[:, 4 + 3 * p, :]).then_inc(self.o_copied, 1)

                def step(g, p, i, more):
                    for u in range(NU):
                        r, w = (P, 2 * SQ) if 2 * u + 2 <= NKB else (LASTK, SQ)
                        act.wait_ge(self.scores_ready, g * NU + (2 * NU + u + 1))
                        act.wait_ge(self.p_used, g * NU + (NU + u + 1))
                        nc.scalar.activation(Pt[0:r, (2 * p + u) % 4, 0:w], ps[0:r, 2 * (u % 2):2 * (u % 2) + 2, :].rearrange(
                            "p b c -> p (b c)")[:, 0:w], ACT.Exp, scale=self.scale).then_inc(self.exp_done, 1)
                        if u == 2:
                            output(g, 1 - p, i)
                    if more:
                        rows(g + 1, 1 - p)

                rows(g0, 0)
                with act.Fori(i0, i1 - 1) as i:
                    step(i * 2, 0, i, True)
                    step(i * 2 + 1, 1, i, True)
                step(end - 2, 0, i1 - 1, True)
                step(end - 1, 1, i1 - 1, False)
                if halves[-1] == 1:
                    output(2 * H, 1, H)


def sparse_tables(maskq, maskk, maskg):
    fills = []
    for n in range(4):
        work = [("mask", None, maskq[n > 0], 0, 512)]
        for s in range(2):
            t = 2 * n + s
            k0 = max(0, (t - 1) * P)
            w = (t + 1) * P - k0
            work.append(("qk", t, (lambda k0, w: lambda K: K[:, k0:k0 + w])(k0, w), s * 256 + 256 - w, w))
        fills.append((work, [(0, 512, 2, (2 * n, 0))]))
    globs = lambda K: K.rearrange("p (j c) -> p j c", c=64)[:, :, 0]
    work = [("mask", None, maskg[0], 0, T * 16)]
    work += [("qk", t, globs, 16 * t, 16) for t in range(T)]
    fills.append((work, [(0, T * 16, T, (0, 1))]))
    tiles = []
    for n in range(2):
        scores = [("mask", None, maskk, 0, 512), ("mask", None, maskk, 512, 512)]
        values = []
        for s in range(4):
            kb = 4 * n + s
            w = min(256, S - kb * P)
            scores.append(("qk", (lambda kb: lambda K: K[:, kb * P:(kb + 1) * P])(kb), kb * P, s * 256, w))
            values += [(s * 256 + P * j, P, kb, j, (kb + j) * P) for j in range(2) if (kb + j) < T]
        tiles.append({"scores": scores, "values": values, "rows": P, "width": S})
    tiles.append({"scores": [("mask", None, maskg[1][:, 0:512], 0, 512), ("mask", None, maskg[1][:, 512:S], 512, 512),
                             ("qk", globs, 0, 0, 512), ("qk", globs, 512, 512, 512)],
                  "values": [(0, 512, None, 2, 0), (512, 512, None, 2, 512)], "rows": 16, "width": S})
    return fills, tiles


def causal_tables(maskq, maskk):
    fills = []
    for parts in (((7, 0, 512),), ((7, 512, 512),), ((6, 0, 512),), ((6, 512, 384), (0, 0, 128)), ((5, 0, 512),),
                  ((5, 512, 256), (1, 0, 256)), ((4, 0, 512),), ((4, 512, 128), (2, 0, 384)), ((3, 0, 512),)):
        col, work, reds, masks = 0, [], [], []
        for t, k0, w in parts:
            work.append(("qk", t, (lambda k0, w: lambda K: K[:, k0:k0 + w])(k0, w), col, w))
            if k0 + w == (t + 1) * P:
                masks.append(("mask", None, maskq, col + w - P, P))
            reds.append((col, w, 1, (t, k0 // 512)))
            col += w
        fills.append((work + masks, reds))
    tiles = []
    for parts in (((0, 0, 1024),), ((1, 128, 896), (7, 896, 128)), ((2, 256, 768), (6, 768, 256)),
                  ((3, 384, 640), (5, 640, 384)), ((4, 512, 512),)):
        col, scores, values, masks = 0, [], [], []
        for kb, q0, w in parts:
            masks.append(("mask", None, maskk, col, P))
            done = 0
            while done < w:
                n = min(w - done, 512 - (col + done) % 512, 512 - (q0 + done) % 512)
                scores.append(("qk", (lambda kb: lambda K: K[:, kb * P:(kb + 1) * P])(kb), q0 + done, col + done, n))
                values.append((col + done, n, kb, kb % 4, q0 + done))
                done += n
            col += w
        tiles.append({"scores": scores + masks, "values": values, "rows": P, "width": col})
    return fills, tiles


def build(nc, a, out):
    ctx = ExitStack()
    with ctx:
        core = Core(nc, ctx)
        X, ps = core.X, core.ps
        start_block(core, a["x"], a["c_ident"])
        ln = LayerNorm(core, ctx)
        turner = Turner(core)
        comb = Combiner(core)
        splitter = Splitter(core)

        def dram(name, shape, dt):
            return nc.dram_tensor(name, shape, dt, kind="Internal").ap()

        def rows_of(scratch, r):
            return scratch.rearrange("h (d r) c -> (h d) r c", r=6)[:, r, :]

        def dst6(scratch, side, c0=0, c1=None):
            return [(rows_of(scratch, r)[:, c0:c1], pair[side]) for r, pair in enumerate(PAIRS)]

        Osum_shape = [P, 4, S]

        def combine(O_dram, W, bias_rows, cross, nparts, c):
            Osum = core.sb(c, "Osum", [P, nparts, S], F32)
            Ssum = core.sb(c, "Ssum", [P, nparts, S], F32)
            tmp = core.sb(c, "Ytmp", [P, S], F32)
            parts = []
            for j in range(nparts):
                if cross:
                    part = []
                    for half in range(2):
                        src = O_dram[3 + half * H:3 + (half + 1) * H, j]
                        part.append(((half * 512, half * 512 + 512), src[:, 0:HD, :],
                                     src[:, HD:HD + 1, :].broadcast_to((H, HD, 512))))
                else:
                    src = O_dram[:, j]
                    part = [((0, S), src[:, 0:HD, :], src[:, HD:HD + 1, :].broadcast_to((H, HD, S)))]
                parts.append(part)
            comb.block(Osum, Ssum, tmp, parts, W, bias_rows)

        O_self = dram("O_self", (H, 4, HD + 1, S), F32)
        O_cross = dram("O_cross", (3 + 2 * H, 4, HD + 1, 512), F32)
        Qs = dram("Qs", (H, 48, S), BF16)
        Ks = dram("Ks", (H, 48, S), BF16)
        Ks0 = dram("Ks0", (H, 48, S2), BF16)
        Ks1 = dram("Ks1", (H, 48, S2), BF16)
        key_bias = dram("key_bias", (1, S2), BF16)

        with ExitStack() as c:
            hT, xn = core.sb(c, "hT", [P, S], F32), core.sb(c, "xn", [P, T, D], F32)
            Wqkv, Wproj = core.sb(c, "Wqkv", [D, 3 * D], F32), core.sb(c, "Wproj", [D, D], F32)
            tables = core.sb(c, "tables", [P, 2688], BF16)
            mq = tables[:, 0:1024].rearrange("p (n c) -> p n c", n=2)
            mk, mgq, mgk = tables[:, 1024:1536], tables[:, 1536:1664], tables[:, 1664:2688]
            Vaug = core.sb(c, "Vaug", [P, H, T, HD + 1], F32)
            tables32 = core.sb(c, "tables32", [P, 2688], F32)
            Vglob = core.sb(c, "Vglob", [16, H, HD + 1], F32)
            ln.block(hT, xn, [(Wqkv[:, :], a["L0_attn_Wqkv"]), (Wproj[:, :], a["L0_attn_Wproj"]),
                              (tables32[:, 0:2688], a["c_sparse"])])
            narrow(core, tables[:, :], tables32[:, 0:2688])
            with ExitStack() as c2:
                sp3 = splitter.buffers(c2)
                sp3.block([(S, project(core, Wqkv[:, 0:D], hT), None, None, dst6(Qs, 0)),
                           (S, project(core, Wqkv[:, D:2 * D], hT), None, None, dst6(Ks, 1))])
            values_block(core, "v0", Vaug, [(P, hT[:, t * P:(t + 1) * P], Wqkv[:, 2 * D:]) for t in range(T)])
            glob_loaded = core.sem("glob_loaded")
            with nc.Block() as block:
                @block.sync
                def _(sp):
                    for j in range(16):
                        sp.dma_start(Vglob[j:j + 1, :, :],
                                     Vaug[64 * (j % 2):64 * (j % 2) + 1, :, j // 2, :]).then_inc(glob_loaded, 16)
                    sp.wait_ge(glob_loaded, 16 * 16)
            fills, tiles = sparse_tables([mq[:, 0, :], mq[:, 1, :]], mk, (mgq, mgk))
            with ExitStack() as c2, core.stage():
                att = SelfAttention(core, "a0_", 1, fills, tiles, 2)
                head = lambda scr: lambda g: scr[bass.ds(g, 1)].rearrange("a r c -> (a r) c")
                one = lambda scr: [((0, 48), (lambda g: scr[bass.ds(g, 1)].rearrange("a r (n c) -> (a r) n c", n=1)))]
                att.run(c2, {"q": one(Qs), "k": one(Ks)}, Vaug, Vglob, HD ** -0.5, O_self)
            with ExitStack() as c2:
                combine(O_self, Wproj[:, :], None, False, 3, c2)

        def cross_values(name, Vaug, ctxT, W, bias_rows):
            values_block(core, name, Vaug, [(min(P, S2 - t * P), ctxT[:, t * P:min(S2, (t + 1) * P)], W)
                                            for t in range(NKB)], bias_rows)

        def context_items(ctx_tok, ctxT_dst, dst):
            items = []
            for n in range(-(-S2 // S)):
                w = min(S, S2 - n * S)

                def matmuls(pe, A, B, n=n, w=w):
                    for t in range(-(-w // P)):
                        r = min(P, w - t * P)
                        last = nc.tensor.transpose(A[:, t * P:t * P + r], ctx_tok[0:r, n * T + t, :], core.ident[0:r, 0:r])
                    return last
                items.append((w, matmuls, None, None, dst6(dst, 1, n * S, n * S + w)))
            return items

        def load_context(ctx_tok):
            src = a["ctx_1024"]
            full = (NKB - 1) * P
            return [(ctx_tok[:, 0:NKB - 1, :], src[0, 0:full, :].rearrange("(t p) d -> p t d", p=P)),
                    (ctx_tok[0:LASTK, NKB - 1, :], src[0, full:S2, :])]

        def rows_load(c, name, src):
            t = core.sb(c, name, [P, src.shape[-1]], F32)
            return t, (t[:, :], src.partition_broadcast(P) if len(src.shape) == 1 else src)

        with ExitStack() as c:
            Wo0, Wo0T = core.sb(c, "Wo0", [D, D], F32), core.sb(c, "Wo0T", [D, D], F32)
            bo0, bo0_load = rows_load(c, "bo0", a["L0_xattn_b_out"])
            Vaug = core.sb(c, "Vaugx", [P, H, NKB, HD + 1], F32)
            with ExitStack() as c2:
                hT, xn = core.sb(c2, "hT", [P, S], F32), core.sb(c2, "xn", [P, T, D], F32)
                ctx_tok = core.sb(c2, "ctx_tok", [P, NKB, D], F32)
                mrow = core.sb(c2, "mrow", [4, S2 // 4], I32)
                brow = core.sb(c2, "brow", [4, S2 // 4], BF16)
                ln.block(hT, xn, load_context(ctx_tok) + [
                    (Wo0[:, :], a["L0_xattn_W_out"]), bo0_load,
                    (mrow[:, :], a["mask_Bx1x1xS2_if1"].rearrange("a b c (p n) -> (a b c p) n", p=4))])
                turner.block([(Wo0[:, :], Wo0T[:, :])])
                sp3 = splitter.buffers(c2)
                items = context_items(ctx_tok, None, Ks0)
                items.append((S, (lambda pe, A, B: [nc.tensor.matmul(A[:, k * 512:(k + 1) * 512], core.ident[:, :],
                                                                    hT[:, k * 512:(k + 1) * 512], start=True, stop=True)
                                                    for k in range(2)][-1]), None, None, dst6(Qs, 0)))
                sp3.block(items)
                vx_ones, vx_done, kb_ready, kb_stored = (core.sem("vx_ones"), core.sem("vx_done"),
                                                         core.sem("kb_ready"), core.sem("kb_stored"))
                with nc.Block() as block:
                    @block.gpsimd
                    def _(pool):
                        nc.gpsimd.memset(Vaug[:, :, NKB - 1, :], 0.0).then_inc(vx_ones, 1)
                        pool.wait_ge(vx_ones, 1)
                        for h in range(H):
                            nc.gpsimd.memset(Vaug[:, h, :, HD:HD + 1], 1.0).then_inc(vx_ones, 1)
                        pool.wait_ge(vx_ones, 1 + H)

                    @block.vector
                    def _(dve):
                        dve.wait_ge(vx_ones, 1 + H)
                        for h in range(H):
                            nc.vector.tensor_copy(Vaug[:, h, 0:NKB - 1, 0:HD],
                                                  ctx_tok[:, 0:NKB - 1, h * HD:(h + 1) * HD]).then_inc(vx_done, 1)
                        nc.vector.tensor_copy(Vaug[0:LASTK, :, NKB - 1, 0:HD], ctx_tok[0:LASTK, NKB - 1, :].rearrange(
                            "p (h d) -> p h d", h=H)).then_inc(vx_done, 1)
                        nc.vector.tensor_scalar(brow[:, :], mrow[:, :], 0.0, MASKED, ALU.is_equal, ALU.mult).then_inc(kb_ready, 1)
                        dve.wait_ge(vx_done, H + 1)

                    @block.sync
                    def _(sp):
                        sp.wait_ge(kb_ready, 1)
                        sp.dma_start(key_bias.rearrange("a (p n) -> (a p) n", p=4), brow[:, :]).then_inc(kb_stored, 16)
                        sp.wait_ge(kb_stored, 16)
            with ExitStack() as c2, core.stage():
                xa = CrossAttention(core, c2, "x0_", float(D) ** -0.5, False)
                xa.clear_block(key_bias)
                xa.block((0, 1), Qs, Ks0, Vaug, O_cross)
            with ExitStack() as c2:
                combine(O_cross, Wo0T[:, :], bo0[:, :], True, 4, c2)

        moe_l0(core, ln, turner, a)
        mla(core, ln, comb, splitter, combine, a, O_self, dram)

        with ExitStack() as c:
            WoT = core.sb(c, "Wo1T", [D, D], F32)
            bo1, bo1_load = rows_load(c, "bo1", a["L1_xattn_bo"])
            Vaug = core.sb(c, "Vaugy", [P, H, NKB, HD + 1], F32)
            with ExitStack() as c2:
                hT, xn = core.sb(c2, "hT", [P, S], F32), core.sb(c2, "xn", [P, T, D], F32)
                ctxT = core.sb(c2, "ctxT", [P, NKB * P], F32)
                W = core.sb(c2, "W4", [D, 4, D], F32)
                WT = core.sb(c2, "W4T", [D, 3, D], F32)
                bqk = core.sb(c2, "bqk", [2, D], F32)
                bqkT = core.sb(c2, "bqkT", [D, 2], F32)
                bv, bv_load = rows_load(c2, "bv1", a["L1_xattn_bv"])
                with ExitStack() as c3:
                    ctx_tok = core.sb(c3, "ctx_tok", [P, NKB, D], F32)
                    ln.block(hT, xn, load_context(ctx_tok) + [
                        (W[:, k, :], a[f"L1_xattn_W{n}"]) for k, n in enumerate("qkvo")] + [
                        bo1_load, bv_load, (bqk[0:1, :], a["L1_xattn_bq"].rearrange("(a d) -> a d", a=1)),
                        (bqk[1:2, :], a["L1_xattn_bk"].rearrange("(a d) -> a d", a=1))])
                    turner.block([(W[:, k, :], WT[:, k, :]) for k in range(3)] + [(W[:, 3, :], WoT[:, :]),
                                 (bqk[:, :], bqkT[:, :])] +
                                 [(ctx_tok[0:min(P, S2 - t * P), t, :], ctxT[:, t * P:min(S2, (t + 1) * P)])
                                  for t in range(NKB)])
                with ExitStack() as c3:
                    sp3 = splitter.buffers(c3)
                    items = [(min(S, S2 - n * S), project(core, WT[:, 1, :], ctxT, min(S, S2 - n * S), n * S), bqkT[:, 1:2], None,
                              dst6(Ks1, 1, n * S, min(S2, (n + 1) * S))) for n in range(-(-S2 // S))]
                    items.append((S, project(core, WT[:, 0, :], hT), bqkT[:, 0:1], None, dst6(Qs, 0)))
                    sp3.block(items)
                    cross_values("vy", Vaug, ctxT, WT[:, 2, :], bv[:, :])
            with ExitStack() as c2, core.stage():
                xa = CrossAttention(core, c2, "x1_", float(HD) ** -0.5, True)
                nat = core.sb(c2, "nat", [P, 4, S2], BF16)
                maskT = core.sb(c2, "maskT", [P, NKB, 512], BF16)
                xa.clear_block(None)
                mask_loaded = [core.sem(f"mask_loaded{p}") for p in range(2)]
                mask_made, mask_turned, mask_taken = core.sem("mask_made"), core.sem("mask_turned"), core.sem("mask_taken")
                for half in range(2):
                    mask_block(core, xa, half, a["mask_Bx1xSxS2_ik1"], nat, maskT, mask_loaded, mask_made, mask_turned, mask_taken)
                    xa.block((half,), Qs, Ks1, Vaug, O_cross, nat, maskT)
            with ExitStack() as c2:
                combine(O_cross, WoT[:, :], bo1[:, :], True, 4, c2)

        encoder(core, ln, turner, a, out)


def mask_block(core, xa, half, mask, nat, maskT, loaded, made, turned, taken):
    nc, ps = core.nc, core.ps
    NC = 4
    W = S2 // NC
    stage = xa.Pt[:, :, :].rearrange("p a b -> p (a b)").bitcast(I32)
    n0 = half * 4 * NC
    with nc.Block() as block:
        @block.sync
        def _(sp):
            for n in range(4 * NC):
                t, c = n // NC, n % NC
                if n >= 2:
                    sp.wait_ge(made, n0 + n - 1)
                q = half * 512 + t * P
                sp.dma_start(stage[:, (n % 2) * 2048:(n % 2) * 2048 + W], mask[0, 0, q:q + P, c * W:(c + 1) * W])\
                  .then_inc(loaded[n % 2], 16)

        @block.vector
        def _(dve):
            if half == 0:
                nc.vector.memset(maskT[:, NKB - 1, :], 0.0).then_inc(taken, 1)
            for n in range(4 * NC):
                t, c = n // NC, n % NC
                dve.wait_ge(loaded[n % 2], 16 * ((n0 + n) // 2 + 1))
                nc.vector.tensor_scalar(nat[:, t, c * W:(c + 1) * W], stage[:, (n % 2) * 2048:(n % 2) * 2048 + W], 1.0, MASKED,
                                        ALU.is_equal, ALU.mult).then_inc(made, 1)
            dve.wait_ge(made, n0 + 4 * NC)

        @block.tensor
        def _(pe):
            pe.wait_ge(made, n0 + 4 * NC)
            for kb in range(NKB):
                r = min(P, S2 - kb * P)
                if kb >= 2:
                    pe.wait_ge(taken, 1 + half * NKB + kb - 1)
                dst = ps[:, kb % 2, 0:256].bitcast(BF16)
                for t in range(4):
                    last = nc.tensor.transpose(dst[0:r, t * P:(t + 1) * P], nat[:, t, kb * P:kb * P + r], core.identb[:, :])
                last.then_inc(turned, 1)

        @block.scalar
        def _(act):
            act.wait_ge(taken, 1)
            for kb in range(NKB):
                r = min(P, S2 - kb * P)
                act.wait_ge(turned, half * NKB + kb + 1)
                nc.scalar.copy(maskT[0:r, kb, :], ps[0:r, kb % 2, 0:256].bitcast(BF16)).then_inc(taken, 1)
            act.wait_ge(taken, 1 + (half + 1) * NKB)


def first_max_onehot(nc, link, L, m, eidx, cand, idx, onehot, want_m=True):
    if want_m:
        link(nc.vector.tensor_reduce(m, L, AXX, ALU.max))
    wide = lambda x: x.unsqueeze(2).broadcast_to((P, T, E))
    link(nc.vector.tensor_tensor(cand, L, wide(m), ALU.is_equal))
    link(nc.vector.tensor_tensor(cand, cand, eidx, ALU.mult))
    link(nc.vector.tensor_reduce(idx, cand, AXX, ALU.min))
    link(nc.vector.tensor_tensor(onehot, eidx, wide(idx), ALU.is_equal))


def moe_l0(core, ln, turner, a):
    nc, ps, X = core.nc, core.ps, core.X
    F = 256
    FC = F // P
    with ExitStack() as c:
        sb = lambda n, s, d=F32: core.sb(c, n, s, d)
        hT, xn = sb("hT", [P, S]), sb("xn", [P, T, D])
        Wg, Wu = sb("Wg", [P, E * FC, D]), sb("Wu", [P, E * FC, D])
        Wd = sb("Wd", [P, E, F])
        WgT, WuT, WdT = sb("WgT", [P, E * FC, P]), sb("WuT", [P, E * FC, P]), sb("WdT", [P, E * FC, D])
        Rw, RwT = sb("Rw", [E, D]), sb("RwT", [D, E])
        eidx = sb("eidx", [P, T, E])
        ln.block(hT, xn, [(Wg[:, :, :], a["L0_ffn_w_gate"].rearrange("e (c p) h -> p (e c) h", p=P)),
                          (Wu[:, :, :], a["L0_ffn_w_up"].rearrange("e (c p) h -> p (e c) h", p=P)),
                          (Wd[:, :, :], a["L0_ffn_w_down"].rearrange("e h f -> h e f")),
                          (Rw[:, :], a["L0_ffn_router_w"]), (eidx[:, :, :], a["c_expert"])])
        turner.block([(Rw[:, :], RwT[:, :])] +
                     [(Wg[:, n, :], WgT[:, n, :]) for n in range(E * FC)] +
                     [(Wu[:, n, :], WuT[:, n, :]) for n in range(E * FC)] +
                     [(Wd[:, n // FC, (n % FC) * P:(n % FC + 1) * P], WdT[:, n, :]) for n in range(E * FC)])
        L, L2, cand, one1, one2 = (sb("r" + k, [P, T, E]) for k in ("L", "L2", "cand", "one1", "one2"))
        fac, keep1, e1, dense, absL = (sb("r" + k, [P, T, E]) for k in ("fac", "keep", "e1", "dense", "abs"))
        m1, m2, idx, tot = (sb("r" + k, [P, T]) for k in ("m1", "m2", "idx", "tot"))
        logits, vec, diff_ready, exp_ready, dense_ready = (core.sem("r_" + k) for k in
                                                          ("logits", "vec", "diff_ready", "exp_ready", "dense_ready"))
        wide = lambda x: x[:, :].unsqueeze(2).broadcast_to((P, T, E))
        with nc.Block() as block:
            @block.tensor
            def _(pe):
                for t in range(T):
                    last = nc.tensor.matmul(ps[:, 0, t * E:(t + 1) * E], hT[:, t * P:(t + 1) * P], RwT[:, :], start=True, stop=True)
                last.then_inc(logits, 1)

            @block.vector
            def _(dve):
                link = Chain(dve, vec)
                dve.wait_ge(logits, 1)
                link(nc.vector.tensor_copy(L[:, :, :], ps[:, 0, 0:T * E].rearrange("p (t e) -> p t e", t=T)))
                link(nc.vector.tensor_scalar(absL[:, :, :], L[:, :, :], -1.0, None, ALU.mult))
                link(nc.vector.tensor_tensor(absL[:, :, :], absL[:, :, :], L[:, :, :], ALU.max))
                for k, (src, m, one) in enumerate(((L, m1, one1), (L2, m2, one2))):
                    if k == 1:
                        link(nc.vector.scalar_tensor_tensor(L2[:, :, :], one1[:, :, :], MASKED, L[:, :, :], ALU.mult, ALU.add))
                    first_max_onehot(nc, link, src[:, :, :], m[:, :], eidx[:, :, :], cand[:, :, :], idx[:, :], one[:, :, :])
                    link(nc.vector.tensor_tensor(fac[:, :, :], absL[:, :, :], wide(m), ALU.max))
                    link(nc.vector.tensor_tensor(cand[:, :, :], wide(m), L[:, :, :], ALU.subtract))
                    link(nc.vector.scalar_tensor_tensor(keep1[:, :, :], fac[:, :, :], 0.02, cand[:, :, :], ALU.mult, ALU.is_ge))
                    nc.vector.tensor_tensor(cand[:, :, :], src[:, :, :], wide(m), ALU.subtract).then_inc(diff_ready, 1)
                    dve.wait_ge(exp_ready, k + 1)
                    link(nc.vector.tensor_tensor(e1[:, :, :], e1[:, :, :], keep1[:, :, :], ALU.mult))
                    link(nc.vector.tensor_reduce(tot[:, :], e1[:, :, :], AXX, ALU.add))
                    link(nc.vector.reciprocal(tot[:, :], tot[:, :]))
                    dst = dense if k == 0 else fac
                    link(nc.vector.tensor_tensor(dst[:, :, :], one[:, :, :], wide(tot), ALU.mult))
                nc.vector.tensor_tensor(dense[:, :, :], dense[:, :, :], fac[:, :, :], ALU.add).then_inc(dense_ready, 1)
                dve.wait_ge(dense_ready, 1)

            @block.scalar
            def _(act):
                for k in range(2):
                    act.wait_ge(diff_ready, k + 1)
                    nc.scalar.activation(e1[:, :, :], cand[:, :, :], ACT.Exp).then_inc(exp_ready, 1)

        gate, hid = sb("gate", [P, 2, 512]), sb("hid", [P, 2, FC, S])
        up_ready, gate_done, hid_ready, down_ready, hid_used, added = (core.sem("f0_" + k) for k in (
            "up_ready", "gate_done", "hid_ready", "down_ready", "hid_used", "added"))
        with nc.Block() as block:
            @block.tensor
            def _(pe):
                def down(e):
                    pe.wait_ge(hid_ready, 4 * (e + 1))
                    for t in range(T):
                        n = e * T + t
                        if n >= 4:
                            pe.wait_ge(added, n - 3)
                        for k in range(FC):
                            last = nc.tensor.matmul(ps[:, 4 + n % 4, 0:D], hid[:, e % 2, k, t * P:(t + 1) * P],
                                                    WdT[:, e * FC + k, :], start=(k == 0), stop=(k == FC - 1))
                        last.then_inc(down_ready, 1)
                    
                for e in range(E):
                    for k in range(FC):
                        for b in range(2):
                            n = (e * FC + k) * 2 + b
                            if n >= 2:
                                pe.wait_ge(hid_ready, n - 1)
                            rhs = hT[:, b * 512:(b + 1) * 512]
                            nc.tensor.matmul(ps[:, 2 * (n % 2), :], WgT[:, e * FC + k, :], rhs, start=True, stop=True)
                            nc.tensor.matmul(ps[:, 2 * (n % 2) + 1, :], WuT[:, e * FC + k, :], rhs, start=True,
                                             stop=True).then_inc(up_ready, 1)
                    if e:
                        down(e - 1)
                down(E - 1)

            @block.scalar
            def _(act):
                for n in range(E * FC * 2):
                    act.wait_ge(up_ready, n + 1)
                    if n >= 2:
                        act.wait_ge(hid_ready, n - 1)
                    nc.scalar.activation(gate[:, n % 2, :], ps[:, 2 * (n % 2), :], ACT.Silu).then_inc(gate_done, 1)

            @block.vector
            def _(dve):
                def add(e):
                    for t in range(T):
                        n = e * T + t
                        dve.wait_ge(down_ready, n + 1)
                        if e:
                            dve.wait_ge(added, n - T + 1)
                        nc.vector.scalar_tensor_tensor(X[:, t, :], ps[:, 4 + n % 4, 0:D], dense[:, t, e:e + 1], X[:, t, :],
                                                       ALU.mult, ALU.add).then_inc(added, 1)
                for e in range(E):
                    for k in range(FC):
                        for b in range(2):
                            n = (e * FC + k) * 2 + b
                            dve.wait_ge(gate_done, n + 1)
                            if e >= 2:
                                dve.wait_ge(down_ready, T * (e - 1))
                            nc.vector.tensor_tensor(hid[:, e % 2, k, b * 512:(b + 1) * 512], ps[:, 2 * (n % 2) + 1, :],
                                                    gate[:, n % 2, :], ALU.mult).then_inc(hid_ready, 1)
                    if e:
                        add(e - 1)
                add(E - 1)
                dve.wait_ge(added, E * T)


def mla(core, ln, comb, splitter, combine, a, O_self, dram):
    nc, ps = core.nc, core.ps
    KV, QR, RD = 32, 64, 32
    Qc, Kc = dram("Qc", (H, 2, HD * 3, S), BF16), dram("Kc", (H, 2, HD * 3, S), BF16)
    Qr, Kr = dram("Qr", (H, 2, RD * 3, S), BF16), dram("Kr", (H, 2, RD * 3, S), BF16)
    with ExitStack() as c:
        sb = lambda n, s, d=F32: core.sb(c, n, s, d)
        Wo = sb("Wo_m", [D, D])
        tables, tables32 = sb("tables", [P, 2 * P], BF16), sb("tables32", [P, 2 * P])
        mq, mk = tables[:, 0:P], tables[:, P:2 * P]
        Vaug = sb("Vaugm", [P, H, T, HD + 1])
        with ExitStack() as c2:
            sb2 = lambda n, s, d=F32: core.sb(c2, n, s, d)
            hT, xn = sb2("hT", [P, S]), sb2("xn", [P, T, D])
            Wkv, Wq = sb2("Wkv", [D, KV]), sb2("Wq_m", [D, QR])
            Wkd, Wvd, Wqd = sb2("Wkd", [KV, D]), sb2("Wvd", [KV, D]), sb2("Wqd", [QR, D])
            Wkr, Wqr = sb2("Wkr", [D, H * RD]), sb2("Wqr", [QR, H * RD])
            Wkt, Wqt = sb2("Wkt", [D, H * RD]), sb2("Wqt", [QR, H * RD])
            cos, sin = sb2("cos", [P, S]), sb2("sin", [P, S])
            gkv = sb2("gkv", [P, KV])
            kvc, sq = sb2("kvc", [P, T, KV]), sb2("sq", [P, T, KV])
            ms, rs = sb2("ms", [P, T]), sb2("rs", [P, T])
            kvT, qcT = sb2("kvT", [KV, S]), sb2("qcT", [QR, S])
            ln.block(hT, xn, [(Wkv[:, :], a["L1_attn_W_kv"]), (Wq[:, :], a["L1_attn_W_q"]), (Wkd[:, :], a["L1_attn_W_kdec"]),
                              (Wvd[:, :], a["L1_attn_W_vdec"]), (Wqd[:, :], a["L1_attn_W_qdec"]),
                              (Wkr[:, :], a["L1_attn_W_krope"]), (Wqr[:, :], a["L1_attn_W_qrope"]),
                              (Wo[:, :], a["L1_attn_W_o"]), (cos[:, :], a["c_cos"]), (sin[:, :], a["c_sin"]),
                              (gkv[:, :], a["L1_attn_g_kv"].partition_broadcast(P)),
                              (tables32[:, :], a["c_causal"])])
            narrow(core, tables[:, :], tables32[:, :])
            kv_ready, q_ready, vec, ms_ready, rt_ready, kvn_ready, turned, took = (core.sem("m_" + k) for k in (
                "kv_ready", "q_ready", "vec", "ms_ready", "rt_ready", "kvn_ready", "turned", "took"))
            with nc.Block() as block:
                @block.tensor
                def _(pe):
                    for t in range(T):
                        last = nc.tensor.matmul(ps[:, 0, t * KV:(t + 1) * KV], hT[:, t * P:(t + 1) * P], Wkv[:, :], start=True, stop=True)
                    last.then_inc(kv_ready, 1)
                    for b in range(2):
                        last = nc.tensor.matmul(ps[0:QR, 1 + b, :], Wq[:, :], hT[:, b * 512:(b + 1) * 512], start=True, stop=True)
                    last.then_inc(q_ready, 1)
                    pe.wait_ge(kvn_ready, 1)
                    for t in range(T):
                        last = nc.tensor.transpose(ps[0:KV, 3 + t // 4, (t % 4) * P:(t % 4 + 1) * P], kvc[:, t, :], core.ident[:, :])
                    last.then_inc(turned, 1)

                @block.vector
                def _(dve):
                    link = Chain(dve, vec)
                    for w, wt, r in ((Wkr, Wkt, D), (Wqr, Wqt, QR)):
                        v = w[0:r, :].rearrange("p (h a d) -> p h a d", h=H, a=2)
                        vt = wt[0:r, :].rearrange("p (h a d) -> p h a d", h=H, a=2)
                        link(nc.vector.tensor_scalar(vt[:, :, 0, :], v[:, :, 1, :], -1.0, None, ALU.mult))
                        link(nc.vector.tensor_copy(vt[:, :, 1, :], v[:, :, 0, :]))
                    dve.wait_ge(kv_ready, 1)
                    link(nc.vector.tensor_copy(kvc[:, :, :], ps[:, 0, 0:T * KV].rearrange("p (t k) -> p t k", t=T)))
                    link(nc.vector.tensor_tensor(sq[:, :, :], kvc[:, :, :], kvc[:, :, :], ALU.mult))
                    link(nc.vector.tensor_reduce(ms[:, :], sq[:, :, :], AXX, ALU.add))
                    nc.vector.tensor_scalar(ms[:, :], ms[:, :], 1.0 / KV, 1e-6, ALU.mult, ALU.add).then_inc(ms_ready, 1)
                    dve.wait_ge(rt_ready, 1)
                    link(nc.vector.reciprocal(rs[:, :], ms[:, :]))
                    link(nc.vector.tensor_tensor(kvc[:, :, :], kvc[:, :, :], rs[:, :].unsqueeze(2).broadcast_to((P, T, KV)), ALU.mult))
                    nc.vector.tensor_tensor(kvc[:, :, :], kvc[:, :, :], gkv[:, :].unsqueeze(1).broadcast_to((P, T, KV)),
                                            ALU.mult).then_inc(kvn_ready, 1)
                    dve.wait_ge(kvn_ready, 1)

                @block.scalar
                def _(act):
                    act.wait_ge(q_ready, 1)
                    nc.scalar.copy(qcT[:, :], ps[0:QR, 1:3, :].rearrange("p b c -> p (b c)")).then_inc(took, 1)
                    act.wait_ge(ms_ready, 1)
                    nc.scalar.activation(ms[:, :], ms[:, :], ACT.Sqrt).then_inc(rt_ready, 1)
                    act.wait_ge(turned, 1)
                    nc.scalar.copy(kvT[:, :], ps[0:KV, 3:5, :].rearrange("p b c -> p (b c)")).then_inc(took, 1)
                    act.wait_ge(took, 2)

            def dsts(scr, side, g0, n):
                out = []
                for ch in range(2):
                    for r in range(3):
                        v = scr[g0:g0 + n, ch].rearrange("h (d r) c -> h d r c", r=3)[:, :, r, :]
                        out.append((v, CHUNK_PAIRS[ch][r][side]))
                return out

            sp3 = splitter.buffers(c2)
            items = [(S, project(core, Wqd[:, :], qcT), None, None, dsts(Qc, 0, 0, H)),
                     (S, project(core, Wkd[:, :], kvT), None, None, dsts(Kc, 1, 0, H))]
            for n in range(4):
                cols = slice(n * P, (n + 1) * P)
                items.append((S, project_two(core, Wqr[:, cols], Wqt[:, cols], qcT), None, (cos[:, :], sin[:, :]), dsts(Qr, 0, 4 * n, 4)))
                items.append((S, project_two(core, Wkr[:, cols], Wkt[:, cols], hT), None, (cos[:, :], sin[:, :]), dsts(Kr, 1, 4 * n, 4)))
            sp3.block(items)
            values_block(core, "vm", Vaug, [(P, kvT[:, t * P:(t + 1) * P], Wvd[:, :]) for t in range(T)])
        with ExitStack() as c2, core.stage():
            fills, tiles = causal_tables(mq, mk)
            att = SelfAttention(core, "a1_", 2, fills, tiles, 2)

            def srcs(content, rope):
                rope_rows = lambda lo, hi: lambda g: rope[bass.ds(g, 1), :, lo:hi, :].rearrange("a n r c -> (a r) n c")
                return [((0, 96), rope_rows(0, 96)),
                        ((99, 123), lambda g: content[bass.ds(g, 1)].rearrange("a n r c -> (a r) n c"))]
            att.run(c2, {"q": srcs(Qc, Qr), "k": srcs(Kc, Kr)}, Vaug, None, float(HD + RD) ** -0.5, O_self)
        with ExitStack() as c2:
            combine(O_self, Wo[:, :], None, False, 4, c2)


def encoder(core, ln, turner, a, out):
    nc, ps, X = core.nc, core.ps, core.X
    DF = 512
    C = DF // P
    with ExitStack() as c:
        sb = lambda n, s, d=F32: core.sb(c, n, s, d)
        hT, xn = sb("hT", [P, S]), sb("xn", [P, T, D])
        W1, W2 = sb("W1", [P, E, DF]), sb("W2", [P, E * C, D])
        b1, b1T = sb("b1", [E * C, P]), sb("b1T", [P, E * C])
        b2 = sb("b2", [P, E * D])
        Wv, Wo, WvT, WoT = sb("Wv_e", [D, D]), sb("Wo_e", [D, D]), sb("WvT_e", [D, D]), sb("WoT_e", [D, D])
        bv, bvT = sb("bv_e", [1, D]), sb("bvT_e", [D, 1])
        Wg, WgT = sb("Wg_e", [E, D]), sb("WgT_e", [D, E])
        e0 = sb("e0", [P, P])
        rows = {k: sb("row_" + k, [P, D]) for k in ("bo", "g1", "be1", "g2", "be2")}
        eidx = sb("eidx", [P, T, E])
        b2_zero, b2_loaded = core.sem("b2_zero"), core.sem("b2_loaded")
        ln.block(hT, xn, [(W1[:, :, :], a["L1_ffn_W1"].rearrange("e d f -> d e f")),
                          (W2[:, :, :], a["L1_ffn_W2"].rearrange("e (c p) d -> p (e c) d", p=P)),
                          (b1[:, :], a["L1_ffn_b1"].rearrange("e (c p) -> (e c) p", p=P)),
                          (Wv[:, :], a["L1_ffn_Wqkv"][2 * D:3 * D, :]), (Wo[:, :], a["L1_ffn_Wo"]),
                          (bv[:, :], a["L1_ffn_bqkv"][2 * D:3 * D].rearrange("(a d) -> a d", a=1)),
                          (Wg[:, :], a["L1_ffn_Wg"]), (eidx[:, :, :], a["c_expert"])] +
                 [(t[:, :], a["L1_ffn_" + k].partition_broadcast(P)) for k, t in rows.items()])
        with nc.Block() as block:
            @block.gpsimd
            def _(pool):
                nc.gpsimd.memset(b2[:, :], 0.0).then_inc(b2_zero, 1)
                nc.gpsimd.memset(e0[:, :], 0.0).then_inc(b2_zero, 1)
                pool.wait_ge(b2_zero, 2)
                nc.gpsimd.memset(e0[0:1, :], 1.0).then_inc(b2_zero, 1)
                pool.wait_ge(b2_zero, 3)

            @block.sync
            def _(sp):
                sp.wait_ge(b2_zero, 3)
                sp.dma_start(b2[0:1, :], a["L1_ffn_b2"].rearrange("(a e) d -> a (e d)", a=1)).then_inc(b2_loaded, 16)
                sp.wait_ge(b2_loaded, 16)
        turner.block([(b1[:, :], b1T[:, :]), (Wv[:, :], WvT[:, :]), (Wo[:, :], WoT[:, :]), (bv[:, :], bvT[:, :]),
                      (Wg[:, :], WgT[:, :])])

        vT, y, L, cand, one = sb("vT_e", [P, S]), sb("y", [P, T, D]), sb("gL", [P, T, E]), sb("gcand", [P, T, E]), sb("gone", [P, T, E])
        m, idx, yT = sb("gm", [P, T]), sb("gidx", [P, T]), sb("yT", [P, S])
        v_ready, v_taken, o_ready, vec, y_ready, y_turned, y_taken, logits = (core.sem("e_" + k) for k in (
            "v_ready", "v_taken", "o_ready", "vec", "y_ready", "y_turned", "y_taken", "logits"))
        call = ln.calls
        ln.calls += 1
        with nc.Block() as block:
            @block.tensor
            def _(pe):
                for b in range(2):
                    nc.tensor.matmul(ps[:, b, :], WvT[:, :], hT[:, b * 512:(b + 1) * 512], start=True, stop=True).then_inc(v_ready, 1)
                pe.wait_ge(v_taken, 2)
                for t in range(T):
                    nc.tensor.matmul(ps[:, 2 + t // 2, (t % 2) * D:(t % 2 + 1) * D], vT[:, t * P:(t + 1) * P], WoT[:, :],
                                     start=True, stop=True).then_inc(o_ready, 1)
                pe.wait_ge(y_ready, 1)
                for t in range(T):
                    nc.tensor.transpose(ps[:, 6 + t // 4, (t % 4) * P:(t % 4 + 1) * P], y[:, t, :], core.ident[:, :]).then_inc(y_turned, 1)
                pe.wait_ge(y_taken, 2)
                for t in range(T):
                    last = nc.tensor.matmul(ps[:, 0, t * E:(t + 1) * E], yT[:, t * P:(t + 1) * P], WgT[:, :], start=True, stop=True)
                last.then_inc(logits, 1)

            @block.scalar
            def _(act):
                for b in range(2):
                    act.wait_ge(v_ready, b + 1)
                    nc.scalar.activation(vT[:, b * 512:(b + 1) * 512], ps[:, b, :], ACT.Identity, bias=bvT[:, 0:1]).then_inc(v_taken, 1)
                ln.root(act, call)
                for b in range(2):
                    act.wait_ge(y_turned, 4 * b + 4)
                    nc.scalar.copy(yT[:, b * 512:(b + 1) * 512], ps[:, 6 + b, :]).then_inc(y_taken, 1)

            @block.vector
            def _(dve):
                link = Chain(dve, vec)
                wide = lambda r: r[:, :].unsqueeze(1).broadcast_to((P, T, D))
                link(nc.vector.tensor_tensor(xn[:, :, :], xn[:, :, :], wide(rows["bo"]), ALU.add))
                dve.wait_ge(o_ready, T)
                for b in range(4):
                    link(nc.vector.tensor_tensor(xn[:, 2 * b:2 * b + 2, :], xn[:, 2 * b:2 * b + 2, :],
                                                 ps[:, 2 + b, 0:2 * D].rearrange("p (t d) -> p t d", t=2), ALU.add))
                lk = Chain(dve, ln.dve_done, ln.chain_n)
                ln.normalise(dve, lk, xn, y, call)
                ln.chain_n = lk.n
                link(nc.vector.tensor_tensor(y[:, :, :], y[:, :, :], wide(rows["g1"]), ALU.mult))
                nc.vector.tensor_tensor(y[:, :, :], y[:, :, :], wide(rows["be1"]), ALU.add).then_inc(y_ready, 1)
                dve.wait_ge(y_ready, 1)
                dve.wait_ge(logits, 1)
                link(nc.vector.tensor_copy(L[:, :, :], ps[:, 0, 0:T * E].rearrange("p (t e) -> p t e", t=T)))
                first_max_onehot(nc, link, L[:, :, :], m[:, :], eidx[:, :, :], cand[:, :, :], idx[:, :], one[:, :, :])

        hid = sb("hid_e", [P, 2, C, S])
        h_ready, h_done, d_ready, added = (core.sem("e2_" + k) for k in ("h_ready", "h_done", "d_ready", "added"))
        call2 = ln.calls
        ln.calls += 1
        z = xn
        stored = core.sem("stored")
        final = core.sem("final")
        with nc.Block() as block:
            @block.tensor
            def _(pe):
                def down(e):
                    pe.wait_ge(h_done, 2 * C * (e + 1))
                    for t in range(T):
                        n = e * T + t
                        if n >= 4:
                            pe.wait_ge(added, n - 3)
                        dst = ps[:, 4 + n % 4, 0:D]
                        nc.tensor.matmul(dst, e0[:, :], b2[:, e * D:(e + 1) * D], start=True, stop=False)
                        for k in range(C):
                            last = nc.tensor.matmul(dst, hid[:, e % 2, k, t * P:(t + 1) * P], W2[:, e * C + k, :], start=False,
                                                    stop=(k == C - 1))
                        last.then_inc(d_ready, 1)
                for e in range(E):
                    for k in range(C):
                        for b in range(2):
                            n = (e * C + k) * 2 + b
                            if n >= 4:
                                pe.wait_ge(h_done, n - 3)
                            nc.tensor.matmul(ps[:, n % 4, :], W1[:, e, k * P:(k + 1) * P], yT[:, b * 512:(b + 1) * 512],
                                             start=True, stop=True).then_inc(h_ready, 1)
                    if e:
                        down(e - 1)
                down(E - 1)

            @block.scalar
            def _(act):
                for e in range(E):
                    if e >= 2:
                        act.wait_ge(d_ready, T * (e - 1))
                    for k in range(C):
                        for b in range(2):
                            n = (e * C + k) * 2 + b
                            act.wait_ge(h_ready, n + 1)
                            nc.scalar.activation(hid[:, e % 2, k, b * 512:(b + 1) * 512], ps[:, n % 4, :], ACT.Relu,
                                                 bias=b1T[:, e * C + k:e * C + k + 1]).then_inc(h_done, 1)
                ln.root(act, call2)

            @block.vector
            def _(dve):
                for n in range(E * T):
                    e, t = n // T, n % T
                    dve.wait_ge(d_ready, n + 1)
                    if e:
                        dve.wait_ge(added, n - T + 1)
                    nc.vector.scalar_tensor_tensor(y[:, t, :], ps[:, 4 + n % 4, 0:D], one[:, t, e:e + 1], y[:, t, :],
                                                   ALU.mult, ALU.add).then_inc(added, 1)
                dve.wait_ge(added, E * T)
                lk = Chain(dve, ln.dve_done, ln.chain_n)
                ln.normalise(dve, lk, y, z, call2)
                wide = lambda r: r[:, :].unsqueeze(1).broadcast_to((P, T, D))
                lk(nc.vector.tensor_tensor(z[:, :, :], z[:, :, :], wide(rows["g2"]), ALU.mult))
                lk(nc.vector.tensor_tensor(z[:, :, :], z[:, :, :], wide(rows["be2"]), ALU.add))
                nc.vector.tensor_tensor(z[:, :, :], z[:, :, :], X[:, :, :], ALU.add).then_inc(final, 1)

            @block.sync
            def _(sp):
                sp.wait_ge(final, 1)
                sp.dma_start(out.rearrange("a (t p) d -> p (a t) d", p=P), z[:, :, :]).then_inc(stored, 16)
                sp.wait_ge(stored, 16)


_INS = ["x", "ctx_1024", "mask_Bx1x1xS2_if1", "mask_Bx1xSxS2_ik1", "L0_attn_Wqkv", "L0_attn_Wproj", "L0_xattn_W_out",
        "L0_xattn_b_out", "L0_ffn_router_w", "L0_ffn_w_gate", "L0_ffn_w_up", "L0_ffn_w_down", "L1_attn_W_kv",
        "L1_attn_g_kv", "L1_attn_W_kdec", "L1_attn_W_vdec", "L1_attn_W_q", "L1_attn_W_qdec", "L1_attn_W_krope",
        "L1_attn_W_qrope", "L1_attn_W_o", "L1_xattn_Wq", "L1_xattn_bq", "L1_xattn_Wk", "L1_xattn_bk", "L1_xattn_Wv",
        "L1_xattn_bv", "L1_xattn_Wo", "L1_xattn_bo", "L1_ffn_Wqkv", "L1_ffn_bqkv", "L1_ffn_Wo", "L1_ffn_bo", "L1_ffn_g1",
        "L1_ffn_be1", "L1_ffn_g2", "L1_ffn_be2", "L1_ffn_Wg", "L1_ffn_W1", "L1_ffn_b1", "L1_ffn_W2", "L1_ffn_b2"]


def shape_constants():
    bf = lambda keep: np.where(keep, 0.0, MASKED).astype(np.float32)
    r, k = np.arange(P)[:, None], np.arange(P)[None, :]
    own, before = k <= r, (k >= r + 1) | (k % 64 == 0)
    never = np.zeros((P, P), bool)
    sparse_q = np.stack([np.concatenate([never, own, before, own], 1), np.concatenate([before, own, before, own], 1)], 1)
    sparse_k = np.concatenate([own.T, before.T, own.T, before.T], 1)
    glob_key = np.arange(16) * 64
    far = glob_key[None, :] // P <= np.arange(T)[:, None] - 2
    c = {"c_ident": np.eye(P, dtype=np.float32)}
    far_q = np.broadcast_to(far.reshape(1, T * 16), (P, T * 16))
    gk = np.zeros((P, S), bool)
    gk[0:16] = np.repeat(far.T, P, axis=1)
    gk[16:] = True
    c["c_sparse"] = bf(np.concatenate([sparse_q.reshape(P, 1024), sparse_k, far_q, gk], 1))
    c["c_causal"] = bf(np.concatenate([own, own.T], 1))
    inv = 1.0 / 10000.0 ** (np.arange(0, 32, 2, dtype=np.float32) / 32)
    f = np.outer(np.arange(S, dtype=np.float32), inv)
    emb = np.concatenate([f, f], -1)
    c["c_cos"] = np.tile(np.cos(emb).T, (4, 1)).astype(np.float32)
    c["c_sin"] = np.tile(np.sin(emb).T, (4, 1)).astype(np.float32)
    c["c_expert"] = np.broadcast_to(np.arange(E, dtype=np.float32) - E, (P, T, E))
    return c


def kernel(**inputs):
    import numpy as _np
    import concourse.bacc as _bacc
    from concourse import mybir as _mybir
    from concourse.bass_utils import run_bass_kernel_spmd as _run

    nc = _bacc.Bacc("TRN2", target_bir_lowering=False, num_devices=1)
    arrays, args = {}, {}
    for name, value in list((n, inputs[n]) for n in _INS) + list(shape_constants().items()):
        v = _np.ascontiguousarray(value)
        arrays[f"in_{name}_dram"] = v
        args[name] = nc.dram_tensor(f"in_{name}_dram", v.shape, _mybir.dt.from_np(v.dtype), kind="ExternalInput").ap()
    out = nc.dram_tensor("out_0_dram", (1, S, D), F32, kind="ExternalOutput").ap()
    build(nc, args, out)
    r = _run(nc, [arrays], core_ids=[0])
    return r.results[0]["out_0_dram"]
```

```python
from contextlib import ExitStack, contextmanager

import numpy as np

import concourse.bass as bass
from concourse import mybir

F32 = mybir.dt.float32
BF16 = mybir.dt.bfloat16
I32 = mybir.dt.int32
ALU = mybir.AluOpType
ACT = mybir.ActivationFunctionType
AXX = mybir.AxisListType.X

P = 128
S = 1024
T = S // P
D = 128
H = 16
HD = D // H
S2 = 6404
NKB = -(-S2 // P)
LASTK = S2 - (NKB - 1) * P
E = 8
MASKED = -(2.0 ** 100)
PAIRS = ((0, 0), (0, 1), (0, 2), (1, 0), (1, 1), (2, 0))
CHUNK_PAIRS = (((0, 0), (0, 1), (1, 0)), ((0, 2), (2, 0), (1, 1)))




class Chain:

    def __init__(self, eng, sem, start=0):
        self.eng, self.sem, self.n = eng, sem, start

    def __call__(self, ins):
        ins.then_inc(self.sem, 1)
        self.n += 1
        self.eng.wait_ge(self.sem, self.n)

    def all(self, instructions):
        for ins in instructions:
            ins.then_inc(self.sem, 1)
        self.n += len(instructions)
        self.eng.wait_ge(self.sem, self.n)


class Core:

    def __init__(self, nc, ctx):
        self.nc, self.ctx, self.names, self.sem_names = nc, ctx, {}, {}
        self.scopes = [(ctx, [])]
        self.X = self.sb(ctx, "X", [P, T, D], F32)
        self.ident = self.sb(ctx, "ident", [P, P], F32)
        self.identb = self.sb(ctx, "identb", [P, P], BF16)
        self.select = self.sb(ctx, "select", [P, T, P], F32)
        self.ps = ctx.enter_context(nc.psum_tensor("ps", [P, 8, 512], F32))

    def sb(self, ctx, name, shape, dt):
        self.names[name] = self.names.get(name, 0) + 1
        name += f"_{self.names[name]}"
        return ctx.enter_context(self.nc.sbuf_tensor(name, shape, dt))

    def sem(self, name):
        self.sem_names[name] = self.sem_names.get(name, 0) + 1
        s = self.scopes[-1][0].enter_context(self.nc.semaphore(f"{name}_{self.sem_names[name]}"))
        self.scopes[-1][1].append(s)
        return s

    @contextmanager
    def stage(self):
        with ExitStack() as ctx:
            self.scopes.append((ctx, []))
            yield
            _, sems = self.scopes.pop()
            with self.nc.Block() as block:
                @block.sync
                def _(sp):
                    for s in sems:
                        sp.sem_clear(s)


def start_block(core, x_dram, ident_dram):
    nc = core.nc
    loaded, copied = core.sem("start_loaded"), core.sem("start_copied")
    with nc.Block() as block:
        @block.sync
        def _(sp):
            sp.dma_start(core.X[:, :, :], x_dram.rearrange("a (t p) d -> p (a t) d", p=P)).then_inc(loaded, 16)
            sp.dma_start(core.ident[:, :], ident_dram).then_inc(loaded, 16)
            sp.wait_ge(loaded, 32)

        @block.vector
        def _(dve):
            dve.wait_ge(loaded, 32)
            nc.vector.tensor_copy(core.identb[:, :], core.ident[:, :]).then_inc(copied, 1)
            for b in range(8):
                nc.vector.memset(core.ps[:, b, :], 0.0).then_inc(copied, 1)
            for t in range(T):
                nc.vector.tensor_copy(core.select[:, t, :].rearrange("p (h d) -> p h d", h=H),
                                      core.ident[:, :].rearrange("p (t h d) -> p t h d", t=T, d=1)[:, t].broadcast_to(
                                          (P, H, HD))).then_inc(copied, 1)
            dve.wait_ge(copied, 9 + T)


def narrow(core, dst, src):
    done = core.sem("narrowed")
    with core.nc.Block() as block:
        @block.vector
        def _(dve):
            core.nc.vector.tensor_copy(dst, src).then_inc(done, 1)
            dve.wait_ge(done, 1)


class LayerNorm:

    def __init__(self, core, ctx):
        self.core = core
        sb = lambda n, s, d=F32: core.sb(ctx, n, s, d)
        self.stats, self.mv = sb("ln_stats", [P, T, 6]), sb("ln_mv", [P, T, 2])
        self.std, self.rstd = sb("ln_std", [P, T]), sb("ln_rstd", [P, T])
        self.dve_done = core.sem("ln_dve_done")
        self.var_ready, self.std_ready = core.sem("ln_var_ready"), core.sem("ln_std_ready")
        self.xn_ready, self.turned, self.hT_ready = core.sem("ln_xn_ready"), core.sem("ln_turned"), core.sem("ln_hT_ready")
        self.loaded = core.sem("ln_loaded")
        self.calls = self.chain_n = self.loads_n = 0

    def normalise(self, dve, link, src, dst, call, eps=1e-5):
        nc = self.core.nc
        link.all([nc.vector.bn_stats(self.stats[:, t, :], src[:, t, :]) for t in range(T)])
        link.all([nc.vector.bn_aggr(self.mv[:, t, :], self.stats[:, t, :]) for t in range(T)])
        nc.vector.tensor_scalar(self.mv[:, :, 1], self.mv[:, :, 1], eps, None, ALU.add).then_inc(self.var_ready, 1)
        dve.wait_ge(self.std_ready, call + 1)
        link(nc.vector.reciprocal(self.rstd[:, :], self.std[:, :]))
        for t in range(T):
            nc.vector.tensor_scalar(dst[:, t, :], src[:, t, :], self.mv[:, t, 0:1], self.rstd[:, t:t + 1],
                                    ALU.subtract, ALU.mult).then_inc(self.xn_ready, 1)
        dve.wait_ge(self.xn_ready, T * (call + 1))

    def root(self, act, call):
        act.wait_ge(self.var_ready, call + 1)
        self.core.nc.scalar.activation(self.std[:, :], self.mv[:, :, 1], ACT.Sqrt).then_inc(self.std_ready, 1)

    def turn(self, pe, call, src, banks=(0, 1)):
        core = self.core
        for t in range(T):
            pe.wait_ge(self.xn_ready, T * call + t + 1)
            core.nc.tensor.transpose(core.ps[:, banks[t // 4], (t % 4) * P:(t % 4 + 1) * P], src[:, t, :],
                                     core.ident[:, :]).then_inc(self.turned, 1)

    def take(self, act, call, hT, banks=(0, 1)):
        core = self.core
        for b in range(2):
            act.wait_ge(self.turned, T * call + 4 * (b + 1))
            core.nc.scalar.copy(hT[:, b * 512:(b + 1) * 512], core.ps[:, banks[b], :]).then_inc(self.hT_ready, 1)

    def block(self, hT, xn, loads, ahead=None):
        core, nc, call = self.core, self.core.nc, self.calls
        self.calls += 1
        with nc.Block() as block:
            @block.sync
            def _(sp):
                for dst, src in loads:
                    sp.dma_start(dst, src).then_inc(self.loaded, 16)
                    self.loads_n += 16
                if ahead:
                    ahead(sp)
                sp.wait_ge(self.loaded, self.loads_n)

            @block.vector
            def _(dve):
                link = Chain(dve, self.dve_done, self.chain_n)
                self.normalise(dve, link, core.X, xn, call)
                self.chain_n = link.n

            @block.scalar
            def _(act):
                self.root(act, call)
                self.take(act, call, hT)

            @block.tensor
            def _(pe):
                self.turn(pe, call, xn)


class Turner:

    def __init__(self, core):
        self.core, self.n = core, 0
        self.turned, self.taken = core.sem("tw_turned"), core.sem("tw_taken")

    def block(self, pairs):
        core, nc, n0 = self.core, self.core.nc, self.n
        self.n += len(pairs)
        pairs = [(src if isinstance(src, list) else [src], dst) for src, dst in pairs]
        with nc.Block() as block:
            @block.tensor
            def _(pe):
                for n, (srcs, dst) in enumerate(pairs):
                    if n >= 4:
                        pe.wait_ge(self.taken, n0 + n - 3)
                    for k, src in enumerate(srcs):
                        r, c = src.shape
                        last = nc.tensor.transpose(core.ps[0:c, n % 4, k * P:k * P + r], src, core.ident[0:r, 0:r])
                    last.then_inc(self.turned, 1)

            @block.scalar
            def _(act):
                for n, (srcs, dst) in enumerate(pairs):
                    r, c = dst.shape
                    act.wait_ge(self.turned, n0 + n + 1)
                    nc.scalar.copy(dst, core.ps[0:r, n % 4, 0:c]).then_inc(self.taken, 1)
                act.wait_ge(self.taken, n0 + len(pairs))


class Splitter:

    def buffers(self, ctx):
        core = self.core
        self.full = core.sb(ctx, "sp_full", [P, 2, 1024], F32)
        self.rest = core.sb(ctx, "sp_rest", [P, 2, 1024], F32)
        self.turned_part = core.sb(ctx, "sp_sin", [P, 1024], F32)
        self.parts = core.sb(ctx, "sp_parts", [P, 3, 3, 1024], BF16)
        return self

    def __init__(self, core):
        self.core = core
        self.projected, self.full_ready = core.sem("sp_projected"), core.sem("sp_full_ready")
        self.hi_ready, self.rest_ready = core.sem("sp_hi_ready"), core.sem("sp_rest_ready")
        self.mid_ready, self.lo_ready = core.sem("sp_mid_ready"), core.sem("sp_lo_ready")
        self.rope_done = core.sem("sp_rope_done")
        self.written = [core.sem(f"sp_written{q}") for q in range(3)]
        self.count, self.ropes, self.writes = 0, 0, [0, 0, 0]

    def finish(self, sp):
        for q in range(3):
            sp.wait_ge(self.written[q], self.writes[q])

    def block(self, items, pool_beside=None, sync_beside=None):
        core, nc = self.core, self.core.nc
        n0, r0, w0 = self.count, self.ropes, list(self.writes)
        assert n0 % 2 == 0
        self.count += len(items) + len(items) % 2
        pad = len(items) % 2
        ps = core.ps

        def done(par, upto):
            return w0[par] + 16 * sum(len(it[4]) for k, it in enumerate(items[:upto]) if k % 3 == par)

        with nc.Block() as block:
            @block.tensor
            def _(pe):
                for n, (w, matmuls, bias, rope, writes) in enumerate(items):
                    if n >= 2:
                        pe.wait_ge(self.full_ready, n0 + n - 1)
                    b = 4 * (n % 2)
                    matmuls(pe, ps[:, b:b + 2, :].rearrange("p b c -> p (b c)"),
                            ps[:, b + 2:b + 4, :].rearrange("p b c -> p (b c)")).then_inc(self.projected, 1 + pad * (n == len(items) - 1))

            @block.scalar
            def _(act):
                def first(n):
                    w, _, bias, rope, _ = items[n]
                    b, q, last = 4 * (n % 2), n % 2, pad * (n == len(items) - 1)
                    if rope is None:
                        act.wait_ge(self.projected, n0 + n + 1)
                        if n >= 2:
                            act.wait_ge(self.rest_ready, n0 + n - 1)
                        src = ps[:, b:b + 2, :].rearrange("p b c -> p (b c)")[:, 0:w]
                        if bias is None:
                            ins = nc.scalar.copy(self.full[:, q, 0:w], src)
                        else:
                            ins = nc.scalar.activation(self.full[:, q, 0:w], src, ACT.Identity, bias=bias)
                        ins.then_inc(self.full_ready, 1 + last)
                    act.wait_ge(self.full_ready, n0 + n + 1)
                    if n >= 3:
                        act.wait_ge(self.written[n % 3], done(n % 3, n))
                    nc.scalar.copy(self.parts[:, n % 3, 0, 0:w], self.full[:, q, 0:w]).then_inc(self.hi_ready, 1 + last)

                first(0)
                for n in range(len(items)):
                    w, last = items[n][0], pad * (n == len(items) - 1)
                    if n + 1 < len(items):
                        first(n + 1)
                    act.wait_ge(self.rest_ready, n0 + n + 1)
                    nc.scalar.copy(self.parts[:, n % 3, 1, 0:w], self.rest[:, n % 2, 0:w]).then_inc(self.mid_ready, 1 + last)

            @block.vector
            def _(dve):
                def rotate(n):
                    _, _, _, rope, _ = items[n]
                    b, q, last = 4 * (n % 2), n % 2, pad * (n == len(items) - 1)
                    if rope is None:
                        return
                    dve.wait_ge(self.projected, n0 + n + 1)
                    if n >= 1:
                        dve.wait_ge(self.full_ready, n0 + n)
                    if n >= 2:
                        dve.wait_ge(self.rest_ready, n0 + n - 1)
                        dve.wait_ge(self.hi_ready, n0 + n - 1)
                    nc.vector.tensor_tensor(self.full[:, q, :], ps[:, b:b + 2, :].rearrange("p b c -> p (b c)"),
                                            rope[0], ALU.mult).then_inc(self.rope_done, 1)
                    nc.vector.tensor_tensor(self.turned_part[:, :], ps[:, b + 2:b + 4, :].rearrange("p b c -> p (b c)"),
                                            rope[1], ALU.mult).then_inc(self.rope_done, 1)
                    self.ropes += 2
                    dve.wait_ge(self.rope_done, self.ropes)
                    nc.vector.tensor_tensor(self.full[:, q, :], self.full[:, q, :], self.turned_part[:, :],
                                            ALU.add).then_inc(self.full_ready, 1 + last)

                def low(n):
                    w, last = items[n][0], pad * (n == len(items) - 1)
                    dve.wait_ge(self.mid_ready, n0 + n + 1)
                    nc.vector.tensor_tensor(self.parts[:, n % 3, 2, 0:w], self.rest[:, n % 2, 0:w], self.parts[:, n % 3, 1, 0:w],
                                            ALU.subtract).then_inc(self.lo_ready, 1 + last)

                rotate(0)
                for n in range(len(items)):
                    w, last = items[n][0], pad * (n == len(items) - 1)
                    if n + 1 < len(items):
                        rotate(n + 1)
                    dve.wait_ge(self.full_ready, n0 + n + 1)
                    dve.wait_ge(self.hi_ready, n0 + n + 1)
                    if n >= 2:
                        dve.wait_ge(self.lo_ready, n0 + n - 1)
                    nc.vector.tensor_tensor(self.rest[:, n % 2, 0:w], self.full[:, n % 2, 0:w], self.parts[:, n % 3, 0, 0:w],
                                            ALU.subtract).then_inc(self.rest_ready, 1 + last)
                    if n >= 1:
                        low(n - 1)
                low(len(items) - 1)

            @block.sync
            def _(sp):
                for n, (w, matmuls, bias, rope, writes) in enumerate(items):
                    sp.wait_ge(self.lo_ready, n0 + n + 1)
                    for dst, part in writes:
                        sp.dma_start(dst, self.parts[:, n % 3, part, 0:w]).then_inc(self.written[n % 3], 16)
                for q in range(3):
                    self.writes[q] = done(q, len(items))
                if sync_beside:
                    sync_beside(sp)

            if pool_beside:
                @block.gpsimd
                def _(pool):
                    pool_beside(pool)


def project(core, w, hT, width=1024, at=0):
    def matmuls(pe, a, b):
        for c in range(0, width, 512):
            n = min(512, width - c)
            last = core.nc.tensor.matmul(a[:, c:c + n], w, hT[:, at + c:at + c + n], start=True, stop=True)
        return last
    return matmuls


def project_two(core, w, turned, hT):
    def matmuls(pe, a, b):
        for dst, weights in ((a, w), (b, turned)):
            for c in range(0, S, 512):
                last = core.nc.tensor.matmul(dst[:, c:c + 512], weights, hT[:, c:c + 512], start=True, stop=True)
        return last
    return matmuls


def values_block(core, name, Vaug, tiles, splitter, bias_rows=None):
    nc = core.nc
    ones, made, taken = core.sem(name + "_ones"), core.sem(name + "_made"), core.sem(name + "_taken")
    with nc.Block() as block:
        @block.gpsimd
        def _(pool):
            nc.gpsimd.memset(Vaug[:, :, len(tiles) - 1, :], 0.0).then_inc(ones, 1)
            pool.wait_ge(ones, 1)
            for h in range(H):
                nc.gpsimd.memset(Vaug[:, h, :, HD:HD + 1], 1.0).then_inc(ones, 1)
            pool.wait_ge(ones, 1 + H)

        @block.sync
        def _(sp):
            splitter.finish(sp)

        @block.tensor
        def _(pe):
            for t, (rows, lhsT, rhs) in enumerate(tiles):
                if t >= 8:
                    pe.wait_ge(taken, t - 7)
                nc.tensor.matmul(core.ps[0:rows, t % 8, 0:D], lhsT, rhs, start=True, stop=True).then_inc(made, 1)

        @block.vector
        def _(dve):
            dve.wait_ge(ones, 1 + H)
            for t, (rows, lhsT, rhs) in enumerate(tiles):
                dve.wait_ge(made, t + 1)
                dst = Vaug[0:rows, :, t, 0:HD]
                src = core.ps[0:rows, t % 8, 0:D].rearrange("p (h d) -> p h d", h=H)
                if bias_rows is None:
                    nc.vector.tensor_copy(dst, src).then_inc(taken, 1)
                else:
                    nc.vector.tensor_tensor(dst, src, bias_rows[0:rows, :].rearrange("p (h d) -> p h d", h=H),
                                            ALU.add).then_inc(taken, 1)
            dve.wait_ge(taken, len(tiles))


def negated_max_parts(nc, link, mx, m, rest, parts, done):
    link(nc.vector.tensor_reduce(m, mx, AXX, ALU.max))
    link(nc.vector.tensor_scalar(parts[:, 0, :], m, -1.0, None, ALU.mult))
    link(nc.vector.scalar_tensor_tensor(rest, m, -1.0, parts[:, 0, :], ALU.mult, ALU.subtract))
    link(nc.vector.tensor_copy(parts[:, 1, :], rest))
    nc.vector.tensor_tensor(parts[:, 2, :], rest, parts[:, 1, :], ALU.subtract).then_inc(done, 1)


class SelfAttention:

    PACE = 2

    def __init__(self, core, name, chunks, fills, tiles, slots, lead):
        self.lead = lead
        self.core, self.name, self.chunks, self.fills, self.tiles, self.slots = core, name, chunks, fills, tiles, slots

    def run(self, ctx, loads, Vaug, Vglob, scale, O_dram):
        core, nc, name = self.core, self.core.nc, self.name
        ps, ident = core.ps, core.identb
        nt, nf = len(self.tiles), len(self.fills)
        LEAD, PACE = self.lead, self.PACE
        sb = lambda n, s, d: core.sb(ctx, name + n, s, d)
        sem = lambda n: core.sem(name + n)
        nch = self.chunks
        Qa = [sb(f"Qa{p}", [P, nch, S], BF16) for p in range(2)]
        Qb = [sb(f"Qb{p}", [P, nch, S], BF16) for p in range(2)]
        Ka = [sb(f"Ka{p}", [P, nch, S], BF16) for p in range(2)]
        Kb = [sb(f"Kb{p}", [P, nch, S], BF16) for p in range(2)]
        V = [sb(f"V{p}", [P, T, HD + 1], F32) for p in range(2)]
        VG = [sb(f"VG{p}", [P, HD + 1], F32) for p in range(2)]
        Pt = [sb(f"P{u}", [P, S], F32) for u in range(nt)]
        O = sb("O", [P, S], F32)
        mx = [sb(f"mx{p}", [P, T, self.slots], F32) for p in range(2)]
        m, rest = sb("m", [P, T], F32), sb("rest", [P, T], F32)
        mparts = [sb(f"mparts{p}", [P, 3, T], BF16) for p in range(2)]
        cleared, slots_cleared = sem("cleared"), sem("slots_cleared")
        qa_ready = [sem(f"qa_ready{p}") for p in range(2)]
        qb_ready = [sem(f"qb_ready{p}") for p in range(2)]
        scores_ready, exp_done, p_used = sem("scores_ready"), sem("exp_done"), sem("p_used")
        fill_ready, fill_taken = sem("fill_ready"), sem("fill_taken")
        maxes_ready, rows_ready, rows_copied = sem("maxes_ready"), sem("rows_ready"), sem("rows_copied")
        o_copied, o_written, v_ready, vec = sem("o_copied"), sem("o_written"), sem("v_ready"), sem("vec")
        vg_ready = sem("vg_ready")
        slots = Qa + Qb + Ka + Kb

        with nc.Block() as block:
            @block.gpsimd
            def _(pool):
                for t in VG:
                    nc.gpsimd.memset(t[:, :], 0.0).then_inc(cleared, 1)
                for t in mx:
                    nc.gpsimd.memset(t[:, :, :], MASKED).then_inc(cleared, 1)
                for t in Pt:
                    nc.gpsimd.memset(t[:, :], 0.0).then_inc(cleared, 1)
                pool.wait_ge(cleared, len(VG) + len(mx) + nt)

            @block.vector
            def _(dve):
                for b in (4, 5):
                    nc.vector.memset(ps[:, b, :], 0.0).then_inc(vec, 1)
                dve.wait_ge(vec, 2)
                for n, t in enumerate(slots):
                    nc.vector.memset(t[:, :, :], 1.0 if n >= 6 else 0.0).then_inc(slots_cleared, 1)
                dve.wait_ge(slots_cleared, 8)

            @block.sync
            def _(sp):
                sp.sem_inc(fill_ready, 2 * nf)
                sp.sem_inc(scores_ready, 2 * nt)
                sp.sem_inc(exp_done, 2)
                sp.sem_inc(fill_taken, 2)
                sp.sem_inc(p_used, 2 * nt)
                sp.sem_inc(o_copied, 1)
                sp.sem_inc(o_written, 4 * 16)

        def load(sp, dst, kind, g, ready):
            for rows, src in loads[kind]:
                sp.dma_start(dst[rows[0]:rows[1], :, :], src(g)).then_inc(ready, 16)

        nq, nk = len(loads["q"]), len(loads["k"])

        with nc.Block() as block:
            @block.sync
            def _(sp):
                def store(g):
                    sp.wait_ge(o_copied, g + 2)
                    for j in range(4):
                        sp.dma_start(O_dram[bass.ds(g, 1), j].rearrange("a r c -> (a r) c"),
                                     O[32 * j:32 * j + HD + 1, :]).then_inc(o_written, 16)

                def pair(i, stores):
                    for p in range(2):
                        g = i * 2 + p
                        sp.wait_ge(fill_ready, g * nf + nf)
                        load(sp, Qa[p], "q", g, qa_ready[p])
                        load(sp, Ka[p], "k", g, qa_ready[p])
                        sp.wait_ge(scores_ready, g * nt + nt)
                        load(sp, Qb[p], "q", g, qb_ready[p])
                        load(sp, Kb[p], "k", g, qb_ready[p])
                        if stores:
                            store(i * 2 + (p - 2))

                pair(0, False)
                with sp.Fori(1, H // 2) as i:
                    pair(i, True)
                store(H - 2)
                store(H - 1)
                sp.wait_ge(o_written, (H + 1) * 64)

            @block.gpsimd
            def _(pool):
                with pool.Fori(0, H // 2) as i:
                    for p in range(2):
                        g = i * 2 + p
                        pool.wait_ge(p_used, g * nt + nt)
                        nc.gpsimd.tensor_copy(V[p][:, :, :], Vaug[:, bass.ds(g, 1), :, :].rearrange(
                            "p a t c -> p (a t) c")).then_inc(v_ready, 1)
                        if Vglob is not None:
                            nc.gpsimd.tensor_copy(VG[p][0:16, :], Vglob[0:16, bass.ds(g, 1), :].rearrange(
                                "p a c -> p (a c)")).then_inc(vg_ready, 1)

            def fill_scores(pe, g, p, f, i):
                n = (p * nf + f) % 2
                pe.wait_ge(fill_taken, g * nf + f + 1)
                if f == 0:
                    pe.wait_ge(qa_ready[p], (i + 1) * 16 * (nq + nk))
                for k, (kind, a, b, col, w) in enumerate(self.fills[f][0]):
                    dst = ps[:, 6 + n, col:col + w]
                    if kind == "mask":
                        last = nc.tensor.matmul(dst, ident[:, :], b, start=(k == 0), stop=False, skip_group_check=True)
                        continue
                    for c in range(nch):
                        rhs = b(Ka[p][:, c, :])
                        last = nc.tensor.matmul(dst, Qa[p][:, c, a * P:(a + 1) * P], rhs, start=(k == 0 and c == 0),
                                                stop=False, skip_group_check=True)
                last.then_inc(fill_ready, 1)

            def max_rows(pe, g, p):
                pe.wait_ge(maxes_ready, g + 1)
                pe.wait_ge(exp_done, g * nt + 1)
                for t in range(T):
                    last = nc.tensor.matmul(ps[96:99, 2 * (p * nt % 2) + t // 4, (t % 4) * P:(t % 4 + 1) * P], mparts[p][:, :, t],
                                            ident[:, :], start=(t % 4 == 0), stop=False, skip_group_check=True)
                last.then_inc(rows_ready, 1)

            def tile_scores(pe, g, p, u, i):
                n = (p * nt + u) % 2
                pe.wait_ge(exp_done, g * nt + u + 1)
                if u == 0:
                    pe.wait_ge(qb_ready[p], (i + 1) * 16 * (nq + nk))
                    pe.wait_ge(rows_copied, g + 1)
                begun = set()
                for kind, a, b, col, w in self.tiles[u]["scores"]:
                    bank, rows = 2 * n + col // 512, self.tiles[u]["rows"]
                    dst = ps[0:rows, bank, col % 512:col % 512 + w]
                    if kind == "mask":
                        last = nc.tensor.matmul(dst, ident[:, 0:rows], b, start=bank not in begun, stop=False,
                                                skip_group_check=True)
                        begun.add(bank)
                        continue
                    for c in range(nch):
                        last = nc.tensor.matmul(dst, a(Kb[p][:, c, :]), Qb[p][:, c, b:b + w], start=bank not in begun,
                                                stop=False, skip_group_check=True)
                        begun.add(bank)
                last.then_inc(scores_ready, 1)

            def tile_values(pe, g, p, u, begun):
                pe.wait_ge(exp_done, 2 + g * nt + u + 1)
                if u == 0:
                    pe.wait_ge(v_ready, g + 1)
                    if Vglob is not None:
                        pe.wait_ge(vg_ready, g + 1)
                    pe.wait_ge(o_copied, g + 1)
                for col, w, kb, j, q0 in self.tiles[u]["values"]:
                    key = (q0 // 512, j)
                    lhsT = VG[p][:, :] if kb is None else V[p][:, kb, :]
                    last = nc.tensor.matmul(ps[32 * j:32 * j + HD + 1, 4 + q0 // 512, q0 % 512:q0 % 512 + w], lhsT,
                                            Pt[u][:, col:col + w], start=key not in begun, stop=False,
                                            skip_group_check=True)
                    begun.add(key)
                last.then_inc(p_used, 1)

            @block.tensor
            def _(pe):
                for f in range(nf):
                    fill_scores(pe, 0, 0, f, 0)
                max_rows(pe, 0, 0)
                for f in range(LEAD):
                    fill_scores(pe, 1, 1, f, 0)

                def head(g, p, i, more, more2):
                    begun = set()
                    f = LEAD
                    for u in range(nt):
                        tile_scores(pe, g, p, u, i)
                        while more and f < min(nf, LEAD + ((u + PACE) * (nf - LEAD)) // nt):
                            fill_scores(pe, g + 1, 1 - p, f, i + p)
                            f += 1
                        if u >= 1:
                            tile_values(pe, g, p, u - 1, begun)
                    if more and LEAD == 0:
                        max_rows(pe, g + 1, 1 - p)
                    tile_values(pe, g, p, nt - 1, begun)
                    if more and LEAD:
                        max_rows(pe, g + 1, 1 - p)
                    if more2:
                        for f in range(LEAD):
                            fill_scores(pe, g + 2, p, f, i + 1)
                with pe.Fori(0, H // 2 - 1) as i:
                    head(i * 2, 0, i, True, True)
                    head(i * 2 + 1, 1, i, True, True)
                head(H - 2, 0, H // 2 - 1, True, False)
                head(H - 1, 1, H // 2 - 1, False, False)

            @block.vector
            def _(dve):
                def maxima(g, p, base):
                    for f in range(nf):
                        dve.wait_ge(fill_ready, g * nf + (2 * nf + f + 1))
                        reds = self.fills[f][1]
                        for k, (col, w, nseg, dst) in enumerate(reds):
                            src = ps[:, 6 + (p * nf + f) % 2, col:col + w]
                            out = mx[p][:, dst[0]:dst[0] + nseg, dst[1]]
                            ins = nc.vector.tensor_reduce(out, src.rearrange("p (n w) -> p n w", n=nseg), AXX, ALU.max)
                            if k == len(reds) - 1:
                                ins.then_inc(fill_taken, 1)
                            else:
                                ins.then_inc(vec, 1)
                    dve.wait_ge(fill_taken, 2 + (g + 1) * nf)
                    extra = sum(len(x[1]) - 1 for x in self.fills)
                    n = 4 + extra
                    start = 2 + g * n + extra
                    if extra:
                        dve.wait_ge(vec, start)
                    link = Chain(dve, vec, start)
                    negated_max_parts(nc, link, mx[p][:, :, :], m[:, :], rest[:, :], mparts[p], maxes_ready)
                    dve.wait_ge(maxes_ready, g + 1)
                maxima(0, 0, 0)
                with dve.Fori(0, H // 2 - 1) as i:
                    maxima(i * 2 + 1, 1, 0)
                    maxima(i * 2 + 2, 0, 0)
                maxima(H - 1, 1, 0)

            @block.scalar
            def _(act):
                def rows(g, p):
                    act.wait_ge(rows_ready, g + 1)
                    nc.scalar.copy(Qb[p][96:99, 0, :], ps[96:99, 2 * (p * nt % 2):2 * (p * nt % 2) + 2, :].rearrange(
                        "p b c -> p (b c)")).then_inc(rows_copied, 1)

                def output(g):
                    act.wait_ge(p_used, g * nt + 3 * nt)
                    act.wait_ge(o_written, g * 64 + 64)
                    nc.scalar.copy(O[:, :], ps[:, 4:6, :].rearrange("p b c -> p (b c)")).then_inc(o_copied, 1)

                def head(g, p, first, more):
                    for u in range(nt):
                        n, r, w = (p * nt + u) % 2, self.tiles[u]["rows"], self.tiles[u]["width"]
                        act.wait_ge(scores_ready, g * nt + (2 * nt + u + 1))
                        act.wait_ge(p_used, g * nt + (nt + u + 1))
                        nc.scalar.activation(Pt[u][0:r, 0:w], ps[0:r, 2 * n:2 * n + 2, :].rearrange(
                            "p b c -> p (b c)")[:, 0:w], ACT.Exp, scale=scale).then_inc(exp_done, 1)
                        if u == 0 and not first:
                            output(g - 1)
                    if more:
                        rows(g + 1, 1 - p)
                rows(0, 0)
                head(0, 0, True, True)
                with act.Fori(0, H // 2 - 1) as i:
                    head(i * 2 + 1, 1, False, True)
                    head(i * 2 + 2, 0, False, True)
                head(H - 1, 1, False, False)
                output(H - 1)


class Combiner:

    def __init__(self, core):
        self.core = core
        sem = core.sem
        self.o_loaded = [sem(f"cb_o_loaded{half}") for half in range(2)]
        self.s_loaded, self.vec, self.inverses = sem("cb_s_loaded"), sem("cb_vec"), sem("cb_inverses")
        self.spread, self.y_ready, self.proj, self.added = sem("cb_spread"), sem("cb_y_ready"), sem("cb_proj"), sem("cb_added")
        self.calls = self.o_loads = self.s_loads = self.chain = 0

    def block(self, Osum, sums, tmp, outputs, s_srcs, W, bias_rows):
        core, nc, call, ps = self.core, self.core.nc, self.calls, self.core.ps
        self.calls += 1
        nparts = len(outputs[0])
        self.o_loads += 16 * nparts
        self.s_loads += 16 * len(s_srcs)
        o_loads, s_loads, chain = self.o_loads, self.s_loads, self.chain
        self.chain += 3 * (nparts - 1) + (bias_rows is not None)
        with nc.Block() as block:
            @block.sync
            def _(sp):
                for rows, src in s_srcs:
                    sp.dma_start(sums[rows[0]:rows[1], :, :], src).then_inc(self.s_loaded, 16)
                for half in range(2):
                    for j, src in enumerate(outputs[half]):
                        sp.dma_start(Osum[:, j, half * 512:(half + 1) * 512], src).then_inc(self.o_loaded[half], 16)
                sp.wait_ge(self.s_loaded, s_loads)
                for half in range(2):
                    sp.wait_ge(self.o_loaded[half], o_loads)

            @block.vector
            def _(dve):
                link = Chain(dve, self.vec, chain)
                if bias_rows is not None:
                    link(nc.vector.tensor_tensor(core.X[:, :, :], core.X[:, :, :], bias_rows.rearrange(
                        "p (a d) -> p a d", a=1).broadcast_to((P, T, D)), ALU.add))
                dve.wait_ge(self.s_loaded, s_loads)
                for j in range(1, nparts):
                    link(nc.vector.tensor_tensor(sums[:, 0, :], sums[:, 0, :], sums[:, j, :], ALU.add))
                nc.vector.reciprocal(sums[:, 0, :], sums[:, 0, :]).then_inc(self.inverses, 1)
                for half in range(2):
                    cols = slice(half * 512, half * 512 + 512)
                    dve.wait_ge(self.o_loaded[half], o_loads)
                    for j in range(1, nparts):
                        link(nc.vector.tensor_tensor(Osum[:, 0, cols], Osum[:, 0, cols], Osum[:, j, cols], ALU.add))
                    dve.wait_ge(self.spread, 2 * call + half + 1)
                    nc.vector.tensor_tensor(tmp[:, cols], Osum[:, 0, cols], ps[:, half, :], ALU.mult).then_inc(self.y_ready, 1)
                for half in range(2):
                    dve.wait_ge(self.proj, 2 * call + half + 1)
                    X = core.X[:, 4 * half:4 * half + 4, :]
                    nc.vector.tensor_tensor(X, X, ps[:, 2 + half, :].rearrange("p (t d) -> p t d", t=4), ALU.add).then_inc(self.added, 1)
                dve.wait_ge(self.added, 2 * (call + 1))

            @block.tensor
            def _(pe):
                pe.wait_ge(self.inverses, call + 1)
                for half in range(2):
                    for t in range(4):
                        last = nc.tensor.matmul(ps[:, half, t * P:(t + 1) * P], core.select[:, 4 * half + t, :],
                                                sums[:, 0, :], start=True, stop=True)
                    last.then_inc(self.spread, 1)
                for half in range(2):
                    pe.wait_ge(self.y_ready, 2 * call + half + 1)
                    for t in range(4 * half, 4 * half + 4):
                        last = nc.tensor.matmul(ps[:, 2 + half, (t % 4) * D:(t % 4 + 1) * D], tmp[:, t * P:(t + 1) * P], W,
                                                start=True, stop=True)
                    last.then_inc(self.proj, 1)


ADDS = [3, 7, 11, 15, 19, 23]


class CrossAttention:

    SQ = 512
    NU = (NKB + 1) // 2
    CH = [0, 1536, 3072, 4608, S2]
    CH_LAST_TILE = [5, 11, 17, 25]
    CH_PIECES = [12, 24, 36, 52]
    NPC = -(-S2 // 512)
    LEAD = 10
    NP = 4 * NPC
    OUT = 4
    ROWS = 3

    def __init__(self, core, ctx, name, scale, masked):
        self.core, self.name, self.scale, self.masked = core, name, scale, masked
        sb = lambda n, s, d: core.sb(ctx, name + n, s, d)
        sem = lambda n: core.sem(name + n)
        SQ = self.SQ
        self.K = [sb(f"K{p}", [P, S2], BF16) for p in range(2)]
        self.Qa = [sb(f"Qa{p}", [P, SQ], BF16) for p in range(2)]
        self.Qb = [sb(f"Qb{p}", [P, SQ], BF16) for p in range(2)]
        self.V = [sb(f"V{p}", [P, NKB, HD + 1], F32) for p in range(2)]
        self.Pt = sb("P", [P, 4, 2 * SQ], F32)
        self.O = [sb(f"O{p}", [P, SQ], F32) for p in range(2)]
        self.mx = [sb(f"mx{p}", [P, 4, self.NPC], F32) for p in range(2)]
        self.m, self.rest = sb("m", [P, 4], F32), sb("rest", [P, 4], F32)
        self.mparts = [sb(f"mparts{p}", [P, 3, 4], BF16) for p in range(2)]
        self.junk = sb("junk", [P, 3, SQ], BF16) if masked else None
        self.cleared, self.k_cleared = sem("cleared"), sem("k_cleared")
        self.k_ready = [[sem(f"k_ready{p}{c}") for c in range(4)] for p in range(2)]
        self.qa_ready = [sem(f"qa_ready{p}") for p in range(2)]
        self.qb_ready = [sem(f"qb_ready{p}") for p in range(2)]
        self.scores_ready, self.exp_done, self.p_used = sem("scores_ready"), sem("exp_done"), sem("p_used")
        self.piece_ready, self.piece_taken = sem("piece_ready"), sem("piece_taken")
        self.maxes_ready, self.rows_ready, self.rows_copied = sem("maxes_ready"), sem("rows_ready"), sem("rows_copied")
        self.o_copied, self.piece_seen = sem("o_copied"), sem("piece_seen")
        self.o_written = [sem(f"o_written{p}") for p in range(2)]
        self.v_ready, self.vec, self.mask_added = sem("v_ready"), sem("vec"), sem("mask_added")
        self.adds = ADDS if masked else []

    def clear_block(self, bias_row, narrower=None, masks=None):
        core, nc = self.core, self.core.nc
        tiles = self.Qa + self.Qb + self.O
        bias_loaded = core.sem(self.name + "bias_loaded")
        with nc.Block() as block:
            @block.gpsimd
            def _(pool):
                for t in tiles:
                    nc.gpsimd.memset(t[:, :], 0.0).then_inc(self.cleared, 1)
                pool.wait_ge(self.cleared, 6)
                if bias_row is not None:
                    for t in self.Qa + self.Qb:
                        nc.gpsimd.memset(t[64:65, :], 1.0).then_inc(self.cleared, 1)
                    pool.wait_ge(self.cleared, 10)
                if narrower:
                    narrower.clear(pool)

            @block.vector
            def _(dve):
                nc.vector.memset(core.ps[:, self.OUT, :], 0.0).then_inc(self.vec, 1)
                for t in self.K:
                    nc.vector.memset(t[:, :], 1.0).then_inc(self.k_cleared, 1)
                dve.wait_ge(self.k_cleared, 2)
                if masks:
                    masks.clear(dve)
                dve.wait_ge(self.vec, 1)

            @block.sync
            def _(sp):
                sp.wait_ge(self.k_cleared, 2)
                if bias_row is not None:
                    for t in self.K:
                        sp.dma_start(t[64:65, :], bias_row).then_inc(bias_loaded, 16)
                    sp.wait_ge(bias_loaded, 32)
                sp.sem_inc(self.piece_ready, 2 * self.NP)
                sp.sem_inc(self.scores_ready, 2 * self.NU)
                sp.sem_inc(self.exp_done, 2)
                sp.sem_inc(self.p_used, self.NU + 4)
                sp.sem_inc(self.piece_taken, 3)
                sp.sem_inc(self.o_copied, 2)

    def block(self, Qs, Ks, Vaug, O_dram, narrower=None, masks=None):
        core, nc = self.core, self.core.nc
        ps, ident, SQ, NU, NPC = core.ps, core.identb, self.SQ, self.NU, self.NPC
        K, Qa, Qb, V, Pt, O, mx, mparts = self.K, self.Qa, self.Qb, self.V, self.Pt, self.O, self.mx, self.mparts
        NP = self.NP
        LEAD = self.LEAD
        Ks_heads = Ks.rearrange("r (h d) c -> h r d c", h=H)
        g0, i0, i1 = 0, 0, H
        end = 2 * i1
        turn = H // 2
        vec0 = 1

        with nc.Block() as block:
            @block.sync
            def _(sp):
                def store(g, p):
                    sp.wait_ge(self.o_copied, g + 1)
                    for j in range(4):
                        sp.dma_start(O_dram[bass.ds(g, 1), j].rearrange("a r c -> (a r) c"),
                                     O[1 - p][32 * j:32 * j + HD + 1, :]).then_inc(self.o_written[1 - p], 16)

                def pair(i, half, fresh):
                    for p in range(2):
                        g = i * 2 + p
                        h = i * 2 + (p - half * H)
                        src = Qs[bass.ds(h, 1), :, half * SQ:(half + 1) * SQ].rearrange("a r c -> (a r) c")
                        sp.wait_ge(self.piece_ready, g * NP + NP)
                        sp.dma_start(Qa[p][0:48, :], src).then_inc(self.qa_ready[p], 16)
                        store(g, p)
                        for c in range(4):
                            sp.wait_ge(self.scores_ready, g * NU + (self.CH_LAST_TILE[c] + 1))
                            if fresh and p == 0:
                                sp.wait_ge(self.piece_taken, (g - 1) * NP + (3 + self.CH_PIECES[c]))
                                masks.load_queries(sp, 1, c)
                                sp.wait_ge(masks.queries_loaded, 64 + 16 * (c + 1))
                            a, b = self.CH[c], self.CH[c + 1]
                            for n in (3, 2, 1):
                                row = {3: 0, 2: 3 * HD, 1: 5 * HD}[n]
                                sp.dma_start(K[p][row:row + n * HD, a:b], Ks_heads[bass.ds(h, 1), 0:n, :, a:b].rearrange(
                                    "a r d c -> (a r) d c")).then_inc(self.k_ready[p][c], 16)
                        sp.dma_start(Qb[p][0:48, :], src).then_inc(self.qb_ready[p], 16)
                        if narrower:
                            narrower.transfers(sp, g, p)

                if masks:
                    sp.wait_ge(masks.queries_loaded, 64)
                with sp.Fori(0, turn) as i:
                    pair(i, 0, False)
                if masks:
                    pair(turn, 1, True)
                with sp.Fori(turn + (masks is not None), H) as i:
                    pair(i, 1, False)
                for g in range(2 * H, 2 * H + 3):
                    store(g, g % 2)
                if narrower:
                    narrower.finish(sp)
                sp.wait_ge(self.o_written[0], 64 * (H + 1))
                sp.wait_ge(self.o_written[1], 64 * (H + 2))

            @block.gpsimd
            def _(pool):
                for half in range(2):
                    with pool.Fori(half * turn, (half + 1) * turn) as i:
                        for p in range(2):
                            g = i * 2 + p
                            pool.wait_ge(self.p_used, g * NU + 4)
                            nc.gpsimd.tensor_copy(V[p][:, :, :], Vaug[:, bass.ds(i * 2 + (p - half * H), 1), :, :].rearrange(
                                "p a t c -> p (a t) c")).then_inc(self.v_ready, 1)
                            if narrower:
                                narrower.convert(pool, g, p, i)

            @block.tensor
            def _(pe):
                def piece(g, p, k, i):
                    c, t = k // 4, k % 4
                    w = min(512, S2 - c * 512)
                    shift = p == 0 and k < 2
                    pe.wait_ge(self.piece_taken, g * NP + (k + 1 + shift))
                    if k == 0:
                        pe.wait_ge(self.qa_ready[p], i * 16 + 16)
                    if t == 0 and c * 512 in self.CH:
                        pe.wait_ge(self.k_ready[p][self.CH.index(c * 512)], i * 48 + 48)
                    ins = nc.tensor.matmul(ps[:, 5 + (k + p) % 3, 0:w], Qa[p][:, t * P:(t + 1) * P],
                                           K[p][:, c * 512:c * 512 + w], start=True, stop=True)
                    ins.then_inc(self.piece_ready, 1)

                def rows(g, p):
                    pe.wait_ge(self.maxes_ready, g + 1)
                    for t in range(4):
                        last = nc.tensor.matmul(ps[96:99, self.ROWS, t * P:(t + 1) * P], mparts[p][:, :, t], ident[:, :],
                                                start=(t == 0), stop=False, skip_group_check=True)
                    last.then_inc(self.rows_ready, 1)

                def banks_free(g, u):
                    if u - 2 in self.adds:
                        pe.wait_ge(self.mask_added, g * len(self.adds) + (self.adds.index(u - 2) + 1))
                    else:
                        pe.wait_ge(self.exp_done, g * NU + (u + 1))

                def scores(g, p, u, i, fresh=None):
                    banks_free(g, u)
                    if u == 0:
                        pe.wait_ge(self.qb_ready[p], i * 16 + 16)
                        pe.wait_ge(self.rows_copied, g + 1)
                    if fresh is not None:
                        pe.wait_ge(masks.keys_ready, fresh * NU + u + 1)
                    for kb in range(2 * u, min(2 * u + 2, NKB)):
                        r = min(P, S2 - kb * P)
                        dst = ps[0:r, 2 * (u % 2) + kb % 2, :]
                        if self.masked and u not in self.adds:
                            nc.tensor.matmul(dst, ident[:, 0:r], masks.by_keys[:, kb, :], start=True, stop=False)
                        last = nc.tensor.matmul(dst, K[p][:, kb * P:kb * P + r], Qb[p][:, :],
                                                start=not self.masked or u in self.adds, stop=True)
                    last.then_inc(self.scores_ready, 1)

                def turn_mask(g, u):
                    banks_free(g, u)
                    for kb in range(2 * u, min(2 * u + 2, NKB)):
                        r = min(P, S2 - kb * P)
                        for t in range(4):
                            last = nc.tensor.transpose(ps[0:r, 2 * (u % 2) + kb % 2, t * 64:(t + 1) * 64].bitcast(BF16),
                                                       masks.by_queries[:, t, kb * P:kb * P + r], ident[:, :])
                    last.then_inc(masks.turned, 1)

                def values(g, p, q):
                    pe.wait_ge(self.exp_done, g * NU + (2 + 2 * q + 2))
                    if q == 0:
                        pe.wait_ge(self.v_ready, g + 1)
                        pe.wait_ge(self.o_copied, g + 3)
                    for kb in range(4 * q, min(4 * q + 4, NKB)):
                        r, u, j = min(P, S2 - kb * P), kb // 2, kb % 4
                        last = nc.tensor.matmul(ps[32 * j:32 * j + HD + 1, self.OUT, :], V[p][0:r, kb, :],
                                                Pt[0:r, (2 * p + u) % 4, (kb % 2) * SQ:(kb % 2 + 1) * SQ],
                                                start=(q == 0), stop=False, skip_group_check=True)
                    last.then_inc(self.p_used, 2)

                def step(g, p, i, more, more2, fresh=None):
                    pieces = [(g + 1, 1 - p, k, i + p) for k in range(LEAD, NP)] if more else []
                    pieces += [(g + 2, p, k, i + 1) for k in range(LEAD)] if more2 else []

                    def some(n):
                        for _ in range(min(n, len(pieces))):
                            piece(*pieces.pop(0))
                    if fresh is not None:
                        pe.wait_ge(self.rows_copied, g + 1)
                        turn_mask(g, 0)
                    for u in range(0, NU, 2):
                        if fresh is not None:
                            turn_mask(g, u + 1)
                        scores(g, p, u, i, fresh)
                        some(1)
                        if fresh is not None and u + 2 < NU:
                            turn_mask(g, u + 2)
                        scores(g, p, u + 1, i, fresh)
                        some(1)
                        if u == NU - 2 and more:
                            some(len(pieces) - (LEAD if more2 else 0))
                            rows(g + 1, 1 - p)
                        if u:
                            values(g, p, u // 2 - 1)
                        some(2)
                    some(len(pieces))
                    values(g, p, NU // 2 - 1)

                for k in range(NP):
                    piece(g0, 0, k, i0)
                rows(g0, 0)
                for k in range(LEAD):
                    piece(g0 + 1, 1, k, i0)
                if masks:
                    step(0, 0, 0, True, True, 0)
                    step(1, 1, 0, True, True)
                    with pe.Fori(1, turn) as i:
                        step(i * 2, 0, i, True, True)
                        step(i * 2 + 1, 1, i, True, True)
                    step(2 * turn, 0, turn, True, True, 1)
                    step(2 * turn + 1, 1, turn, True, True)
                with pe.Fori(turn + 1 if masks else 0, i1 - 1) as i:
                    step(i * 2, 0, i, True, True)
                    step(i * 2 + 1, 1, i, True, True)
                step(end - 2, 0, i1 - 1, True, False)
                step(end - 1, 1, i1 - 1, False, False)

            @block.vector
            def _(dve):
                def piece(g, p, k):
                    c, t = k // 4, k % 4
                    w = min(512, S2 - c * 512)
                    dve.wait_ge(self.piece_ready, g * NP + (2 * NP + k + 1))
                    src = ps[:, 5 + (k + p) % 3, 0:w]
                    if masks:
                        dve.sem_inc(self.piece_seen, 1)
                        ins = nc.vector.tensor_tensor_reduce(self.junk[:, (k + p) % 3, 0:w], src,
                                                             masks.by_queries[:, t, c * 512:c * 512 + w], 1.0,
                                                             MASKED, ALU.add, ALU.max, mx[p][:, t, c:c + 1])
                    else:
                        ins = nc.vector.tensor_reduce(mx[p][:, t, c:c + 1], src, AXX, ALU.max)
                    ins.then_inc(self.piece_taken, 1)

                def maximum(g, p):
                    dve.wait_ge(self.piece_taken, g * NP + (3 + NP))
                    link = Chain(dve, self.vec, g * 4 + vec0)
                    negated_max_parts(nc, link, mx[p][:, :, :], self.m[:, :], self.rest[:, :], mparts[p], self.maxes_ready)
                    dve.wait_ge(self.maxes_ready, g + 1)

                def add_mask(g, p, u):
                    dve.wait_ge(self.scores_ready, g * NU + (2 * NU + u + 1))
                    dve.wait_ge(self.p_used, g * NU + (NU + u + 1))
                    nc.vector.tensor_tensor(Pt[:, (2 * p + u) % 4, :], ps[:, 2 * (u % 2):2 * (u % 2) + 2, :].rearrange(
                        "p b c -> p (b c)"), masks.by_keys[:, 2 * u:2 * u + 2, :].rearrange("p b c -> p (b c)"),
                        ALU.add).then_inc(self.mask_added, 1)

                def step(g, p, more, more2):
                    pieces = [(g + 1, 1 - p, k) for k in range(LEAD, NP)] if more else []
                    pieces += [(g + 2, p, k) for k in range(LEAD)] if more2 else []
                    for n in range(NP):
                        if n % 4 == 1 and n // 2 + 1 in self.adds:
                            add_mask(g, p, n // 2 + 1)
                        if n < len(pieces):
                            piece(*pieces[n])
                        if more and n == NP - LEAD - 1:
                            maximum(g + 1, 1 - p)

                for k in range(NP):
                    piece(g0, 0, k)
                maximum(g0, 0)
                for k in range(LEAD):
                    piece(g0 + 1, 1, k)
                with dve.Fori(i0, i1 - 1) as i:
                    step(i * 2, 0, True, True)
                    step(i * 2 + 1, 1, True, True)
                step(end - 2, 0, True, False)
                step(end - 1, 1, False, False)

            @block.scalar
            def _(act):
                def rows(g, p):
                    act.wait_ge(self.rows_ready, g + 1)
                    nc.scalar.copy(Qb[p][96:99, :], ps[96:99, self.ROWS, :]).then_inc(self.rows_copied, 1)

                def output(g, p, n):
                    act.wait_ge(self.p_used, g * NU + (NU + 4))
                    act.wait_ge(self.o_written[p], n * 64 + 64)
                    nc.scalar.copy(O[p][:, :], ps[:, self.OUT, :]).then_inc(self.o_copied, 1)

                def take_mask(u, fresh):
                    r, n = (P, 2) if 2 * u + 2 <= NKB else (LASTK, 1)
                    act.wait_ge(masks.turned, fresh * NU + u + 1)
                    nc.scalar.copy(masks.by_keys[0:r, 2 * u:2 * u + n, :],
                                   ps[0:r, 2 * (u % 2):2 * (u % 2) + n, 0:256].bitcast(BF16)).then_inc(masks.keys_ready, 1)

                def step(g, p, i, more, fresh=None):
                    output(g, 1 - p, i)
                    if fresh is not None:
                        take_mask(0, fresh)
                    for u in range(NU):
                        r, w = (P, 2 * SQ) if 2 * u + 2 <= NKB else (LASTK, SQ)
                        if fresh is not None and u + 1 < NU:
                            take_mask(u + 1, fresh)
                        dst = Pt[0:r, (2 * p + u) % 4, 0:w]
                        if u in self.adds:
                            act.wait_ge(self.mask_added, g * len(self.adds) + (self.adds.index(u) + 1))
                            src = dst
                        else:
                            act.wait_ge(self.scores_ready, g * NU + (2 * NU + u + 1))
                            act.wait_ge(self.p_used, g * NU + (NU + u + 1))
                            src = ps[0:r, 2 * (u % 2):2 * (u % 2) + 2, :].rearrange("p b c -> p (b c)")[:, 0:w]
                        nc.scalar.activation(dst, src, ACT.Exp, scale=self.scale).then_inc(self.exp_done, 1)
                    if more:
                        rows(g + 1, 1 - p)

                rows(g0, 0)
                if masks:
                    step(0, 0, 0, True, 0)
                    step(1, 1, 0, True)
                    with act.Fori(1, turn) as i:
                        step(i * 2, 0, i, True)
                        step(i * 2 + 1, 1, i, True)
                    step(2 * turn, 0, turn, True, 1)
                    step(2 * turn + 1, 1, turn, True)
                with act.Fori(turn + 1 if masks else 0, i1 - 1) as i:
                    step(i * 2, 0, i, True)
                    step(i * 2 + 1, 1, i, True)
                step(end - 2, 0, i1 - 1, True)
                step(end - 1, 1, i1 - 1, False)
                output(2 * H, 1, H)


def sparse_tables(maskq, maskk, maskg):
    fills = []
    for n in range(4):
        work = [("mask", None, maskq[n > 0], 0, 512)]
        for s in range(2):
            t = 2 * n + s
            k0 = max(0, (t - 1) * P)
            w = (t + 1) * P - k0
            work.append(("qk", t, (lambda k0, w: lambda K: K[:, k0:k0 + w])(k0, w), s * 256 + 256 - w, w))
        fills.append((work, [(0, 512, 2, (2 * n, 0))]))
    globs = lambda K: K.rearrange("p (j c) -> p j c", c=64)[:, :, 0]
    work = [("mask", None, maskg[0], 0, T * 16)]
    work += [("qk", t, globs, 16 * t, 16) for t in range(T)]
    fills.append((work, [(0, T * 16, T, (0, 1))]))
    tiles = []
    for n in range(2):
        scores = [("mask", None, maskk, 0, 512), ("mask", None, maskk, 512, 512)]
        values = []
        for s in range(4):
            kb = 4 * n + s
            w = min(256, S - kb * P)
            scores.append(("qk", (lambda kb: lambda K: K[:, kb * P:(kb + 1) * P])(kb), kb * P, s * 256, w))
            values += [(s * 256 + P * j, P, kb, j, (kb + j) * P) for j in range(2) if (kb + j) < T]
        tiles.append({"scores": scores, "values": values, "rows": P, "width": S})
    tiles.append({"scores": [("mask", None, maskg[1][:, 0:512], 0, 512), ("mask", None, maskg[1][:, 512:S], 512, 512),
                             ("qk", globs, 0, 0, 512), ("qk", globs, 512, 512, 512)],
                  "values": [(0, 512, None, 2, 0), (512, 512, None, 2, 512)], "rows": 16, "width": S})
    return fills, tiles


def causal_tables(maskq, maskk):
    fills = []
    for parts in (((7, 0, 512),), ((7, 512, 512),), ((6, 0, 512),), ((6, 512, 384), (0, 0, 128)), ((5, 0, 512),),
                  ((5, 512, 256), (1, 0, 256)), ((4, 0, 512),), ((4, 512, 128), (2, 0, 384)), ((3, 0, 512),)):
        col, work, reds, masks = 0, [], [], []
        for t, k0, w in parts:
            work.append(("qk", t, (lambda k0, w: lambda K: K[:, k0:k0 + w])(k0, w), col, w))
            if k0 + w == (t + 1) * P:
                masks.append(("mask", None, maskq, col + w - P, P))
            reds.append((col, w, 1, (t, k0 // 512)))
            col += w
        fills.append((work + masks, reds))
    tiles = []
    for parts in (((0, 0, 1024),), ((1, 128, 896), (7, 896, 128)), ((2, 256, 768), (6, 768, 256)),
                  ((3, 384, 640), (5, 640, 384)), ((4, 512, 512),)):
        col, scores, values, masks = 0, [], [], []
        for kb, q0, w in parts:
            masks.append(("mask", None, maskk, col, P))
            done = 0
            while done < w:
                n = min(w - done, 512 - (col + done) % 512, 512 - (q0 + done) % 512)
                scores.append(("qk", (lambda kb: lambda K: K[:, kb * P:(kb + 1) * P])(kb), q0 + done, col + done, n))
                values.append((col + done, n, kb, kb % 4, q0 + done))
                done += n
            col += w
        tiles.append({"scores": scores + masks, "values": values, "rows": P, "width": col})
    return fills, tiles


def build(nc, a, out):
    ctx = ExitStack()
    with ctx:
        core = Core(nc, ctx)
        X, ps = core.X, core.ps
        start_block(core, a["x"], a["c_ident"])
        ln = LayerNorm(core, ctx)
        turner = Turner(core)
        comb = Combiner(core)
        splitter = Splitter(core)

        def dram(name, shape, dt):
            return nc.dram_tensor(name, shape, dt, kind="Internal").ap()

        def rows_of(scratch, r):
            return scratch.rearrange("h (d r) c -> (h d) r c", r=6)[:, r, :]

        def dst6(scratch, side, c0=0, c1=None):
            return [(rows_of(scratch, r)[:, c0:c1], pair[side]) for r, pair in enumerate(PAIRS)]

        def dst3(scratch, c0, c1):
            return [(scratch[part, :, c0:c1], part) for part in range(3)]

        def combine(O_dram, W, bias_rows, cross, nparts, c):
            Osum = core.sb(c, "Osum", [P, nparts, S], F32)
            sums = core.sb(c, "sums", [P, nparts, P], F32)
            tmp = core.sb(c, "Ytmp", [P, S], F32)
            s_srcs = []
            if cross:
                outputs = [[O_dram[3 + half * H:3 + (half + 1) * H, j, 0:HD, :] for j in range(nparts)] for half in range(2)]
                for t in range(T):
                    half, q = t // 4, (t % 4) * P
                    s_srcs.append(((H * t, H * t + H), O_dram[3 + half * H:3 + (half + 1) * H, 0:nparts, HD, q:q + P]))
            else:
                outputs = [[O_dram[:, j, 0:HD, half * 512:(half + 1) * 512] for j in range(nparts)] for half in range(2)]
                for t in range(T):
                    s_srcs.append(((H * t, H * t + H), O_dram[:, 0:nparts, HD, t * P:(t + 1) * P]))
            comb.block(Osum, sums, tmp, outputs, s_srcs, W, bias_rows)

        O_self = dram("O_self", (H, 4, HD + 1, S), F32)
        O_cross = dram("O_cross", (3 + 2 * H, 4, HD + 1, 512), F32)
        Qs = dram("Qs", (H, 48, S), BF16)
        Ks = dram("Ks", (H, 48, S), BF16)
        Ks0 = dram("Ks0", (3, P, S2), BF16)
        Ks1 = dram("Ks1", (3, P, S2), BF16)
        dstQ = [(Qs[:, HD * r:HD * (r + 1), :], pair[0]) for r, pair in enumerate(PAIRS)]
        key_bias = dram("key_bias", (1, S2), BF16)
        narrow_mask = dram("narrow_mask", (32 + S, S2), BF16)

        with ExitStack() as c:
            hT, xn = core.sb(c, "hT", [P, S], F32), core.sb(c, "xn", [P, T, D], F32)
            Wqkv, Wproj = core.sb(c, "Wqkv", [D, 3 * D], F32), core.sb(c, "Wproj", [D, D], F32)
            tables = core.sb(c, "tables", [P, 2688], BF16)
            mq = tables[:, 0:1024].rearrange("p (n c) -> p n c", n=2)
            mk, mgq, mgk = tables[:, 1024:1536], tables[:, 1536:1664], tables[:, 1664:2688]
            Vaug = core.sb(c, "Vaug", [P, H, T, HD + 1], F32)
            tables32 = core.sb(c, "tables32", [P, 2688], F32)
            Vglob = core.sb(c, "Vglob", [16, H, HD + 1], F32)
            ln.block(hT, xn, [(Wqkv[:, :], a["L0_attn_Wqkv"]), (Wproj[:, :], a["L0_attn_Wproj"]),
                              (tables32[:, 0:2688], a["c_sparse"])])
            narrow(core, tables[:, :], tables32[:, 0:2688])
            with ExitStack() as c2:
                sp3 = splitter.buffers(c2)
                sp3.block([(S, project(core, Wqkv[:, 0:D], hT), None, None, dst6(Qs, 0)),
                           (S, project(core, Wqkv[:, D:2 * D], hT), None, None, dst6(Ks, 1))])
                values_block(core, "v0", Vaug, [(P, hT[:, t * P:(t + 1) * P], Wqkv[:, 2 * D:]) for t in range(T)], sp3)
            glob_loaded = core.sem("glob_loaded")
            with nc.Block() as block:
                @block.sync
                def _(sp):
                    for j in range(16):
                        sp.dma_start(Vglob[j:j + 1, :, :],
                                     Vaug[64 * (j % 2):64 * (j % 2) + 1, :, j // 2, :]).then_inc(glob_loaded, 16)
                    sp.wait_ge(glob_loaded, 16 * 16)
            fills, tiles = sparse_tables([mq[:, 0, :], mq[:, 1, :]], mk, (mgq, mgk))
            with ExitStack() as c2, core.stage():
                att = SelfAttention(core, "a0_", 1, fills, tiles, 2, 0)
                head = lambda scr: lambda g: scr[bass.ds(g, 1)].rearrange("a r c -> (a r) c")
                one = lambda scr: [((0, 48), (lambda g: scr[bass.ds(g, 1)].rearrange("a r (n c) -> (a r) n c", n=1)))]
                att.run(c2, {"q": one(Qs), "k": one(Ks)}, Vaug, Vglob, HD ** -0.5, O_self)
            with ExitStack() as c2:
                combine(O_self, Wproj[:, :], None, False, 3, c2)

        def cross_values(name, Vaug, ctxT, W, bias_rows):
            values_block(core, name, Vaug, [(min(P, S2 - t * P), ctxT[:, t * P:min(S2, (t + 1) * P)], W)
                                            for t in range(NKB)], splitter, bias_rows)

        def context_items(ctx_tok, ctxT_dst, dst):
            items = []
            for n in range(-(-S2 // S)):
                w = min(S, S2 - n * S)

                def matmuls(pe, A, B, n=n, w=w):
                    for t in range(-(-w // P)):
                        r = min(P, w - t * P)
                        last = nc.tensor.transpose(A[:, t * P:t * P + r], ctx_tok[0:r, n * T + t, :], core.ident[0:r, 0:r])
                    return last
                items.append((w, matmuls, None, None, dst3(dst, n * S, n * S + w)))
            return items

        def load_context(ctx_tok):
            src = a["ctx_1024"]
            full = (NKB - 1) * P
            return [(ctx_tok[:, 0:NKB - 1, :], src[0, 0:full, :].rearrange("(t p) d -> p t d", p=P)),
                    (ctx_tok[0:LASTK, NKB - 1, :], src[0, full:S2, :])]

        def rows_load(c, name, src):
            t = core.sb(c, name, [P, src.shape[-1]], F32)
            return t, (t[:, :], src.partition_broadcast(P) if len(src.shape) == 1 else src)

        with ExitStack() as c:
            Wo0, Wo0T = core.sb(c, "Wo0", [D, D], F32), core.sb(c, "Wo0T", [D, D], F32)
            bo0, bo0_load = rows_load(c, "bo0", a["L0_xattn_b_out"])
            Vaug = core.sb(c, "Vaugx", [P, H, NKB, HD + 1], F32)
            with ExitStack() as c2:
                hT, xn = core.sb(c2, "hT", [P, S], F32), core.sb(c2, "xn", [P, T, D], F32)
                ctx_tok = core.sb(c2, "ctx_tok", [P, NKB, D], F32)
                mrow = core.sb(c2, "mrow", [4, S2 // 4], I32)
                brow = core.sb(c2, "brow", [4, S2 // 4], BF16)
                ln.block(hT, xn, load_context(ctx_tok) + [
                    (Wo0[:, :], a["L0_xattn_W_out"]), bo0_load,
                    (mrow[:, :], a["mask_Bx1x1xS2_if1"].rearrange("a b c (p n) -> (a b c p) n", p=4))])
                turner.block([(Wo0[:, :], Wo0T[:, :])])
                sp3 = splitter.buffers(c2)
                items = context_items(ctx_tok, None, Ks0)
                items.append((S, (lambda pe, A, B: [nc.tensor.matmul(A[:, k * 512:(k + 1) * 512], core.ident[:, :],
                                                                    hT[:, k * 512:(k + 1) * 512], start=True, stop=True)
                                                    for k in range(2)][-1]), None, None, dstQ))
                vx_ones, vx_done, kb_ready, kb_stored = (core.sem("vx_ones"), core.sem("vx_done"),
                                                         core.sem("kb_ready"), core.sem("kb_stored"))

                def values_beside(pool):
                    nc.gpsimd.tensor_scalar(brow[:, :], mrow[:, :], 0.0, MASKED, ALU.is_equal, ALU.mult).then_inc(kb_ready, 1)
                    nc.gpsimd.memset(Vaug[:, :, NKB - 1, :], 0.0).then_inc(vx_ones, 1)
                    pool.wait_ge(kb_ready, 1)
                    pool.wait_ge(vx_ones, 1)
                    for h in range(H):
                        nc.gpsimd.memset(Vaug[:, h, :, HD:HD + 1], 1.0).then_inc(vx_ones, 1)
                    pool.wait_ge(vx_ones, 1 + H)
                    for h in range(H):
                        nc.gpsimd.tensor_copy(Vaug[:, h, 0:NKB - 1, 0:HD],
                                              ctx_tok[:, 0:NKB - 1, h * HD:(h + 1) * HD]).then_inc(vx_done, 1)
                    nc.gpsimd.tensor_copy(Vaug[0:LASTK, :, NKB - 1, 0:HD], ctx_tok[0:LASTK, NKB - 1, :].rearrange(
                        "p (h d) -> p h d", h=H)).then_inc(vx_done, 1)
                    pool.wait_ge(vx_done, H + 1)

                def bias_beside(sp):
                    sp.wait_ge(kb_ready, 1)
                    sp.dma_start(key_bias.rearrange("a (p n) -> (a p) n", p=4), brow[:, :]).then_inc(kb_stored, 16)
                    sp.wait_ge(kb_stored, 16)
                    splitter.finish(sp)
                sp3.block(items, values_beside, bias_beside)
            with ExitStack() as c2, core.stage():
                xa = CrossAttention(core, c2, "x0_", float(D) ** -0.5, False)
                narrower = MaskNarrower(core, c2, a["mask_Bx1xSxS2_ik1"], narrow_mask)
                xa.clear_block(key_bias, narrower)
                xa.block(Qs, Ks0, Vaug, O_cross, narrower=narrower)
            with ExitStack() as c2:
                combine(O_cross, Wo0T[:, :], bo0[:, :], True, 4, c2)

        moe_l0(core, ln, turner, a)
        mla(core, ln, comb, splitter, combine, a, O_self, dram)

        with ExitStack() as c:
            WoT = core.sb(c, "Wo1T", [D, D], F32)
            bo1, bo1_load = rows_load(c, "bo1", a["L1_xattn_bo"])
            Vaug = core.sb(c, "Vaugy", [P, H, NKB, HD + 1], F32)
            masks = Masks(core, c, narrow_mask)

            def load_masks(sp):
                for c in range(4):
                    masks.load_queries(sp, 0, c)
            with ExitStack() as c2:
                hT, xn = core.sb(c2, "hT", [P, S], F32), core.sb(c2, "xn", [P, T, D], F32)
                ctxT = core.sb(c2, "ctxT", [P, NKB * P], F32)
                W = core.sb(c2, "W4", [D, 4, D], F32)
                WT = core.sb(c2, "W4T", [D, 3, D], F32)
                bqk = core.sb(c2, "bqk", [2, D], F32)
                bqkT = core.sb(c2, "bqkT", [D, 2], F32)
                bv, bv_load = rows_load(c2, "bv1", a["L1_xattn_bv"])
                with ExitStack() as c3:
                    ctx_tok = core.sb(c3, "ctx_tok", [P, NKB, D], F32)
                    ln.block(hT, xn, load_context(ctx_tok) + [
                        (W[:, k, :], a[f"L1_xattn_W{n}"]) for k, n in enumerate("qkvo")] + [
                        bo1_load, bv_load, (bqk[0:1, :], a["L1_xattn_bq"].rearrange("(a d) -> a d", a=1)),
                        (bqk[1:2, :], a["L1_xattn_bk"].rearrange("(a d) -> a d", a=1))], load_masks)
                    turner.block([(W[:, k, :], WT[:, k, :]) for k in range(3)] + [(W[:, 3, :], WoT[:, :]),
                                 (bqk[:, :], bqkT[:, :])] +
                                 [([ctx_tok[0:min(P, S2 - t * P), t, :] for t in range(t0, min(NKB, t0 + 4))],
                                   ctxT[:, t0 * P:min(S2, (t0 + 4) * P)]) for t0 in range(0, NKB, 4)])
                with ExitStack() as c3:
                    sp3 = splitter.buffers(c3)
                    items = [(min(S, S2 - n * S), project(core, WT[:, 1, :], ctxT, min(S, S2 - n * S), n * S), bqkT[:, 1:2], None,
                              dst3(Ks1, n * S, min(S2, (n + 1) * S))) for n in range(-(-S2 // S))]
                    items.append((S, project(core, WT[:, 0, :], hT), bqkT[:, 0:1], None, dstQ))
                    sp3.block(items)
                    cross_values("vy", Vaug, ctxT, WT[:, 2, :], bv[:, :])
            with ExitStack() as c2, core.stage():
                xa = CrossAttention(core, c2, "x1_", float(HD) ** -0.5, True)
                masks.place_keys(c2)
                xa.clear_block(None, masks=masks)
                xa.block(Qs, Ks1, Vaug, O_cross, masks=masks)
            with ExitStack() as c2:
                combine(O_cross, WoT[:, :], bo1[:, :], True, 4, c2)

        encoder(core, ln, turner, a, out)


class MaskNarrower:

    W = S2 // 4

    def __init__(self, core, ctx, mask, narrow_dram):
        self.core = core
        self.src = mask[0, 0].rearrange("(g q) (n c) -> g (q n) c", g=2 * H, c=self.W)
        self.dst = narrow_dram.rearrange("(g q) (n c) -> g (q n) c", g=2 * H + 1, c=self.W)
        self.wide = [core.sb(ctx, f"mask_wide{p}", [P, self.W], I32) for p in range(2)]
        self.made = [core.sb(ctx, f"mask_made{p}", [P, self.W], BF16) for p in range(2)]
        self.loaded = [core.sem(f"mask_loaded{p}") for p in range(2)]
        self.stored = [core.sem(f"mask_stored{p}") for p in range(2)]
        self.done, self.seen, self.pool_seen = core.sem("mask_done"), core.sem("mask_seen"), core.sem("mask_pool_seen")

    def clear(self, pool):
        self.core.nc.gpsimd.memset(self.made[1][:, :], 0.0).then_inc(self.done, 2)
        pool.wait_ge(self.done, 2)
        pool.sem_inc(self.stored[0], 16)

    def transfers(self, sp, g, p):
        src = self.src[bass.ds(g, 1)].rearrange("g p c -> (g p) c")
        sp.wait_ge(self.done, g + 1)
        sp.sem_inc(self.seen, 1)
        sp.dma_start(self.wide[p][:, :], src).then_inc(self.loaded[p], 16)
        self.store(sp, g, p)

    def store(self, sp, g, p):
        dst = self.dst[bass.ds(g, 1)].rearrange("g p c -> (g p) c")
        sp.wait_ge(self.done, g + 2)
        sp.sem_inc(self.seen, 1)
        sp.dma_start(dst, self.made[1 - p][:, :]).then_inc(self.stored[1 - p], 16)

    def convert(self, pool, g, p, i):
        pool.wait_ge(self.loaded[p], i * 16 + 16)
        pool.wait_ge(self.stored[p], i * 16 + 16)
        pool.sem_inc(self.pool_seen, 1)
        self.core.nc.gpsimd.tensor_scalar(self.made[p][:, :], self.wide[p][:, :], 1.0, MASKED,
                                          ALU.is_equal, ALU.mult).then_inc(self.done, 1)

    def finish(self, sp):
        self.store(sp, 2 * H, 0)
        sp.wait_ge(self.stored[0], 16 * (H + 1))
        sp.wait_ge(self.stored[1], 16 * (H + 1))


class Masks:

    def __init__(self, core, ctx, narrow_dram):
        self.core, self.src = core, narrow_dram[32:, :]
        self.by_queries = core.sb(ctx, "mask_by_queries", [P, 4, S2], BF16)
        self.queries_loaded, self.cleared = core.sem("mask_queries_loaded"), core.sem("mask_cleared")
        self.turned, self.keys_ready = core.sem("mask_turned"), core.sem("mask_keys_ready")

    def place_keys(self, ctx):
        self.by_keys = self.core.sb(ctx, "mask_by_keys", [P, NKB, 512], BF16)

    def clear(self, dve):
        self.core.nc.vector.memset(self.by_keys[:, NKB - 1, :], 0.0).then_inc(self.cleared, 1)
        dve.wait_ge(self.cleared, 1)

    def load_queries(self, sp, half, c):
        a, b = CrossAttention.CH[c], CrossAttention.CH[c + 1]
        sp.dma_start(self.by_queries[:, :, a:b], self.src[half * 512:(half + 1) * 512, a:b].rearrange(
            "(t p) c -> p t c", p=P)).then_inc(self.queries_loaded, 16)


def first_max_onehot(nc, link, L, m, eidx, cand, idx, onehot, want_m=True):
    if want_m:
        link(nc.vector.tensor_reduce(m, L, AXX, ALU.max))
    wide = lambda x: x.unsqueeze(2).broadcast_to((P, T, E))
    link(nc.vector.tensor_tensor(cand, L, wide(m), ALU.is_equal))
    link(nc.vector.tensor_tensor(cand, cand, eidx, ALU.mult))
    link(nc.vector.tensor_reduce(idx, cand, AXX, ALU.min))
    link(nc.vector.tensor_tensor(onehot, eidx, wide(idx), ALU.is_equal))


def moe_l0(core, ln, turner, a):
    nc, ps, X = core.nc, core.ps, core.X
    F = 256
    FC = F // P
    with ExitStack() as c:
        sb = lambda n, s, d=F32: core.sb(c, n, s, d)
        hT, xn = sb("hT", [P, S]), sb("xn", [P, T, D])
        Wg, Wu = sb("Wg", [P, E * FC, D]), sb("Wu", [P, E * FC, D])
        Wd = sb("Wd", [P, E, F])
        WgT, WuT, WdT = sb("WgT", [P, E * FC, P]), sb("WuT", [P, E * FC, P]), sb("WdT", [P, E * FC, D])
        Rw, RwT = sb("Rw", [E, D]), sb("RwT", [D, E])
        eidx = sb("eidx", [P, T, E])
        ln.block(hT, xn, [(Wg[:, :, :], a["L0_ffn_w_gate"].rearrange("e (c p) h -> p (e c) h", p=P)),
                          (Wu[:, :, :], a["L0_ffn_w_up"].rearrange("e (c p) h -> p (e c) h", p=P)),
                          (Wd[:, :, :], a["L0_ffn_w_down"].rearrange("e h f -> h e f")),
                          (Rw[:, :], a["L0_ffn_router_w"]), (eidx[:, :, :], a["c_expert"])])
        turner.block([(Rw[:, :], RwT[:, :])] +
                     [(Wg[:, n, :], WgT[:, n, :]) for n in range(E * FC)] +
                     [(Wu[:, n, :], WuT[:, n, :]) for n in range(E * FC)] +
                     [(Wd[:, n // FC, (n % FC) * P:(n % FC + 1) * P], WdT[:, n, :]) for n in range(E * FC)])
        L, L2, cand, one1, one2 = (sb("r" + k, [P, T, E]) for k in ("L", "L2", "cand", "one1", "one2"))
        fac, keep1, e1, dense, absL = (sb("r" + k, [P, T, E]) for k in ("fac", "keep", "e1", "dense", "abs"))
        m1, m2, idx, tot = (sb("r" + k, [P, T]) for k in ("m1", "m2", "idx", "tot"))
        logits, vec, diff_ready, exp_ready, dense_ready = (core.sem("r_" + k) for k in
                                                          ("logits", "vec", "diff_ready", "exp_ready", "dense_ready"))
        wide = lambda x: x[:, :].unsqueeze(2).broadcast_to((P, T, E))
        with nc.Block() as block:
            @block.tensor
            def _(pe):
                for t in range(T):
                    last = nc.tensor.matmul(ps[:, 0, t * E:(t + 1) * E], hT[:, t * P:(t + 1) * P], RwT[:, :], start=True, stop=True)
                last.then_inc(logits, 1)

            @block.vector
            def _(dve):
                link = Chain(dve, vec)
                dve.wait_ge(logits, 1)
                link(nc.vector.tensor_copy(L[:, :, :], ps[:, 0, 0:T * E].rearrange("p (t e) -> p t e", t=T)))
                link(nc.vector.tensor_scalar(absL[:, :, :], L[:, :, :], -1.0, None, ALU.mult))
                link(nc.vector.tensor_tensor(absL[:, :, :], absL[:, :, :], L[:, :, :], ALU.max))
                for k, (src, m, one) in enumerate(((L, m1, one1), (L2, m2, one2))):
                    if k == 1:
                        link(nc.vector.scalar_tensor_tensor(L2[:, :, :], one1[:, :, :], MASKED, L[:, :, :], ALU.mult, ALU.add))
                    first_max_onehot(nc, link, src[:, :, :], m[:, :], eidx[:, :, :], cand[:, :, :], idx[:, :], one[:, :, :])
                    link(nc.vector.tensor_tensor(fac[:, :, :], absL[:, :, :], wide(m), ALU.max))
                    link(nc.vector.tensor_tensor(cand[:, :, :], wide(m), L[:, :, :], ALU.subtract))
                    link(nc.vector.scalar_tensor_tensor(keep1[:, :, :], fac[:, :, :], 0.02, cand[:, :, :], ALU.mult, ALU.is_ge))
                    nc.vector.tensor_tensor(cand[:, :, :], src[:, :, :], wide(m), ALU.subtract).then_inc(diff_ready, 1)
                    dve.wait_ge(exp_ready, k + 1)
                    link(nc.vector.tensor_tensor(e1[:, :, :], e1[:, :, :], keep1[:, :, :], ALU.mult))
                    link(nc.vector.tensor_reduce(tot[:, :], e1[:, :, :], AXX, ALU.add))
                    link(nc.vector.reciprocal(tot[:, :], tot[:, :]))
                    dst = dense if k == 0 else fac
                    link(nc.vector.tensor_tensor(dst[:, :, :], one[:, :, :], wide(tot), ALU.mult))
                nc.vector.tensor_tensor(dense[:, :, :], dense[:, :, :], fac[:, :, :], ALU.add).then_inc(dense_ready, 1)
                dve.wait_ge(dense_ready, 1)

            @block.scalar
            def _(act):
                for k in range(2):
                    act.wait_ge(diff_ready, k + 1)
                    nc.scalar.activation(e1[:, :, :], cand[:, :, :], ACT.Exp).then_inc(exp_ready, 1)

        gate, hid = sb("gate", [P, 2, 512]), sb("hid", [P, 2, FC, S])
        up_ready, gate_done, hid_ready, down_ready, hid_used, added = (core.sem("f0_" + k) for k in (
            "up_ready", "gate_done", "hid_ready", "down_ready", "hid_used", "added"))
        with nc.Block() as block:
            @block.tensor
            def _(pe):
                def down(e):
                    pe.wait_ge(hid_ready, 4 * (e + 1))
                    for t in range(T):
                        n = e * T + t
                        if n >= 4:
                            pe.wait_ge(added, n - 3)
                        for k in range(FC):
                            last = nc.tensor.matmul(ps[:, 4 + n % 4, 0:D], hid[:, e % 2, k, t * P:(t + 1) * P],
                                                    WdT[:, e * FC + k, :], start=(k == 0), stop=(k == FC - 1))
                        last.then_inc(down_ready, 1)
                    
                for e in range(E):
                    for k in range(FC):
                        for b in range(2):
                            n = (e * FC + k) * 2 + b
                            if n >= 2:
                                pe.wait_ge(hid_ready, n - 1)
                            rhs = hT[:, b * 512:(b + 1) * 512]
                            nc.tensor.matmul(ps[:, 2 * (n % 2), :], WgT[:, e * FC + k, :], rhs, start=True, stop=True)
                            nc.tensor.matmul(ps[:, 2 * (n % 2) + 1, :], WuT[:, e * FC + k, :], rhs, start=True,
                                             stop=True).then_inc(up_ready, 1)
                    if e:
                        down(e - 1)
                down(E - 1)

            @block.scalar
            def _(act):
                for n in range(E * FC * 2):
                    act.wait_ge(up_ready, n + 1)
                    if n >= 2:
                        act.wait_ge(hid_ready, n - 1)
                    nc.scalar.activation(gate[:, n % 2, :], ps[:, 2 * (n % 2), :], ACT.Silu).then_inc(gate_done, 1)

            @block.vector
            def _(dve):
                def add(e):
                    for t in range(T):
                        n = e * T + t
                        dve.wait_ge(down_ready, n + 1)
                        if e:
                            dve.wait_ge(added, n - T + 1)
                        nc.vector.scalar_tensor_tensor(X[:, t, :], ps[:, 4 + n % 4, 0:D], dense[:, t, e:e + 1], X[:, t, :],
                                                       ALU.mult, ALU.add).then_inc(added, 1)
                for e in range(E):
                    for k in range(FC):
                        for b in range(2):
                            n = (e * FC + k) * 2 + b
                            dve.wait_ge(gate_done, n + 1)
                            if e >= 2:
                                dve.wait_ge(down_ready, T * (e - 1))
                            nc.vector.tensor_tensor(hid[:, e % 2, k, b * 512:(b + 1) * 512], ps[:, 2 * (n % 2) + 1, :],
                                                    gate[:, n % 2, :], ALU.mult).then_inc(hid_ready, 1)
                    if e:
                        add(e - 1)
                add(E - 1)
                dve.wait_ge(added, E * T)


def mla(core, ln, comb, splitter, combine, a, O_self, dram):
    nc, ps = core.nc, core.ps
    KV, QR, RD = 32, 64, 32
    Qc, Kc = dram("Qc", (H, 2, HD * 3, S), BF16), dram("Kc", (H, 2, HD * 3, S), BF16)
    Qr, Kr = dram("Qr", (H, 2, RD * 3, S), BF16), dram("Kr", (H, 2, RD * 3, S), BF16)
    with ExitStack() as c:
        sb = lambda n, s, d=F32: core.sb(c, n, s, d)
        Wo = sb("Wo_m", [D, D])
        tables, tables32 = sb("tables", [P, 2 * P], BF16), sb("tables32", [P, 2 * P])
        mq, mk = tables[:, 0:P], tables[:, P:2 * P]
        Vaug = sb("Vaugm", [P, H, T, HD + 1])
        with ExitStack() as c2:
            sb2 = lambda n, s, d=F32: core.sb(c2, n, s, d)
            hT, xn = sb2("hT", [P, S]), sb2("xn", [P, T, D])
            Wkv, Wq = sb2("Wkv", [D, KV]), sb2("Wq_m", [D, QR])
            Wkd, Wvd, Wqd = sb2("Wkd", [KV, D]), sb2("Wvd", [KV, D]), sb2("Wqd", [QR, D])
            Wkr, Wqr = sb2("Wkr", [D, H * RD]), sb2("Wqr", [QR, H * RD])
            Wkt, Wqt = sb2("Wkt", [D, H * RD]), sb2("Wqt", [QR, H * RD])
            cos, sin = sb2("cos", [P, S]), sb2("sin", [P, S])
            gkv = sb2("gkv", [P, KV])
            kvc, sq = sb2("kvc", [P, T, KV]), sb2("sq", [P, T, KV])
            ms, rs = sb2("ms", [P, T]), sb2("rs", [P, T])
            kvT, qcT = sb2("kvT", [KV, S]), sb2("qcT", [QR, S])
            ln.block(hT, xn, [(Wkv[:, :], a["L1_attn_W_kv"]), (Wq[:, :], a["L1_attn_W_q"]), (Wkd[:, :], a["L1_attn_W_kdec"]),
                              (Wvd[:, :], a["L1_attn_W_vdec"]), (Wqd[:, :], a["L1_attn_W_qdec"]),
                              (Wkr[:, :], a["L1_attn_W_krope"]), (Wqr[:, :], a["L1_attn_W_qrope"]),
                              (Wo[:, :], a["L1_attn_W_o"]), (cos[:, :], a["c_cos"]), (sin[:, :], a["c_sin"]),
                              (gkv[:, :], a["L1_attn_g_kv"].partition_broadcast(P)),
                              (tables32[:, :], a["c_causal"])])
            narrow(core, tables[:, :], tables32[:, :])
            kv_ready, q_ready, vec, ms_ready, rt_ready, kvn_ready, turned, took = (core.sem("m_" + k) for k in (
                "kv_ready", "q_ready", "vec", "ms_ready", "rt_ready", "kvn_ready", "turned", "took"))
            with nc.Block() as block:
                @block.tensor
                def _(pe):
                    for t in range(T):
                        last = nc.tensor.matmul(ps[:, 0, t * KV:(t + 1) * KV], hT[:, t * P:(t + 1) * P], Wkv[:, :], start=True, stop=True)
                    last.then_inc(kv_ready, 1)
                    for b in range(2):
                        last = nc.tensor.matmul(ps[0:QR, 1 + b, :], Wq[:, :], hT[:, b * 512:(b + 1) * 512], start=True, stop=True)
                    last.then_inc(q_ready, 1)
                    pe.wait_ge(kvn_ready, 1)
                    for t in range(T):
                        last = nc.tensor.transpose(ps[0:KV, 3 + t // 4, (t % 4) * P:(t % 4 + 1) * P], kvc[:, t, :], core.ident[:, :])
                    last.then_inc(turned, 1)

                @block.vector
                def _(dve):
                    link = Chain(dve, vec)
                    for w, wt, r in ((Wkr, Wkt, D), (Wqr, Wqt, QR)):
                        v = w[0:r, :].rearrange("p (h a d) -> p h a d", h=H, a=2)
                        vt = wt[0:r, :].rearrange("p (h a d) -> p h a d", h=H, a=2)
                        link(nc.vector.tensor_scalar(vt[:, :, 0, :], v[:, :, 1, :], -1.0, None, ALU.mult))
                        link(nc.vector.tensor_copy(vt[:, :, 1, :], v[:, :, 0, :]))
                    dve.wait_ge(kv_ready, 1)
                    link(nc.vector.tensor_copy(kvc[:, :, :], ps[:, 0, 0:T * KV].rearrange("p (t k) -> p t k", t=T)))
                    link(nc.vector.tensor_tensor(sq[:, :, :], kvc[:, :, :], kvc[:, :, :], ALU.mult))
                    link(nc.vector.tensor_reduce(ms[:, :], sq[:, :, :], AXX, ALU.add))
                    nc.vector.tensor_scalar(ms[:, :], ms[:, :], 1.0 / KV, 1e-6, ALU.mult, ALU.add).then_inc(ms_ready, 1)
                    dve.wait_ge(rt_ready, 1)
                    link(nc.vector.reciprocal(rs[:, :], ms[:, :]))
                    link(nc.vector.tensor_tensor(kvc[:, :, :], kvc[:, :, :], rs[:, :].unsqueeze(2).broadcast_to((P, T, KV)), ALU.mult))
                    nc.vector.tensor_tensor(kvc[:, :, :], kvc[:, :, :], gkv[:, :].unsqueeze(1).broadcast_to((P, T, KV)),
                                            ALU.mult).then_inc(kvn_ready, 1)
                    dve.wait_ge(kvn_ready, 1)

                @block.scalar
                def _(act):
                    act.wait_ge(q_ready, 1)
                    nc.scalar.copy(qcT[:, :], ps[0:QR, 1:3, :].rearrange("p b c -> p (b c)")).then_inc(took, 1)
                    act.wait_ge(ms_ready, 1)
                    nc.scalar.activation(ms[:, :], ms[:, :], ACT.Sqrt).then_inc(rt_ready, 1)
                    act.wait_ge(turned, 1)
                    nc.scalar.copy(kvT[:, :], ps[0:KV, 3:5, :].rearrange("p b c -> p (b c)")).then_inc(took, 1)
                    act.wait_ge(took, 2)

            def dsts(scr, side, g0, n):
                out = []
                for ch in range(2):
                    for r in range(3):
                        v = scr[g0:g0 + n, ch].rearrange("h (d r) c -> h d r c", r=3)[:, :, r, :]
                        out.append((v, CHUNK_PAIRS[ch][r][side]))
                return out

            sp3 = splitter.buffers(c2)
            items = [(S, project(core, Wqd[:, :], qcT), None, None, dsts(Qc, 0, 0, H)),
                     (S, project(core, Wkd[:, :], kvT), None, None, dsts(Kc, 1, 0, H))]
            for n in range(4):
                cols = slice(n * P, (n + 1) * P)
                items.append((S, project_two(core, Wqr[:, cols], Wqt[:, cols], qcT), None, (cos[:, :], sin[:, :]), dsts(Qr, 0, 4 * n, 4)))
                items.append((S, project_two(core, Wkr[:, cols], Wkt[:, cols], hT), None, (cos[:, :], sin[:, :]), dsts(Kr, 1, 4 * n, 4)))
            sp3.block(items)
            values_block(core, "vm", Vaug, [(P, kvT[:, t * P:(t + 1) * P], Wvd[:, :]) for t in range(T)], sp3)
        with ExitStack() as c2, core.stage():
            fills, tiles = causal_tables(mq, mk)
            att = SelfAttention(core, "a1_", 2, fills, tiles, 2, 2)

            def srcs(content, rope):
                rope_rows = lambda lo, hi: lambda g: rope[bass.ds(g, 1), :, lo:hi, :].rearrange("a n r c -> (a r) n c")
                return [((0, 96), rope_rows(0, 96)),
                        ((99, 123), lambda g: content[bass.ds(g, 1)].rearrange("a n r c -> (a r) n c"))]
            att.run(c2, {"q": srcs(Qc, Qr), "k": srcs(Kc, Kr)}, Vaug, None, float(HD + RD) ** -0.5, O_self)
        with ExitStack() as c2:
            combine(O_self, Wo[:, :], None, False, 4, c2)


def encoder(core, ln, turner, a, out):
    nc, ps, X = core.nc, core.ps, core.X
    DF = 512
    C = DF // P
    with ExitStack() as c:
        sb = lambda n, s, d=F32: core.sb(c, n, s, d)
        hT, xn = sb("hT", [P, S]), sb("xn", [P, T, D])
        W1, W2 = sb("W1", [P, E, DF]), sb("W2", [P, E * C, D])
        b1, b1T = sb("b1", [E * C, P]), sb("b1T", [P, E * C])
        b2 = sb("b2", [P, E * D])
        Wv, Wo, WvT, WoT = sb("Wv_e", [D, D]), sb("Wo_e", [D, D]), sb("WvT_e", [D, D]), sb("WoT_e", [D, D])
        bv, bvT = sb("bv_e", [1, D]), sb("bvT_e", [D, 1])
        Wg, WgT = sb("Wg_e", [E, D]), sb("WgT_e", [D, E])
        e0 = sb("e0", [P, P])
        rows = {k: sb("row_" + k, [P, D]) for k in ("bo", "g1", "be1", "g2", "be2")}
        eidx = sb("eidx", [P, T, E])
        b2_zero, b2_loaded = core.sem("b2_zero"), core.sem("b2_loaded")
        ln.block(hT, xn, [(W1[:, :, :], a["L1_ffn_W1"].rearrange("e d f -> d e f")),
                          (W2[:, :, :], a["L1_ffn_W2"].rearrange("e (c p) d -> p (e c) d", p=P)),
                          (b1[:, :], a["L1_ffn_b1"].rearrange("e (c p) -> (e c) p", p=P)),
                          (Wv[:, :], a["L1_ffn_Wqkv"][2 * D:3 * D, :]), (Wo[:, :], a["L1_ffn_Wo"]),
                          (bv[:, :], a["L1_ffn_bqkv"][2 * D:3 * D].rearrange("(a d) -> a d", a=1)),
                          (Wg[:, :], a["L1_ffn_Wg"]), (eidx[:, :, :], a["c_expert"])] +
                 [(t[:, :], a["L1_ffn_" + k].partition_broadcast(P)) for k, t in rows.items()])
        with nc.Block() as block:
            @block.gpsimd
            def _(pool):
                nc.gpsimd.memset(b2[:, :], 0.0).then_inc(b2_zero, 1)
                nc.gpsimd.memset(e0[:, :], 0.0).then_inc(b2_zero, 1)
                pool.wait_ge(b2_zero, 2)
                nc.gpsimd.memset(e0[0:1, :], 1.0).then_inc(b2_zero, 1)
                pool.wait_ge(b2_zero, 3)

            @block.sync
            def _(sp):
                sp.wait_ge(b2_zero, 3)
                sp.dma_start(b2[0:1, :], a["L1_ffn_b2"].rearrange("(a e) d -> a (e d)", a=1)).then_inc(b2_loaded, 16)
                sp.wait_ge(b2_loaded, 16)
        turner.block([(b1[:, :], b1T[:, :]), (Wv[:, :], WvT[:, :]), (Wo[:, :], WoT[:, :]), (bv[:, :], bvT[:, :]),
                      (Wg[:, :], WgT[:, :])])

        vT, y, L, cand, one = sb("vT_e", [P, S]), sb("y", [P, T, D]), sb("gL", [P, T, E]), sb("gcand", [P, T, E]), sb("gone", [P, T, E])
        m, idx, yT = sb("gm", [P, T]), sb("gidx", [P, T]), sb("yT", [P, S])
        v_ready, v_taken, o_ready, vec, y_ready, y_turned, y_taken, logits = (core.sem("e_" + k) for k in (
            "v_ready", "v_taken", "o_ready", "vec", "y_ready", "y_turned", "y_taken", "logits"))
        call = ln.calls
        ln.calls += 1
        with nc.Block() as block:
            @block.tensor
            def _(pe):
                for b in range(2):
                    nc.tensor.matmul(ps[:, b, :], WvT[:, :], hT[:, b * 512:(b + 1) * 512], start=True, stop=True).then_inc(v_ready, 1)
                pe.wait_ge(v_taken, 2)
                for t in range(T):
                    nc.tensor.matmul(ps[:, 2 + t // 2, (t % 2) * D:(t % 2 + 1) * D], vT[:, t * P:(t + 1) * P], WoT[:, :],
                                     start=True, stop=True).then_inc(o_ready, 1)
                pe.wait_ge(y_ready, 1)
                for t in range(T):
                    nc.tensor.transpose(ps[:, 6 + t // 4, (t % 4) * P:(t % 4 + 1) * P], y[:, t, :], core.ident[:, :]).then_inc(y_turned, 1)
                pe.wait_ge(y_taken, 2)
                for t in range(T):
                    last = nc.tensor.matmul(ps[:, 0, t * E:(t + 1) * E], yT[:, t * P:(t + 1) * P], WgT[:, :], start=True, stop=True)
                last.then_inc(logits, 1)

            @block.scalar
            def _(act):
                for b in range(2):
                    act.wait_ge(v_ready, b + 1)
                    nc.scalar.activation(vT[:, b * 512:(b + 1) * 512], ps[:, b, :], ACT.Identity, bias=bvT[:, 0:1]).then_inc(v_taken, 1)
                ln.root(act, call)
                for b in range(2):
                    act.wait_ge(y_turned, 4 * b + 4)
                    nc.scalar.copy(yT[:, b * 512:(b + 1) * 512], ps[:, 6 + b, :]).then_inc(y_taken, 1)

            @block.vector
            def _(dve):
                link = Chain(dve, vec)
                wide = lambda r: r[:, :].unsqueeze(1).broadcast_to((P, T, D))
                link(nc.vector.tensor_tensor(xn[:, :, :], xn[:, :, :], wide(rows["bo"]), ALU.add))
                dve.wait_ge(o_ready, T)
                for b in range(4):
                    link(nc.vector.tensor_tensor(xn[:, 2 * b:2 * b + 2, :], xn[:, 2 * b:2 * b + 2, :],
                                                 ps[:, 2 + b, 0:2 * D].rearrange("p (t d) -> p t d", t=2), ALU.add))
                lk = Chain(dve, ln.dve_done, ln.chain_n)
                ln.normalise(dve, lk, xn, y, call)
                ln.chain_n = lk.n
                link(nc.vector.tensor_tensor(y[:, :, :], y[:, :, :], wide(rows["g1"]), ALU.mult))
                nc.vector.tensor_tensor(y[:, :, :], y[:, :, :], wide(rows["be1"]), ALU.add).then_inc(y_ready, 1)
                dve.wait_ge(y_ready, 1)
                dve.wait_ge(logits, 1)
                link(nc.vector.tensor_copy(L[:, :, :], ps[:, 0, 0:T * E].rearrange("p (t e) -> p t e", t=T)))
                first_max_onehot(nc, link, L[:, :, :], m[:, :], eidx[:, :, :], cand[:, :, :], idx[:, :], one[:, :, :])

        hid = sb("hid_e", [P, 2, C, S])
        h_ready, h_done, d_ready, added = (core.sem("e2_" + k) for k in ("h_ready", "h_done", "d_ready", "added"))
        call2 = ln.calls
        ln.calls += 1
        z = xn
        stored = core.sem("stored")
        final = core.sem("final")
        with nc.Block() as block:
            @block.tensor
            def _(pe):
                def down(e):
                    pe.wait_ge(h_done, 2 * C * (e + 1))
                    for t in range(T):
                        n = e * T + t
                        if n >= 4:
                            pe.wait_ge(added, n - 3)
                        dst = ps[:, 4 + n % 4, 0:D]
                        nc.tensor.matmul(dst, e0[:, :], b2[:, e * D:(e + 1) * D], start=True, stop=False)
                        for k in range(C):
                            last = nc.tensor.matmul(dst, hid[:, e % 2, k, t * P:(t + 1) * P], W2[:, e * C + k, :], start=False,
                                                    stop=(k == C - 1))
                        last.then_inc(d_ready, 1)
                for e in range(E):
                    for k in range(C):
                        for b in range(2):
                            n = (e * C + k) * 2 + b
                            if n >= 4:
                                pe.wait_ge(h_done, n - 3)
                            nc.tensor.matmul(ps[:, n % 4, :], W1[:, e, k * P:(k + 1) * P], yT[:, b * 512:(b + 1) * 512],
                                             start=True, stop=True).then_inc(h_ready, 1)
                    if e:
                        down(e - 1)
                down(E - 1)

            @block.scalar
            def _(act):
                for e in range(E):
                    if e >= 2:
                        act.wait_ge(d_ready, T * (e - 1))
                    for k in range(C):
                        for b in range(2):
                            n = (e * C + k) * 2 + b
                            act.wait_ge(h_ready, n + 1)
                            nc.scalar.activation(hid[:, e % 2, k, b * 512:(b + 1) * 512], ps[:, n % 4, :], ACT.Relu,
                                                 bias=b1T[:, e * C + k:e * C + k + 1]).then_inc(h_done, 1)
                ln.root(act, call2)

            @block.vector
            def _(dve):
                for n in range(E * T):
                    e, t = n // T, n % T
                    dve.wait_ge(d_ready, n + 1)
                    if e:
                        dve.wait_ge(added, n - T + 1)
                    nc.vector.scalar_tensor_tensor(y[:, t, :], ps[:, 4 + n % 4, 0:D], one[:, t, e:e + 1], y[:, t, :],
                                                   ALU.mult, ALU.add).then_inc(added, 1)
                dve.wait_ge(added, E * T)
                lk = Chain(dve, ln.dve_done, ln.chain_n)
                ln.normalise(dve, lk, y, z, call2)
                wide = lambda r: r[:, :].unsqueeze(1).broadcast_to((P, T, D))
                lk(nc.vector.tensor_tensor(z[:, :, :], z[:, :, :], wide(rows["g2"]), ALU.mult))
                lk(nc.vector.tensor_tensor(z[:, :, :], z[:, :, :], wide(rows["be2"]), ALU.add))
                nc.vector.tensor_tensor(z[:, :, :], z[:, :, :], X[:, :, :], ALU.add).then_inc(final, 1)

            @block.sync
            def _(sp):
                sp.wait_ge(final, 1)
                sp.dma_start(out.rearrange("a (t p) d -> p (a t) d", p=P), z[:, :, :]).then_inc(stored, 16)
                sp.wait_ge(stored, 16)


_INS = ["x", "ctx_1024", "mask_Bx1x1xS2_if1", "mask_Bx1xSxS2_ik1", "L0_attn_Wqkv", "L0_attn_Wproj", "L0_xattn_W_out",
        "L0_xattn_b_out", "L0_ffn_router_w", "L0_ffn_w_gate", "L0_ffn_w_up", "L0_ffn_w_down", "L1_attn_W_kv",
        "L1_attn_g_kv", "L1_attn_W_kdec", "L1_attn_W_vdec", "L1_attn_W_q", "L1_attn_W_qdec", "L1_attn_W_krope",
        "L1_attn_W_qrope", "L1_attn_W_o", "L1_xattn_Wq", "L1_xattn_bq", "L1_xattn_Wk", "L1_xattn_bk", "L1_xattn_Wv",
        "L1_xattn_bv", "L1_xattn_Wo", "L1_xattn_bo", "L1_ffn_Wqkv", "L1_ffn_bqkv", "L1_ffn_Wo", "L1_ffn_bo", "L1_ffn_g1",
        "L1_ffn_be1", "L1_ffn_g2", "L1_ffn_be2", "L1_ffn_Wg", "L1_ffn_W1", "L1_ffn_b1", "L1_ffn_W2", "L1_ffn_b2"]


def shape_constants():
    bf = lambda keep: np.where(keep, 0.0, MASKED).astype(np.float32)
    r, k = np.arange(P)[:, None], np.arange(P)[None, :]
    own, before = k <= r, (k >= r + 1) | (k % 64 == 0)
    never = np.zeros((P, P), bool)
    sparse_q = np.stack([np.concatenate([never, own, before, own], 1), np.concatenate([before, own, before, own], 1)], 1)
    sparse_k = np.concatenate([own.T, before.T, own.T, before.T], 1)
    glob_key = np.arange(16) * 64
    far = glob_key[None, :] // P <= np.arange(T)[:, None] - 2
    c = {"c_ident": np.eye(P, dtype=np.float32)}
    far_q = np.broadcast_to(far.reshape(1, T * 16), (P, T * 16))
    gk = np.zeros((P, S), bool)
    gk[0:16] = np.repeat(far.T, P, axis=1)
    gk[16:] = True
    c["c_sparse"] = bf(np.concatenate([sparse_q.reshape(P, 1024), sparse_k, far_q, gk], 1))
    c["c_causal"] = bf(np.concatenate([own, own.T], 1))
    inv = 1.0 / 10000.0 ** (np.arange(0, 32, 2, dtype=np.float32) / 32)
    f = np.outer(np.arange(S, dtype=np.float32), inv)
    emb = np.concatenate([f, f], -1)
    c["c_cos"] = np.tile(np.cos(emb).T, (4, 1)).astype(np.float32)
    c["c_sin"] = np.tile(np.sin(emb).T, (4, 1)).astype(np.float32)
    c["c_expert"] = np.broadcast_to(np.arange(E, dtype=np.float32) - E, (P, T, E))
    return c


def kernel(**inputs):
    import numpy as _np
    import concourse.bacc as _bacc
    from concourse import mybir as _mybir
    from concourse.bass_utils import run_bass_kernel_spmd as _run

    nc = _bacc.Bacc("TRN2", target_bir_lowering=False, num_devices=1)
    arrays, args = {}, {}
    for name, value in list((n, inputs[n]) for n in _INS) + list(shape_constants().items()):
        v = _np.ascontiguousarray(value)
        arrays[f"in_{name}_dram"] = v
        args[name] = nc.dram_tensor(f"in_{name}_dram", v.shape, _mybir.dt.from_np(v.dtype), kind="ExternalInput").ap()
    out = nc.dram_tensor("out_0_dram", (1, S, D), F32, kind="ExternalOutput").ap()
    build(nc, args, out)
    r = _run(nc, [arrays], core_ids=[0])
    return r.results[0]["out_0_dram"]
```
